# Optimizing a Trainium2 kernel written in Bass

```python
import numpy as np
import jax
import jax.numpy as jnp

def _softmax(x, axis=-1):
    return jax.nn.softmax(x, axis=axis)

def _gelu(x):
    return jax.nn.gelu(x, approximate=True)

def _silu(x):
    return jax.nn.silu(x)

def _sigmoid(x):
    return jax.nn.sigmoid(x)

def _layernorm(x, axis=-1, eps=1e-05):
    m = jnp.mean(x, axis=axis, keepdims=True)
    v = jnp.var(x, axis=axis, keepdims=True)
    return (x - m) / jnp.sqrt(v + eps)

def _scatter_add(tgt, idx, src, axis=0):
    return tgt.at[idx].add(src)

def _segment_sum(src, seg, n):
    return jax.ops.segment_sum(src, seg, n)
kernel_name = 'mk_vit_tower_d4_tok_img768_r4_ed808c'

def setup_inputs(seed: int=0):
    np.random.seed(seed)
    _w = jnp.asarray

    def _rec_inputs():
        import jax
        import jax.numpy as jnp
        _rk = jax.random.key(seed)
        x = -0.00016672 + 0.999947 * jax.random.normal(jax.random.fold_in(_rk, 1), (32, 3, 96, 96), jnp.float32)
        return x
    x = _rec_inputs()

    def _L0_tok_setup():
        import jax, jax.numpy as jnp
        import numpy as np
        P1, P2 = (16, 16)
        EPS = 0.0001

        def _patchify(x):
            b, c, H, W = x.shape
            h, w = (H // P1, W // P2)
            x = x.reshape(b, c, h, P1, w, P2)
            x = x.transpose(0, 2, 4, 3, 5, 1)
            return x.reshape(b, h * w, P1 * P2 * c)

        def _rmsnorm2d(x, weight):
            ms = jnp.mean(jnp.square(x), axis=(-2, -1), keepdims=True)
            return x * jax.lax.rsqrt(ms + EPS) * weight
        key = jax.random.key(seed)
        k0, k1, k2, k3, k4 = jax.random.split(key, 5)
        B, C, H, W_ = (64, 3, 96, 96)
        num_patches = H // P1 * (W_ // P2)
        patch_dim = C * P1 * P2
        proj_dim = 192
        x = jax.random.normal(k0, (B, C, H, W_), dtype=jnp.float32)
        g1 = 1.0 + 0.02 * jax.random.normal(k1, (num_patches, patch_dim), dtype=jnp.float32)
        W = jax.random.normal(k2, (proj_dim, patch_dim), dtype=jnp.float32) * patch_dim ** (-0.5)
        b = jax.random.normal(k3, (proj_dim,), dtype=jnp.float32) * 0.01
        g2 = 1.0 + 0.02 * jax.random.normal(k4, (num_patches, proj_dim), dtype=jnp.float32)
        return {'x': x, 'g1': g1, 'W': W, 'b': b, 'g2': g2}
    _L0_tok_all = _L0_tok_setup()
    _L0_tok_in = {k: v for k, v in _L0_tok_all.items() if k in ('g1', 'W', 'b', 'g2')}
    del _L0_tok_all

    def _L0_attn_setup():
        import jax, jax.numpy as jnp
        import numpy as np
        B, N, DIM = (16, 577, 192)
        HEADS, DIM_HEAD = (12, 64)
        INNER = HEADS * DIM_HEAD
        key = jax.random.key(seed)
        k1, k2, k3, k4 = jax.random.split(key, 4)
        x = jax.random.normal(k1, (B, N, DIM), dtype=jnp.float32)
        w_qkv = jax.random.normal(k2, (DIM, 3 * INNER), dtype=jnp.float32) * 0.02
        scale = jnp.full((HEADS,), DIM_HEAD ** (-0.5), dtype=jnp.float32)
        w_out = jax.random.normal(k3, (INNER, DIM), dtype=jnp.float32) * 0.02
        b_out = jnp.zeros((DIM,), dtype=jnp.float32)
        return {'x': x, 'w_qkv': w_qkv, 'scale': scale, 'w_out': w_out, 'b_out': b_out}
    _L0_attn_all = _L0_attn_setup()
    _L0_attn_in = {k: v for k, v in _L0_attn_all.items() if k in ('w_qkv', 'scale', 'w_out', 'b_out')}
    del _L0_attn_all

    def _L0_ffn_setup():
        import jax, jax.numpy as jnp
        import numpy as np
        B, T, C = (4, 512, 192)
        E, K = (8, 2)

        def _mlp(x, wfc, wproj):
            h = jnp.square(jax.nn.relu(x @ wfc))
            return h @ wproj
        key = jax.random.key(seed)
        ks = jax.random.split(key, 6)
        s = 0.02
        return {'x': jax.random.normal(ks[0], (B, T, C), jnp.float32), 'w_fc_sh': jax.random.normal(ks[1], (C, C), jnp.float32) * s, 'w_proj_sh': jax.random.normal(ks[2], (C, C), jnp.float32) * s, 'w1': jax.random.normal(ks[3], (E, C, C), jnp.float32) * s, 'w2': jax.random.normal(ks[4], (E, C, C), jnp.float32) * s, 'router_w': jax.random.normal(ks[5], (E, C), jnp.float32) * s, 'balance_bias': jnp.zeros((E,), jnp.float32)}
    _L0_ffn_all = _L0_ffn_setup()
    _L0_ffn_in = {k: v for k, v in _L0_ffn_all.items() if k in ('w_fc_sh', 'w_proj_sh', 'w1', 'w2', 'router_w', 'balance_bias')}
    del _L0_ffn_all

    def _L1_attn_setup():
        import jax, jax.numpy as jnp
        import numpy as np
        HALF_WIN = 6

        def _local_attn(x, w_qkv, w_proj, b_proj, num_heads=12):
            B, N, C = x.shape
            H = num_heads
            D = C // H
            W = 2 * HALF_WIN + 1
            qkv = (x @ w_qkv).reshape(B, N, 3, H, D)
            q, k, v = (qkv[:, :, 0], qkv[:, :, 1], qkv[:, :, 2])
            offs = jnp.arange(-HALF_WIN, HALF_WIN + 1)
            idx = jnp.arange(N)[:, None] + offs[None, :]
            valid = (idx >= 0) & (idx < N)
            idxc = jnp.clip(idx, 0, N - 1)
            k_win = k[:, idxc]
            v_win = v[:, idxc]
            scale = D ** (-0.5)
            scores = jnp.einsum('bnhd,bnwhd->bnhw', q, k_win) * scale
            neg = jnp.asarray(jnp.finfo(scores.dtype).min, scores.dtype)
            scores = jnp.where(valid[None, :, None, :], scores, neg)
            p = jax.nn.softmax(scores, axis=-1)
            out = jnp.einsum('bnhw,bnwhd->bnhd', p, v_win)
            out = out.reshape(B, N, C)
            return out @ w_proj + b_proj
        key = jax.random.key(seed)
        k1, k2, k3 = jax.random.split(key, 3)
        B, N, C = (2, 1024, 192)
        x = jax.random.normal(k1, (B, N, C), dtype=jnp.float32)
        s = 1.0 / np.sqrt(C)
        w_qkv = jax.random.uniform(k2, (C, 3 * C), jnp.float32, -s, s)
        w_proj = jax.random.uniform(k3, (C, C), jnp.float32, -s, s)
        b_proj = jnp.zeros((C,), jnp.float32)
        return {'x': x, 'w_qkv': w_qkv, 'w_proj': w_proj, 'b_proj': b_proj}
    _L1_attn_all = _L1_attn_setup()
    _L1_attn_in = {k: v for k, v in _L1_attn_all.items() if k in ('w_qkv', 'w_proj', 'b_proj')}
    del _L1_attn_all

    def _L1_ffn_setup():
        import jax, jax.numpy as jnp
        import numpy as np
        B, S, D_IN, D_HID, D_OUT = (32, 128, 192, 768, 192)
        key = jax.random.key(seed)
        k1, k2, k3, k4 = jax.random.split(key, 4)
        init_k = float(np.sqrt(1.0 / D_IN))
        init_k2 = float(np.sqrt(1.0 / D_HID))
        x = jax.random.normal(k1, (B, S, D_IN), dtype=jnp.float32)
        in_weight = jax.random.uniform(k2, (D_HID, D_IN), dtype=jnp.float32, minval=-init_k, maxval=init_k)
        in_bias = jax.random.uniform(k3, (D_HID,), dtype=jnp.float32, minval=-init_k, maxval=init_k)
        out_weight = jax.random.uniform(k4, (D_HID, D_OUT), dtype=jnp.float32, minval=-init_k2, maxval=init_k2)
        return {'x': x, 'in_weight': in_weight, 'in_bias': in_bias, 'out_weight': out_weight}
    _L1_ffn_all = _L1_ffn_setup()
    _L1_ffn_in = {k: v for k, v in _L1_ffn_all.items() if k in ('in_weight', 'in_bias', 'out_weight')}
    del _L1_ffn_all

    def _L2_attn_setup():
        import jax, jax.numpy as jnp
        import numpy as np
        N_HEAD = 12

        def _rotate_half(x):
            x_even = x[..., ::2]
            x_odd = x[..., 1::2]
            return jnp.stack((-x_odd, x_even), axis=-1).reshape(x.shape)

        def _rope_tables(T, D, dtype):
            inv_freq = 1.0 / 10000.0 ** (jnp.arange(0, D, 2, dtype=jnp.float32) / D)
            freqs = jnp.arange(T, dtype=jnp.float32)[:, None] * inv_freq[None, :]
            cos = jnp.repeat(jnp.cos(freqs), 2, axis=-1).astype(dtype)
            sin = jnp.repeat(jnp.sin(freqs), 2, axis=-1).astype(dtype)
            return (cos, sin)
        key = jax.random.key(seed)
        ks = jax.random.split(key, 5)
        B, T, C = (8, 256, 192)
        return {'x': jax.random.normal(ks[0], (B, T, C), dtype=jnp.float32), 'W_attn': jax.random.normal(ks[1], (C, 3 * C), dtype=jnp.float32) * C ** (-0.5), 'b_attn': jax.random.normal(ks[2], (3 * C,), dtype=jnp.float32) * 0.02, 'W_proj': jax.random.normal(ks[3], (C, C), dtype=jnp.float32) * C ** (-0.5), 'b_proj': jax.random.normal(ks[4], (C,), dtype=jnp.float32) * 0.02}
    _L2_attn_all = _L2_attn_setup()
    _L2_attn_in = {k: v for k, v in _L2_attn_all.items() if k in ('W_attn', 'b_attn', 'W_proj', 'b_proj')}
    del _L2_attn_all

    def _L2_ffn_setup():
        import jax, jax.numpy as jnp
        import numpy as np
        H = 12
        ALPHA = (1, 2, 3)
        DEPTH = 5
        BLOCK_DEPTH = 3
        TOTAL_DEPTH_M1 = 14 - 1
        SMALL_ACTIVE = BLOCK_DEPTH <= DEPTH <= TOTAL_DEPTH_M1 - BLOCK_DEPTH

        def _ln(x, g, b, eps=1e-05):
            m = jnp.mean(x, axis=-1, keepdims=True)
            v = jnp.mean((x - m) ** 2, axis=-1, keepdims=True)
            return (x - m) * jax.lax.rsqrt(v + eps) * g + b

        def _attn_branch(xp, w_qkv, w_proj, b_proj, keep_heads, keep_ch):
            B2, N, C = xp.shape
            hd = C // H
            scale = hd ** (-0.5)
            qkv = (xp @ w_qkv).reshape(B2, N, 3, H, hd).transpose(2, 0, 3, 1, 4)
            hmask = (jnp.arange(H) < keep_heads).astype(xp.dtype)[None, :, None, None]
            q, k, v = (qkv[0] * hmask, qkv[1] * hmask, qkv[2] * hmask)
            a = jax.nn.softmax(jnp.einsum('bhnd,bhmd->bhnm', q, k) * scale, axis=-1)
            o = jnp.einsum('bhnm,bhmd->bhnd', a, v).transpose(0, 2, 1, 3).reshape(B2, N, C)
            o = o @ w_proj + b_proj
            cmask = (jnp.arange(C) < keep_ch).astype(xp.dtype)
            return o * cmask

        def _mlp_branch(xp, w1, b1, w2, b2, keep_ch):
            C = xp.shape[-1]
            cmask = (jnp.arange(C) < keep_ch).astype(xp.dtype)
            h = jax.nn.gelu(xp * cmask @ w1 + b1, approximate=False)
            return (h @ w2 + b2) * cmask
        key = jax.random.key(seed)
        ks = jax.random.split(key, 8)
        B, N, C = (64, 257, 192)
        HID = 4 * C

        def w(k, shape):
            return jax.random.normal(k, shape, jnp.float32) * 0.02
        return {'x': jax.random.normal(ks[0], (B, N, C), jnp.float32), 'gumbel_weights': jax.random.uniform(ks[1], (3,), jnp.float32), 'n1l_g': jnp.ones((C,), jnp.float32), 'n1l_b': jnp.zeros((C,), jnp.float32), 'n1s_g': jnp.ones((C,), jnp.float32), 'n1s_b': jnp.zeros((C,), jnp.float32), 'w_qkv': w(ks[2], (C, 3 * C)), 'w_proj': w(ks[3], (C, C)), 'b_proj': jnp.zeros((C,), jnp.float32), 'n2l_g': jnp.ones((C,), jnp.float32), 'n2l_b': jnp.zeros((C,), jnp.float32), 'n2s_g': jnp.ones((C,), jnp.float32), 'n2s_b': jnp.zeros((C,), jnp.float32), 'w_fc1': w(ks[4], (C, HID)), 'b_fc1': jnp.zeros((HID,), jnp.float32), 'w_fc2': w(ks[5], (HID, C)), 'b_fc2': jnp.zeros((C,), jnp.float32)}
    _L2_ffn_all = _L2_ffn_setup()
    _L2_ffn_in = {k: v for k, v in _L2_ffn_all.items() if k in ('gumbel_weights', 'n1l_g', 'n1l_b', 'n1s_g', 'n1s_b', 'w_qkv', 'w_proj', 'b_proj', 'n2l_g', 'n2l_b', 'n2s_g', 'n2s_b', 'w_fc1', 'b_fc1', 'w_fc2', 'b_fc2')}
    del _L2_ffn_all

    def _L3_attn_setup():
        import jax, jax.numpy as jnp
        import numpy as np
        from jax import lax
        H = 192
        I = 384
        N = 16
        R = 48
        K = 4
        NL = 16
        B, L = (2, 256)
        EPS = 1e-05

        def rmsnorm(x, w):
            return x * lax.rsqrt(jnp.mean(x * x, axis=-1, keepdims=True) + EPS) * w

        def causal_conv(u, w, b):
            uc = jnp.swapaxes(u, 1, 2)
            y = lax.conv_general_dilated(uc, w, (1,), [(K - 1, 0)], dimension_numbers=('NCH', 'OIH', 'NCH'), feature_group_count=I)
            return jnp.swapaxes(y + b[None, :, None], 1, 2)

        def selective_scan(u, dt, A, Bm, Cm, Dp):

            def step(h, inp):
                u_t, dt_t, B_t, C_t = inp
                dA = jnp.exp(dt_t[:, :, None] * A)
                h = dA * h + (dt_t * u_t)[:, :, None] * B_t[:, None, :]
                y = jnp.einsum('bin,bn->bi', h, C_t)
                return (h, y)
            inputs = tuple((jnp.moveaxis(a, 1, 0) for a in (u, dt, Bm, Cm)))
            h0 = jnp.zeros((u.shape[0],) + A.shape, u.dtype)
            _, ys = lax.scan(step, h0, inputs)
            return jnp.moveaxis(ys, 0, 1) + u * Dp

        def mamba_layer(x, p):
            in_w, cw, cb, xp_w, dtw, dtb, a_log, dp, ow, nw = p
            h = rmsnorm(x, nw)
            xz = jnp.einsum('blh,ch->blc', h, in_w)
            u, z = jnp.split(xz, 2, axis=-1)
            u = jax.nn.silu(causal_conv(u, cw, cb))
            proj = jnp.einsum('bli,ci->blc', u, xp_w)
            dt_r, Bm, Cm = (proj[..., :R], proj[..., R:R + N], proj[..., R + N:])
            dt = jax.nn.softplus(jnp.einsum('blr,ir->bli', dt_r, dtw) + dtb)
            A = -jnp.exp(a_log)
            y = selective_scan(u, dt, A, Bm, Cm, dp)
            y = y * jax.nn.silu(z)
            return x + jnp.einsum('bli,hi->blh', y, ow)
        key = jax.random.key(seed)
        ks = jax.random.split(key, 8)
        s = 0.02
        x = jax.random.normal(ks[0], (B, L, H), jnp.float32)
        in_proj_w = jax.random.normal(ks[1], (NL, 2 * I, H), jnp.float32) * s
        conv_w = jax.random.normal(ks[2], (NL, I, 1, K), jnp.float32) * 0.1
        conv_b = jnp.zeros((NL, I), jnp.float32)
        x_proj_w = jax.random.normal(ks[3], (NL, R + 2 * N, I), jnp.float32) * s
        dt_proj_w = jax.random.normal(ks[4], (NL, I, R), jnp.float32) * 0.01
        dt_proj_b = -4.0 + 0.1 * jax.random.normal(ks[5], (NL, I), jnp.float32)
        A_log = jnp.log(jnp.tile(jnp.arange(1, N + 1, dtype=jnp.float32), (NL, I, 1)))
        D = jnp.ones((NL, I), jnp.float32)
        out_proj_w = jax.random.normal(ks[6], (NL, H, I), jnp.float32) * s
        norm_w = jnp.ones((NL, H), jnp.float32)
        final_norm_w = jnp.ones((H,), jnp.float32)
        return {'x': x, 'in_proj_w': in_proj_w, 'conv_w': conv_w, 'conv_b': conv_b, 'x_proj_w': x_proj_w, 'dt_proj_w': dt_proj_w, 'dt_proj_b': dt_proj_b, 'A_log': A_log, 'D': D, 'out_proj_w': out_proj_w, 'norm_w': norm_w, 'final_norm_w': final_norm_w}
    _L3_attn_all = _L3_attn_setup()
    _L3_attn_in = {k: v for k, v in _L3_attn_all.items() if k in ('in_proj_w', 'conv_w', 'conv_b', 'x_proj_w', 'dt_proj_w', 'dt_proj_b', 'A_log', 'D', 'out_proj_w', 'norm_w', 'final_norm_w')}
    del _L3_attn_all

    def _L3_ffn_setup():
        import jax, jax.numpy as jnp
        import numpy as np
        H = 192
        R = 64
        E = 8
        B, S = (8, 512)
        key = jax.random.key(seed)
        ks = jax.random.split(key, 10)
        s_in = 1.0 / np.sqrt(H)
        s_r = 1.0 / np.sqrt(R)
        return {'x': jax.random.normal(ks[0], (B, S, H), dtype=jnp.float32), 'enc_w': jax.random.uniform(ks[1], (H, R), jnp.float32, -s_in, s_in), 'enc_b': jax.random.uniform(ks[2], (R,), jnp.float32, -s_in, s_in), 'sw_w': jax.random.uniform(ks[3], (R, E), jnp.float32, -s_r, s_r), 'sw_b': jax.random.uniform(ks[4], (E,), jnp.float32, -s_r, s_r), 'w1': jax.random.uniform(ks[5], (E, H, R), jnp.float32, -s_in, s_in), 'b1': jax.random.uniform(ks[6], (E, R), jnp.float32, -s_in, s_in), 'w2': jax.random.uniform(ks[7], (E, R, H), jnp.float32, -s_r, s_r), 'b2': jax.random.uniform(ks[8], (E, H), jnp.float32, -s_r, s_r)}
    _L3_ffn_all = _L3_ffn_setup()
    _L3_ffn_in = {k: v for k, v in _L3_ffn_all.items() if k in ('enc_w', 'enc_b', 'sw_w', 'sw_b', 'w1', 'b1', 'w2', 'b2')}
    del _L3_ffn_all
    return {'x': x, 'L0_tok_g1': _L0_tok_in['g1'], 'L0_tok_W': _L0_tok_in['W'], 'L0_tok_b': _L0_tok_in['b'], 'L0_tok_g2': _L0_tok_in['g2'], 'L0_attn_w_qkv': _L0_attn_in['w_qkv'], 'L0_attn_scale': _L0_attn_in['scale'], 'L0_attn_w_out': _L0_attn_in['w_out'], 'L0_attn_b_out': _L0_attn_in['b_out'], 'L0_ffn_w_fc_sh': _L0_ffn_in['w_fc_sh'], 'L0_ffn_w_proj_sh': _L0_ffn_in['w_proj_sh'], 'L0_ffn_w1': _L0_ffn_in['w1'], 'L0_ffn_w2': _L0_ffn_in['w2'], 'L0_ffn_router_w': _L0_ffn_in['router_w'], 'L0_ffn_balance_bias': _L0_ffn_in['balance_bias'], 'L1_attn_w_qkv': _L1_attn_in['w_qkv'], 'L1_attn_w_proj': _L1_attn_in['w_proj'], 'L1_attn_b_proj': _L1_attn_in['b_proj'], 'L1_ffn_in_weight': _L1_ffn_in['in_weight'], 'L1_ffn_in_bias': _L1_ffn_in['in_bias'], 'L1_ffn_out_weight': _L1_ffn_in['out_weight'], 'L2_attn_W_attn': _L2_attn_in['W_attn'], 'L2_attn_b_attn': _L2_attn_in['b_attn'], 'L2_attn_W_proj': _L2_attn_in['W_proj'], 'L2_attn_b_proj': _L2_attn_in['b_proj'], 'L2_ffn_gumbel_weights': _L2_ffn_in['gumbel_weights'], 'L2_ffn_n1l_g': _L2_ffn_in['n1l_g'], 'L2_ffn_n1l_b': _L2_ffn_in['n1l_b'], 'L2_ffn_n1s_g': _L2_ffn_in['n1s_g'], 'L2_ffn_n1s_b': _L2_ffn_in['n1s_b'], 'L2_ffn_w_qkv': _L2_ffn_in['w_qkv'], 'L2_ffn_w_proj': _L2_ffn_in['w_proj'], 'L2_ffn_b_proj': _L2_ffn_in['b_proj'], 'L2_ffn_n2l_g': _L2_ffn_in['n2l_g'], 'L2_ffn_n2l_b': _L2_ffn_in['n2l_b'], 'L2_ffn_n2s_g': _L2_ffn_in['n2s_g'], 'L2_ffn_n2s_b': _L2_ffn_in['n2s_b'], 'L2_ffn_w_fc1': _L2_ffn_in['w_fc1'], 'L2_ffn_b_fc1': _L2_ffn_in['b_fc1'], 'L2_ffn_w_fc2': _L2_ffn_in['w_fc2'], 'L2_ffn_b_fc2': _L2_ffn_in['b_fc2'], 'L3_attn_in_proj_w': _L3_attn_in['in_proj_w'], 'L3_attn_conv_w': _L3_attn_in['conv_w'], 'L3_attn_conv_b': _L3_attn_in['conv_b'], 'L3_attn_x_proj_w': _L3_attn_in['x_proj_w'], 'L3_attn_dt_proj_w': _L3_attn_in['dt_proj_w'], 'L3_attn_dt_proj_b': _L3_attn_in['dt_proj_b'], 'L3_attn_A_log': _L3_attn_in['A_log'], 'L3_attn_D': _L3_attn_in['D'], 'L3_attn_out_proj_w': _L3_attn_in['out_proj_w'], 'L3_attn_norm_w': _L3_attn_in['norm_w'], 'L3_attn_final_norm_w': _L3_attn_in['final_norm_w'], 'L3_ffn_enc_w': _L3_ffn_in['enc_w'], 'L3_ffn_enc_b': _L3_ffn_in['enc_b'], 'L3_ffn_sw_w': _L3_ffn_in['sw_w'], 'L3_ffn_sw_b': _L3_ffn_in['sw_b'], 'L3_ffn_w1': _L3_ffn_in['w1'], 'L3_ffn_b1': _L3_ffn_in['b1'], 'L3_ffn_w2': _L3_ffn_in['w2'], 'L3_ffn_b2': _L3_ffn_in['b2']}

def reference(x, L0_tok_g1, L0_tok_W, L0_tok_b, L0_tok_g2, L0_attn_w_qkv, L0_attn_scale, L0_attn_w_out, L0_attn_b_out, L0_ffn_w_fc_sh, L0_ffn_w_proj_sh, L0_ffn_w1, L0_ffn_w2, L0_ffn_router_w, L0_ffn_balance_bias, L1_attn_w_qkv, L1_attn_w_proj, L1_attn_b_proj, L1_ffn_in_weight, L1_ffn_in_bias, L1_ffn_out_weight, L2_attn_W_attn, L2_attn_b_attn, L2_attn_W_proj, L2_attn_b_proj, L2_ffn_gumbel_weights, L2_ffn_n1l_g, L2_ffn_n1l_b, L2_ffn_n1s_g, L2_ffn_n1s_b, L2_ffn_w_qkv, L2_ffn_w_proj, L2_ffn_b_proj, L2_ffn_n2l_g, L2_ffn_n2l_b, L2_ffn_n2s_g, L2_ffn_n2s_b, L2_ffn_w_fc1, L2_ffn_b_fc1, L2_ffn_w_fc2, L2_ffn_b_fc2, L3_attn_in_proj_w, L3_attn_conv_w, L3_attn_conv_b, L3_attn_x_proj_w, L3_attn_dt_proj_w, L3_attn_dt_proj_b, L3_attn_A_log, L3_attn_D, L3_attn_out_proj_w, L3_attn_norm_w, L3_attn_final_norm_w, L3_ffn_enc_w, L3_ffn_enc_b, L3_ffn_sw_w, L3_ffn_sw_b, L3_ffn_w1, L3_ffn_b1, L3_ffn_w2, L3_ffn_b2):
    import jax
    import jax.numpy as jnp

    def _L0_tok_ref(x, g1, W, b, g2):
        import jax, jax.numpy as jnp
        import numpy as np
        P1, P2 = (16, 16)
        EPS = 0.0001

        def _patchify(x):
            b, c, H, W = x.shape
            h, w = (H // P1, W // P2)
            x = x.reshape(b, c, h, P1, w, P2)
            x = x.transpose(0, 2, 4, 3, 5, 1)
            return x.reshape(b, h * w, P1 * P2 * c)

        def _rmsnorm2d(x, weight):
            ms = jnp.mean(jnp.square(x), axis=(-2, -1), keepdims=True)
            return x * jax.lax.rsqrt(ms + EPS) * weight
        p = _patchify(x)
        p = _rmsnorm2d(p, g1)
        y = jnp.einsum('bnd,ed->bne', p, W) + b
        return _rmsnorm2d(y, g2)

    def _L0_attn_ref(x, w_qkv, scale, w_out, b_out):
        import jax, jax.numpy as jnp
        import numpy as np
        B, N, DIM = (16, 577, 192)
        HEADS, DIM_HEAD = (12, 64)
        INNER = HEADS * DIM_HEAD
        b, n, _ = x.shape
        h = scale.shape[0]
        dh = w_qkv.shape[1] // (3 * h)
        qkv = x @ w_qkv
        q, k, v = jnp.split(qkv, 3, axis=-1)
        to_heads = lambda t: t.reshape(b, n, h, dh).transpose(0, 2, 1, 3)
        q, k, v = (to_heads(q), to_heads(k), to_heads(v))
        dots = jnp.einsum('bhid,bhjd->bhij', q, k) * scale[None, :, None, None]
        se = dots.mean(axis=1, keepdims=True)
        diag = jnp.eye(n, dtype=bool)
        neg_inf = jnp.array(-jnp.inf, dots.dtype)
        dots = jnp.where(diag, neg_inf, dots)
        top_k = int(n * 0.75)
        _, idx = jax.lax.top_k(dots, top_k)
        bi = jnp.arange(b)[:, None, None, None]
        hi = jnp.arange(h)[None, :, None, None]
        ii = jnp.arange(n)[None, None, :, None]
        keep = jnp.zeros((b, h, n, n), dtype=bool).at[bi, hi, ii, idx].set(True)
        dots = jnp.where(keep, dots, neg_inf) + se
        attn = jax.nn.softmax(dots, axis=-1)
        out = jnp.einsum('bhij,bhjd->bhid', attn, v)
        out = out.transpose(0, 2, 1, 3).reshape(b, n, h * dh)
        return out @ w_out + b_out

    def _L0_ffn_ref(x, w_fc_sh, w_proj_sh, w1, w2, router_w, balance_bias):
        import jax, jax.numpy as jnp
        import numpy as np
        B, T, C = (4, 512, 192)
        E, K = (8, 2)

        def _mlp(x, wfc, wproj):
            h = jnp.square(jax.nn.relu(x @ wfc))
            return h @ wproj
        Bx, Tx, Cx = x.shape
        shared = _mlp(x, w_fc_sh, w_proj_sh)
        xf = x.reshape(-1, Cx)
        logits = xf.astype(jnp.float32) @ router_w.T
        scores = jax.nn.sigmoid(logits)
        _, idx = jax.lax.top_k(scores + balance_bias, K)
        tw = jnp.take_along_axis(scores, idx, axis=-1)
        tw = tw / (tw.sum(-1, keepdims=True) + 1e-20)
        combine = (jax.nn.one_hot(idx, E, dtype=tw.dtype) * tw[..., None]).sum(1)
        h = jnp.square(jax.nn.relu(jnp.einsum('nc,ech->neh', xf, w1)))
        y = jnp.einsum('neh,ehc->nec', h, w2)
        routed = jnp.einsum('nec,ne->nc', y, combine)
        return shared + routed.reshape(Bx, Tx, Cx)

    def _L1_attn_ref(x, w_qkv, w_proj, b_proj):
        import jax, jax.numpy as jnp
        import numpy as np
        HALF_WIN = 6

        def _local_attn(x, w_qkv, w_proj, b_proj, num_heads=12):
            B, N, C = x.shape
            H = num_heads
            D = C // H
            W = 2 * HALF_WIN + 1
            qkv = (x @ w_qkv).reshape(B, N, 3, H, D)
            q, k, v = (qkv[:, :, 0], qkv[:, :, 1], qkv[:, :, 2])
            offs = jnp.arange(-HALF_WIN, HALF_WIN + 1)
            idx = jnp.arange(N)[:, None] + offs[None, :]
            valid = (idx >= 0) & (idx < N)
            idxc = jnp.clip(idx, 0, N - 1)
            k_win = k[:, idxc]
            v_win = v[:, idxc]
            scale = D ** (-0.5)
            scores = jnp.einsum('bnhd,bnwhd->bnhw', q, k_win) * scale
            neg = jnp.asarray(jnp.finfo(scores.dtype).min, scores.dtype)
            scores = jnp.where(valid[None, :, None, :], scores, neg)
            p = jax.nn.softmax(scores, axis=-1)
            out = jnp.einsum('bnhw,bnwhd->bnhd', p, v_win)
            out = out.reshape(B, N, C)
            return out @ w_proj + b_proj
        return _local_attn(x, w_qkv, w_proj, b_proj)

    def _L1_ffn_ref(x, in_weight, in_bias, out_weight):
        import jax, jax.numpy as jnp
        import numpy as np
        B, S, D_IN, D_HID, D_OUT = (32, 128, 192, 768, 192)
        lead = x.shape[:-1]
        xt = x.reshape(-1, in_weight.shape[1])
        h = jax.nn.gelu(jnp.einsum('td,hd->th', xt, in_weight) + in_bias, approximate=False)
        out = jnp.einsum('th,ho->to', h, out_weight)
        return out.reshape(*lead, out_weight.shape[1])

    def _L2_attn_ref(x, W_attn, b_attn, W_proj, b_proj):
        import jax, jax.numpy as jnp
        import numpy as np
        N_HEAD = 12

        def _rotate_half(x):
            x_even = x[..., ::2]
            x_odd = x[..., 1::2]
            return jnp.stack((-x_odd, x_even), axis=-1).reshape(x.shape)

        def _rope_tables(T, D, dtype):
            inv_freq = 1.0 / 10000.0 ** (jnp.arange(0, D, 2, dtype=jnp.float32) / D)
            freqs = jnp.arange(T, dtype=jnp.float32)[:, None] * inv_freq[None, :]
            cos = jnp.repeat(jnp.cos(freqs), 2, axis=-1).astype(dtype)
            sin = jnp.repeat(jnp.sin(freqs), 2, axis=-1).astype(dtype)
            return (cos, sin)
        B, T, C = x.shape
        H = N_HEAD
        D = C // H
        qkv = x @ W_attn + b_attn
        q, k, v = jnp.split(qkv, 3, axis=-1)
        q = q.reshape(B, T, H, D).transpose(0, 2, 1, 3)
        k = k.reshape(B, T, H, D).transpose(0, 2, 1, 3)
        v = v.reshape(B, T, H, D).transpose(0, 2, 1, 3)
        cos, sin = _rope_tables(T, D, x.dtype)
        q = q * cos + _rotate_half(q) * sin
        k = k * cos + _rotate_half(k) * sin
        att = jnp.einsum('bhqd,bhkd->bhqk', q, k) * D ** (-0.5)
        causal = jnp.tril(jnp.ones((T, T), dtype=bool))
        att = jnp.where(causal, att, -jnp.inf)
        att = jax.nn.softmax(att, axis=-1)
        y = jnp.einsum('bhqk,bhkd->bhqd', att, v)
        y = y.transpose(0, 2, 1, 3).reshape(B, T, C)
        return y @ W_proj + b_proj

    def _L2_ffn_ref(x, gumbel_weights, n1l_g, n1l_b, n1s_g, n1s_b, w_qkv, w_proj, b_proj, n2l_g, n2l_b, n2s_g, n2s_b, w_fc1, b_fc1, w_fc2, b_fc2):
        import jax, jax.numpy as jnp
        import numpy as np
        H = 12
        ALPHA = (1, 2, 3)
        DEPTH = 5
        BLOCK_DEPTH = 3
        TOTAL_DEPTH_M1 = 14 - 1
        SMALL_ACTIVE = BLOCK_DEPTH <= DEPTH <= TOTAL_DEPTH_M1 - BLOCK_DEPTH

        def _ln(x, g, b, eps=1e-05):
            m = jnp.mean(x, axis=-1, keepdims=True)
            v = jnp.mean((x - m) ** 2, axis=-1, keepdims=True)
            return (x - m) * jax.lax.rsqrt(v + eps) * g + b

        def _attn_branch(xp, w_qkv, w_proj, b_proj, keep_heads, keep_ch):
            B2, N, C = xp.shape
            hd = C // H
            scale = hd ** (-0.5)
            qkv = (xp @ w_qkv).reshape(B2, N, 3, H, hd).transpose(2, 0, 3, 1, 4)
            hmask = (jnp.arange(H) < keep_heads).astype(xp.dtype)[None, :, None, None]
            q, k, v = (qkv[0] * hmask, qkv[1] * hmask, qkv[2] * hmask)
            a = jax.nn.softmax(jnp.einsum('bhnd,bhmd->bhnm', q, k) * scale, axis=-1)
            o = jnp.einsum('bhnm,bhmd->bhnd', a, v).transpose(0, 2, 1, 3).reshape(B2, N, C)
            o = o @ w_proj + b_proj
            cmask = (jnp.arange(C) < keep_ch).astype(xp.dtype)
            return o * cmask

        def _mlp_branch(xp, w1, b1, w2, b2, keep_ch):
            C = xp.shape[-1]
            cmask = (jnp.arange(C) < keep_ch).astype(xp.dtype)
            h = jax.nn.gelu(xp * cmask @ w1 + b1, approximate=False)
            return (h @ w2 + b2) * cmask
        B, N, C = x.shape
        B2 = B // 2
        nl = _ln(x[:B2], n1l_g, n1l_b)
        ns = _ln(x[B2:], n1s_g, n1s_b)
        a_large = _attn_branch(nl, w_qkv, w_proj, b_proj, H, C)
        if SMALL_ACTIVE:
            a_small = sum((gumbel_weights[i] * _attn_branch(ns, w_qkv, w_proj, b_proj, H // ALPHA[i], C // ALPHA[i]) for i in range(3)))
            attn_out = jnp.concatenate([a_large, a_small], axis=0)
        else:
            attn_out = jnp.concatenate([a_large, a_large], axis=0)
        x = x + attn_out
        nl2 = _ln(x[:B2], n2l_g, n2l_b)
        ns2 = _ln(x[B2:], n2s_g, n2s_b)
        m_large = _mlp_branch(nl2, w_fc1, b_fc1, w_fc2, b_fc2, C)
        if SMALL_ACTIVE:
            m_small = sum((gumbel_weights[i] * _mlp_branch(ns2, w_fc1, b_fc1, w_fc2, b_fc2, C // ALPHA[i]) for i in range(3)))
            mlp_out = jnp.concatenate([m_large, m_small], axis=0)
        else:
            mlp_out = jnp.concatenate([m_large, m_large], axis=0)
        return x + mlp_out

    def _L3_attn_ref(x, in_proj_w, conv_w, conv_b, x_proj_w, dt_proj_w, dt_proj_b, A_log, D, out_proj_w, norm_w, final_norm_w):
        import jax, jax.numpy as jnp
        import numpy as np
        from jax import lax
        H = 192
        I = 384
        N = 16
        R = 48
        K = 4
        NL = 16
        B, L = (2, 256)
        EPS = 1e-05

        def rmsnorm(x, w):
            return x * lax.rsqrt(jnp.mean(x * x, axis=-1, keepdims=True) + EPS) * w

        def causal_conv(u, w, b):
            uc = jnp.swapaxes(u, 1, 2)
            y = lax.conv_general_dilated(uc, w, (1,), [(K - 1, 0)], dimension_numbers=('NCH', 'OIH', 'NCH'), feature_group_count=I)
            return jnp.swapaxes(y + b[None, :, None], 1, 2)

        def selective_scan(u, dt, A, Bm, Cm, Dp):

            def step(h, inp):
                u_t, dt_t, B_t, C_t = inp
                dA = jnp.exp(dt_t[:, :, None] * A)
                h = dA * h + (dt_t * u_t)[:, :, None] * B_t[:, None, :]
                y = jnp.einsum('bin,bn->bi', h, C_t)
                return (h, y)
            inputs = tuple((jnp.moveaxis(a, 1, 0) for a in (u, dt, Bm, Cm)))
            h0 = jnp.zeros((u.shape[0],) + A.shape, u.dtype)
            _, ys = lax.scan(step, h0, inputs)
            return jnp.moveaxis(ys, 0, 1) + u * Dp

        def mamba_layer(x, p):
            in_w, cw, cb, xp_w, dtw, dtb, a_log, dp, ow, nw = p
            h = rmsnorm(x, nw)
            xz = jnp.einsum('blh,ch->blc', h, in_w)
            u, z = jnp.split(xz, 2, axis=-1)
            u = jax.nn.silu(causal_conv(u, cw, cb))
            proj = jnp.einsum('bli,ci->blc', u, xp_w)
            dt_r, Bm, Cm = (proj[..., :R], proj[..., R:R + N], proj[..., R + N:])
            dt = jax.nn.softplus(jnp.einsum('blr,ir->bli', dt_r, dtw) + dtb)
            A = -jnp.exp(a_log)
            y = selective_scan(u, dt, A, Bm, Cm, dp)
            y = y * jax.nn.silu(z)
            return x + jnp.einsum('bli,hi->blh', y, ow)
        params = (in_proj_w, conv_w, conv_b, x_proj_w, dt_proj_w, dt_proj_b, A_log, D, out_proj_w, norm_w)

        def body(carry, p):
            return (mamba_layer(carry, p), None)
        out, _ = lax.scan(body, x, params)
        return rmsnorm(out, final_norm_w)

    def _L3_ffn_ref(x, enc_w, enc_b, sw_w, sw_b, w1, b1, w2, b2):
        import jax, jax.numpy as jnp
        import numpy as np
        H = 192
        R = 64
        E = 8
        B, S = (8, 512)
        b, s, d = x.shape
        xt = x.reshape(-1, d)
        x_enc = xt @ enc_w + enc_b
        route_prob = jax.nn.softmax(x_enc @ sw_w + sw_b, axis=-1)
        route_prob_max = jnp.max(route_prob, axis=-1)
        routes = jnp.argmax(route_prob, axis=-1)
        onehot = jax.nn.one_hot(routes, E, dtype=xt.dtype)
        h = jnp.einsum('td,edr->ter', xt, w1) + b1[None]
        h = jax.nn.gelu(h, approximate=False)
        h = h * onehot[..., None]
        out = jnp.einsum('ter,erd->td', h, w2) + onehot @ b2
        out = out * route_prob_max[:, None]
        return out.reshape(b, s, d)
    h = _L0_tok_ref(x, L0_tok_g1, L0_tok_W, L0_tok_b, L0_tok_g2)
    h = h + _L0_attn_ref(_layernorm(h, axis=-1), L0_attn_w_qkv, L0_attn_scale, L0_attn_w_out, L0_attn_b_out)
    h = h + _L0_ffn_ref(_layernorm(h, axis=-1), L0_ffn_w_fc_sh, L0_ffn_w_proj_sh, L0_ffn_w1, L0_ffn_w2, L0_ffn_router_w, L0_ffn_balance_bias)
    h = h + _L1_attn_ref(_layernorm(h, axis=-1), L1_attn_w_qkv, L1_attn_w_proj, L1_attn_b_proj)
    h = h + _L1_ffn_ref(_layernorm(h, axis=-1), L1_ffn_in_weight, L1_ffn_in_bias, L1_ffn_out_weight)
    h = h + _L2_attn_ref(_layernorm(h, axis=-1), L2_attn_W_attn, L2_attn_b_attn, L2_attn_W_proj, L2_attn_b_proj)
    h = h + _L2_ffn_ref(_layernorm(h, axis=-1), L2_ffn_gumbel_weights, L2_ffn_n1l_g, L2_ffn_n1l_b, L2_ffn_n1s_g, L2_ffn_n1s_b, L2_ffn_w_qkv, L2_ffn_w_proj, L2_ffn_b_proj, L2_ffn_n2l_g, L2_ffn_n2l_b, L2_ffn_n2s_g, L2_ffn_n2s_b, L2_ffn_w_fc1, L2_ffn_b_fc1, L2_ffn_w_fc2, L2_ffn_b_fc2)
    h = h + _L3_attn_ref(_layernorm(h, axis=-1), L3_attn_in_proj_w, L3_attn_conv_w, L3_attn_conv_b, L3_attn_x_proj_w, L3_attn_dt_proj_w, L3_attn_dt_proj_b, L3_attn_A_log, L3_attn_D, L3_attn_out_proj_w, L3_attn_norm_w, L3_attn_final_norm_w)
    h = h + _L3_ffn_ref(_layernorm(h, axis=-1), L3_ffn_enc_w, L3_ffn_enc_b, L3_ffn_sw_w, L3_ffn_sw_b, L3_ffn_w1, L3_ffn_b1, L3_ffn_w2, L3_ffn_b2)
    return h

_drawn_inputs = setup_inputs


def setup_inputs(seed=0):
    import zlib

    import numpy as np

    out = dict(_drawn_inputs(seed))
    spreads = {'L0_attn_scale': (0.125, 0.6),
     'L0_attn_b_out': (0.0, 0.1),
     'L0_ffn_balance_bias': (0.0, 0.393),
     'L1_attn_b_proj': (0.0, 0.1),
     'L2_ffn_n1l_g': (1.0, 0.6),
     'L2_ffn_n1l_b': (0.0, 0.8),
     'L2_ffn_n1s_g': (1.0, 0.6),
     'L2_ffn_n1s_b': (0.0, 0.8),
     'L2_ffn_b_proj': (0.0, 0.1),
     'L2_ffn_n2l_g': (1.0, 0.6),
     'L2_ffn_n2l_b': (0.0, 0.8),
     'L2_ffn_n2s_g': (1.0, 0.6),
     'L2_ffn_n2s_b': (0.0, 0.8),
     'L2_ffn_b_fc1': (0.0, 0.75),
     'L2_ffn_b_fc2': (0.0, 0.1),
     'L3_attn_conv_b': (0.0, 0.8),
     'L3_attn_D': (1.0, 0.6),
     'L3_attn_norm_w': (1.0, 0.6),
     'L3_attn_final_norm_w': (1.0, 0.2)}
    factors = {'L0_tok_b': 4.494,
     'L0_tok_g2': 2.668,
     'L0_ffn_w1': 3.214,
     'L0_ffn_w2': 2.754,
     'L0_ffn_router_w': 4.471,
     'L1_ffn_in_bias': 3.271,
     'L2_attn_b_attn': 2.881,
     'L2_attn_b_proj': 3.275,
     'L2_ffn_gumbel_weights': 6.151,
     'L2_ffn_w_qkv': 5.557,
     'L2_ffn_w_proj': 5.565,
     'L3_attn_in_proj_w': 8.0,
     'L3_attn_conv_w': 8.0,
     'L3_attn_x_proj_w': 8.0,
     'L3_attn_dt_proj_w': 8.0,
     'L3_attn_dt_proj_b': 8.0,
     'L3_attn_A_log': 8.0,
     'L3_attn_out_proj_w': 8.0,
     'L3_ffn_enc_w': 4.635,
     'L3_ffn_enc_b': 8.0,
     'L3_ffn_sw_w': 4.698,
     'L3_ffn_sw_b': 8.0,
     'L3_ffn_w1': 4.89,
     'L3_ffn_b1': 8.0,
     'L3_ffn_w2': 4.611,
     'L3_ffn_b2': 8.0}
    for name, (base, spread) in spreads.items():
        noise = np.random.default_rng([zlib.crc32(name.encode()), seed]).standard_normal(out[name].shape)
        drawn = base * np.exp(spread * noise) if base else spread * noise
        out[name] = jnp.asarray(drawn.astype(out[name].dtype))
    for name, factor in factors.items():
        out[name] = (out[name] * factor).astype(out[name].dtype)
    return out
```

```python
from contextlib import ExitStack

import numpy as np

import concourse.bass as bass
from concourse import mybir

F32 = mybir.dt.float32
BF16 = mybir.dt.bfloat16
ALU = mybir.AluOpType
ACT = mybir.ActivationFunctionType
AX = mybir.AxisListType

B = 32
N = 36
C = 192
T = B * N
CP = 96
KC = C // CP
IMG = 3
TW = IMG * N
NT = -(-B // IMG)
TP = NT * TW
CH = 384
NCH = T // CH
HALF = T // 2
Q4 = T // 4
H = 12
LN_EPS = 1e-5
TOK_EPS = 1e-4
NEG = -1e30
KEEP = int(N * 0.75)
LAYERS = 16
DI = 384
JC = DI // 128
ST = 16
DR = 48
E8 = 8


class Signal:

    def __init__(self, nc, name):
        self.sem = nc.alloc_semaphore(name)
        self.base = 0
        self.total = 0

    def at(self, n):
        return n + self.base

    def raised(self, n):
        self.base += n

    def next(self):
        self.total += 1
        return self.base + self.total

    def restart(self):
        self.base, self.total = self.base + self.total, 0

    def counted(self, n):
        self.total += n
        return self.sem


def after_first(n):
    return not isinstance(n, int) or n > 0


def bc(ap, shape):
    return ap.broadcast_to(shape)


def build(nc, a, out):
    ctx = ExitStack()
    sig = {}

    def S(name):
        if name not in sig:
            sig[name] = Signal(nc, name)
        return sig[name]

    def sb(stack, name, shape, dt=F32):
        return stack.enter_context(nc.sbuf_tensor(name, shape, dt))

    with ctx:
        h = sb(ctx, "h", [CP, KC, TP])
        xn = sb(ctx, "xn", [CP, KC, TP])
        ones_mean = sb(ctx, "ones_mean", [128, 128])
        ident = sb(ctx, "ident", [128, 128])
        ident_bf = sb(ctx, "ident_bf", [TW, TW], BF16)
        eps = sb(ctx, "eps", [128, 2])
        ones_row = sb(ctx, "ones_row", [1, 128])
        ps = ctx.enter_context(nc.psum_tensor("ps", [128, 8, 512], F32))

        def loaded(group):
            return S("loaded_" + group)

        def layer_norm(src, dst, name, affine=None):
            with ExitStack() as st:
                d = sb(st, name + "_d", [CP, KC, T])
                sq = sb(st, name + "_sq", [CP, KC, T])
                std = sb(st, name + "_std", [CP, T])
                rstd = sb(st, name + "_rstd", [CP, T])
                mean_ready, centered, squared = S("ln_mean"), S("ln_centered"), S("ln_squared")
                var_ready, std_ready, rstd_ready, normed = S("ln_var"), S("ln_std"), S("ln_rstd"), S("ln_normed")
                with nc.Block() as block:
                    @block.tensor
                    def _(pe):
                        for c in range(NCH):
                            for k in range(KC):
                                last = pe.matmul(ps[:CP, c, :CH], ones_mean[:CP, :CP], src[:, k, c * CH:(c + 1) * CH],
                                                 start=k == 0, stop=k == KC - 1)
                            last.then_inc(mean_ready.sem, 1)
                        for c in range(NCH):
                            pe.wait_ge(squared.sem, squared.at(c + 1))
                            for k in range(KC):
                                last = pe.matmul(ps[:CP, 3 + c, :CH], ones_mean[:CP, :CP], sq[:, k, c * CH:(c + 1) * CH],
                                                 start=k == 0, stop=k == KC - 1)
                            last.then_inc(var_ready.sem, 1)

                    @block.vector
                    def _(dve):
                        for c in range(NCH):
                            cs = slice(c * CH, (c + 1) * CH)
                            dve.wait_ge(mean_ready.sem, mean_ready.at(c + 1))
                            dve.tensor_tensor(d[:, :, cs], src[:, :, cs], bc(ps[:CP, c:c + 1, :CH], [CP, KC, CH]),
                                              ALU.subtract).then_inc(centered.sem, 1)
                        for c in range(NCH):
                            cs = slice(c * CH, (c + 1) * CH)
                            dve.wait_ge(std_ready.sem, std_ready.at(c + 1))
                            dve.reciprocal(rstd[:, cs], std[:, cs]).then_inc(rstd_ready.sem, 1)
                            dve.wait_ge(rstd_ready.sem, rstd_ready.at(c + 1))
                            dve.tensor_tensor(dst[:, :, cs], d[:, :, cs],
                                              bc(rstd[:, cs].unsqueeze(1), [CP, KC, CH]),
                                              ALU.mult).then_inc(normed.sem, 1)

                    @block.scalar
                    def _(act):
                        for c in range(NCH):
                            cs = slice(c * CH, (c + 1) * CH)
                            act.wait_ge(centered.sem, centered.at(c + 1))
                            act.activation(sq[:, :, cs], d[:, :, cs], ACT.Square).then_inc(squared.sem, 1)
                        for c in range(NCH):
                            cs = slice(c * CH, (c + 1) * CH)
                            act.wait_ge(var_ready.sem, var_ready.at(c + 1))
                            act.activation(std[:, cs], ps[:CP, 3 + c, :CH], ACT.Sqrt,
                                           bias=eps[:CP, 0:1]).then_inc(std_ready.sem, 1)
                        if affine is not None:
                            gamma, beta = affine
                            act.wait_ge(normed.sem, normed.at(NCH))
                            for half in range(2):
                                hs = slice(half * HALF, (half + 1) * HALF)
                                for k in range(KC):
                                    act.activation(dst[:, k, hs], dst[:, k, hs], ACT.Identity,
                                                   bias=beta[:, half, k:k + 1], scale=gamma[:, half, k:k + 1])
                for s in (mean_ready, centered, squared, var_ready, std_ready, rstd_ready, normed):
                    s.raised(NCH)

        def attention(name, group, x, wq, wk, wv, mask, out_t, heads16=True, rope=None, select=None):
            D = 16 if heads16 else 64
            NQ = H * (32 if heads16 else 64) // 128
            NG = 4 if heads16 else 2
            INNER = H * D
            OP = CP if heads16 else 128
            OC = INNER // OP

            def place(head):
                chunk, g = head // NG, head % NG
                if heads16:
                    return chunk, 32 * g, g, chunk
                return chunk, 64 * g, 2 * g + chunk // 3, chunk % 3

            with ExitStack() as st:
                xt = sb(st, name + "_xt", [CP, KC, TW])
                qt = sb(st, name + "_qt", [128, NQ, TW])
                kt = sb(st, name + "_kt", [128, NQ, TW])
                if rope:
                    rot = sb(st, name + "_rot", [128, 4, NQ, TW])
                vt = sb(st, name + "_vt", [TW, INNER])
                p = sb(st, name + "_p", [TW, 4, 3, TW])
                pt = sb(st, name + "_pt", [TW, 4, 3, TW])
                nmax = sb(st, name + "_nmax", [TW, 4, 3])
                total = sb(st, name + "_total", [TW, H])
                rtot = sb(st, name + "_rtot", [TW, H])
                o = sb(st, name + "_o", [TW, INNER])
                if select is not None:
                    m8 = sb(st, name + "_m8", [TW, 4, 3, 8])
                    kept = sb(st, name + "_kept", [TW, 4, 3, TW])
                    shifted = sb(st, name + "_shifted", [TW, 4, 3, TW])
                    se = sb(st, name + "_se", [TW, TW])
                    nscale = sb(st, name + "_nscale", [128, NQ])

                x_copied, qk_made, qk_copied = S("at_x_copied"), S("at_qk_made"), S("at_qk_copied")
                se_made, se_copied, scored, maxed = S("at_se_made"), S("at_se_copied"), S("at_scored"), S("at_maxed")
                exped, p_turned, p_copied = S("at_exped"), S("at_p_turned"), S("at_p_copied")
                v_made, v_copied, o_made, recip = S("at_v_made"), S("at_v_copied"), S("at_o_made"), S("at_recip")
                o_scaled, o_turned, o_copied = S("at_o_scaled"), S("at_o_turned"), S("at_o_copied")
                rotated, dropped, moved, capped, scale_set = (
                    S("at_rotated"), S("at_dropped"), S("at_moved"), S("at_capped"), S("at_scale"))
                scores_read = moved if select is not None else exped

                def chunks2(n):
                    return [(i // 3, (i % 3) * TW) for i in range(n)]

                def pair(first, n):
                    nb = n // 3
                    return ps[:, first:first + nb, :3 * TW].rearrange("p b (s t) -> p b s t", s=3)

                with nc.Block() as block:
                    @block.gpsimd
                    def _(pool):
                        def copy_x(t):
                            if after_first(t):
                                pool.wait_ge(v_made.sem, v_made.at(t))
                            pool.tensor_copy(xt[:, :, :], x[:, :, bass.ds(t * TW, TW)]).then_inc(x_copied.sem, 1)
                        copy_x(0)
                        with pool.Fori(1, NT) as t:
                            copy_x(t)

                    @block.tensor
                    def _(pe):
                        def front(t):
                            pe.wait_ge(x_copied.sem, x_copied.at(t + 1))
                            if after_first(t):
                                pe.wait_ge(v_copied.sem, v_copied.at(t))
                            for w, first in ((wq, 6), (wk, 4)):
                                for i, (b, col) in enumerate(chunks2(NQ)):
                                    for k in range(KC):
                                        last = pe.matmul(ps[:, first + b, col:col + TW], w[:, k, i * 128:(i + 1) * 128],
                                                         xt[:, k, :], start=k == 0, stop=k == KC - 1)
                            if rope:
                                for w, first in ((rope[0], 7), (rope[1], 5)):
                                    for i in range(NQ):
                                        for k in range(KC):
                                            last = pe.matmul(ps[:, first, i * TW:(i + 1) * TW],
                                                             w[:, k, i * 128:(i + 1) * 128], xt[:, k, :],
                                                             start=k == 0, stop=k == KC - 1)
                            last.then_inc(qk_made.sem, 1)
                            pe.wait_ge(qk_copied.sem, qk_copied.at(t + 1))
                            if select is not None:
                                for i in range(NQ):
                                    last = pe.matmul(ps[:TW, 6, :TW], qt[:, i, :], kt[:, i, :],
                                                     start=i == 0, stop=i == NQ - 1)
                                last.then_inc(se_made.sem, 1)
                            if after_first(t):
                                pe.wait_ge(scores_read.sem, scores_read.at(t))
                            for head in range(H):
                                chunk, r, b, s = place(head)
                                pe.matmul(ps[:TW, b, s * TW:(s + 1) * TW], qt[r:r + D, chunk, :],
                                          kt[r:r + D, chunk, :], start=s == 0, stop=False,
                                          skip_group_check=True)
                            for b in range(4):
                                last = pe.matmul(ps[:TW, b, :3 * TW], ident_bf[:, :], mask, start=False, stop=True,
                                                 skip_group_check=True)
                            last.then_inc(scored.sem, 1)

                        def values(t):
                            if after_first(t):
                                pe.wait_ge(o_copied.sem, o_copied.at(t))
                            if select is not None:
                                pe.wait_ge(se_copied.sem, se_copied.at(t + 1))
                            for half in range(1 if heads16 else 2):
                                w = INNER if heads16 else INNER // 2
                                for k in range(KC):
                                    last = pe.matmul(ps[:TW, 6 + half, :w], xt[:, k, :], wv[:, k, half * w:(half + 1) * w],
                                                     start=k == 0, stop=k == KC - 1 and not rope)
                                if rope:
                                    last = pe.matmul(ps[:TW, 6, :w], ones_row[:, :TW], rope[4], start=False, stop=True)
                            last.then_inc(v_made.sem, 1)

                        def back(t, fronts):
                            pe.wait_ge(exped.sem, exped.at(t + 1))
                            pe.wait_ge(qk_copied.sem, qk_copied.at(fronts))
                            for g in range(3):
                                if g == 2:
                                    pe.wait_ge(p_copied.sem, p_copied.at(3 * t + 1))
                                for i in range(4):
                                    e = 4 * g + i
                                    last = pe.transpose(ps[:TW, 4 + g % 2, i * TW:(i + 1) * TW],
                                                        p[:, e // 3, e % 3, :], ident[:TW, :TW])
                                last.then_inc(p_turned.sem, 1)
                            pe.wait_ge(p_copied.sem, p_copied.at(3 * t + 3))
                            pe.wait_ge(v_copied.sem, v_copied.at(t + 1))
                            if select is not None:
                                pe.wait_ge(se_copied.sem, se_copied.at(fronts))
                            for head in range(H):
                                _, _, b, s = place(head)
                                half, col = (0, head * D) if heads16 else (head // 6, head % 6 * D)
                                last = pe.matmul(ps[:TW, 6 + half, col:col + D], pt[:, b, s, :],
                                                 vt[:, head * D:(head + 1) * D], start=True, stop=True)
                            last.then_inc(o_made.sem, 1)
                            pe.wait_ge(o_scaled.sem, o_scaled.at(t + 1))
                            for i in range(OC):
                                b, col = i // 3, (i % 3) * TW
                                last = pe.transpose(ps[:OP, 6 + b, col:col + TW], o[:, i * OP:(i + 1) * OP],
                                                    ident[:TW, :TW])
                            last.then_inc(o_turned.sem, 1)

                        pe.wait_ge(loaded(group).sem, loaded(group).total)
                        front(0)
                        values(0)
                        with pe.Fori(1, NT) as t:
                            front(t)
                            back(t - 1, t + 1)
                            values(t)
                        back(NT - 1, NT)

                    @block.scalar
                    def _(act):
                        def exps(t):
                            act.wait_ge(maxed.sem, maxed.at(t + 1))
                            if after_first(3 * t):
                                act.wait_ge(p_turned.sem, p_turned.at(3 * t))
                            if after_first(t):
                                act.wait_ge(recip.sem, recip.at(t))
                            for head in range(H):
                                _, _, b, s = place(head)
                                src = p[:, b, s, :] if select is not None else ps[:TW, b, s * TW:(s + 1) * TW]
                                if select is not None:
                                    src = kept[:, b, s, :]
                                last = act.activation(p[:, b, s, :], src, ACT.Exp, bias=nmax[:, b, s:s + 1],
                                                      accum_out=total[:, head:head + 1])
                            last.then_inc(exped.sem, 1)
                        exps(0)
                        with act.Fori(1, NT) as t:
                            exps(t)

                    @block.vector
                    def _(dve):
                        def front(t):
                            dve.wait_ge(qk_made.sem, qk_made.at(t + 1))
                            if after_first(t):
                                dve.wait_ge(scored.sem, scored.at(t))
                            if rope:
                                bias, tables = rope[2], rope[3]
                                for part in range(4):
                                    bank = (6, 7, 4, 5)[part]
                                    for i in range(NQ):
                                        last = dve.scalar_tensor_tensor(
                                            rot[:, part, i, :], ps[:, bank, i * TW:(i + 1) * TW], bias[:, part, i:i + 1],
                                            tables[:, part, :], ALU.add, ALU.mult)
                                last.then_inc(rotated.sem, 1)
                                dve.wait_ge(rotated.sem, rotated.at(t + 1))
                                dve.tensor_tensor(qt[:, :, :], rot[:, 0, :, :], rot[:, 1, :, :], ALU.add)
                                dve.tensor_tensor(kt[:, :, :], rot[:, 2, :, :], rot[:, 3, :, :],
                                                  ALU.add).then_inc(qk_copied.sem, 1)
                            elif select is None:
                                dve.tensor_scalar(qt[:, :, :].unsqueeze(1), pair(6, NQ), D ** -0.5, None, ALU.mult)
                                dve.tensor_copy(kt[:, :, :].unsqueeze(1), pair(4, NQ)).then_inc(qk_copied.sem, 1)
                            else:
                                for i, (b, col) in enumerate(chunks2(NQ)):
                                    dve.tensor_scalar(qt[:, i, :], ps[:, 6 + b, col:col + TW], nscale[:, i:i + 1], None,
                                                      ALU.mult)
                                dve.tensor_copy(kt[:, :, :].rearrange("p (b s) t -> p b s t", s=3),
                                                pair(4, NQ)).then_inc(qk_copied.sem, 1)
                                dve.wait_ge(se_made.sem, se_made.at(t + 1))
                                dve.tensor_scalar(se[:, :], ps[:TW, 6, :TW], -1.0 / H, None,
                                                  ALU.mult).then_inc(se_copied.sem, 1)
                            dve.wait_ge(scored.sem, scored.at(t + 1))
                            if select is not None:
                                def shift(b0):
                                    dve.tensor_tensor(shifted[:, b0:b0 + 2, :, :],
                                                      bc(se[:, :].unsqueeze(1).unsqueeze(1), [TW, 2, 3, TW]),
                                                      ps[:TW, b0:b0 + 2, :3 * TW].rearrange("p b (s t) -> p b s t", s=3),
                                                      ALU.subtract)
                                dve.wait_ge(se_copied.sem, se_copied.at(t + 1))
                                shift(0)
                                for b in range(4):
                                    for s in range(3):
                                        last = dve.max(m8[:, b, s, :], ps[:TW, b, s * TW:(s + 1) * TW])
                                last.then_inc(dropped.sem, 1)
                                dve.wait_ge(dropped.sem, dropped.at(t + 1))
                                if after_first(t):
                                    dve.wait_ge(exped.sem, exped.at(t))
                                shift(2)
                                for b in range(4):
                                    for s in range(3):
                                        last = dve.match_replace(kept[:, b, s, :], m8[:, b, s, :],
                                                                 ps[:TW, b, s * TW:(s + 1) * TW], NEG)
                                last.then_inc(moved.sem, 1)
                                dve.wait_ge(moved.sem, moved.at(t + 1))
                                dve.scalar_tensor_tensor(kept[:, :, :, :].rearrange("p b s t -> p (b s t)"),
                                                         kept[:, :, :, :].rearrange("p b s t -> p (b s t)"), -0.5 * NEG,
                                                         shifted[:, :, :, :].rearrange("p b s t -> p (b s t)"),
                                                         ALU.add, ALU.min).then_inc(capped.sem, 1)
                                dve.wait_ge(capped.sem, capped.at(t + 1))
                                dve.tensor_reduce(nmax[:, :, :], kept[:, :, :, :], AX.X, ALU.max,
                                                  negate=True).then_inc(maxed.sem, 1)
                            else:
                                dve.tensor_reduce(nmax[:, :, :],
                                                  ps[:TW, 0:4, :3 * TW].rearrange("p b (s t) -> p b s t", s=3),
                                                  AX.X, ALU.max, negate=True).then_inc(maxed.sem, 1)

                        def values(t):
                            dve.wait_ge(v_made.sem, v_made.at(t + 1))
                            if after_first(t):
                                dve.wait_ge(o_made.sem, o_made.at(t))
                            if heads16:
                                dve.tensor_copy(vt[:, :], ps[:TW, 6, :INNER]).then_inc(v_copied.sem, 1)
                            else:
                                dve.tensor_copy(vt[:, :].rearrange("p (b c) -> p b c", b=2),
                                                ps[:TW, 6:8, :INNER // 2]).then_inc(v_copied.sem, 1)

                        def back(t):
                            if after_first(t):
                                dve.wait_ge(o_made.sem, o_made.at(t))
                            ptf = pt[:, :, :, :].rearrange("p b s t -> p (b s) t")
                            for g in range(3):
                                dve.wait_ge(p_turned.sem, p_turned.at(3 * t + g + 1))
                                dve.tensor_copy(ptf[:, 4 * g:4 * g + 4, :],
                                                ps[:TW, 4 + g % 2, :4 * TW].rearrange("p (s t) -> p s t", s=4)
                                                ).then_inc(p_copied.sem, 1)
                            dve.wait_ge(exped.sem, exped.at(t + 1))
                            dve.reciprocal(rtot[:, :], total[:, :]).then_inc(recip.sem, 1)
                            dve.wait_ge(recip.sem, recip.at(t + 1))
                            dve.wait_ge(o_made.sem, o_made.at(t + 1))
                            if after_first(t):
                                dve.wait_ge(o_turned.sem, o_turned.at(t))
                            nb = 1 if heads16 else 2
                            for b in range(nb):
                                hb = H // nb
                                last = dve.tensor_tensor(
                                    o[:, b * hb * D:(b + 1) * hb * D].rearrange("p (h d) -> p h d", d=D),
                                    ps[:TW, 6 + b, :hb * D].rearrange("p (h d) -> p h d", d=D),
                                    bc(rtot[:, b * hb:(b + 1) * hb].unsqueeze(2), [TW, hb, D]), ALU.mult)
                            last.then_inc(o_scaled.sem, 1)
                            dve.wait_ge(o_turned.sem, o_turned.at(t + 1))
                            if heads16:
                                dve.tensor_copy(out_t[:, :, bass.ds(t * TW, TW)],
                                                ps[:OP, 6, :OC * TW].rearrange("p (s t) -> p s t", t=TW)
                                                ).then_inc(o_copied.sem, 1)
                            else:
                                for b in range(2):
                                    last = dve.tensor_copy(out_t[:, 3 * b:3 * b + 3, bass.ds(t * TW, TW)],
                                                           ps[:OP, 6 + b, :3 * TW].rearrange("p (s t) -> p s t", s=3))
                                last.then_inc(o_copied.sem, 1)

                        dve.wait_ge(loaded(group).sem, loaded(group).total)
                        if select is not None:
                            dve.tensor_scalar(nscale[:, :], select, -1.0, None, ALU.mult).then_inc(scale_set.sem, 1)
                            dve.wait_ge(scale_set.sem, scale_set.at(1))
                        front(0)
                        values(0)
                        front(1)
                        back(0)
                        values(1)
                        with dve.Fori(2, NT) as t:
                            front(t)
                            back(t - 1)
                            values(t)
                        back(NT - 1)
                for s in (x_copied, qk_made, qk_copied, scored, maxed, exped, v_made, v_copied, o_made, recip,
                          o_scaled, o_turned, o_copied):
                    s.raised(NT)
                p_turned.raised(3 * NT)
                p_copied.raised(3 * NT)
                if rope:
                    rotated.raised(NT)
                if select is not None:
                    for s in (se_made, se_copied, dropped, moved, capped):
                        s.raised(NT)
                    scale_set.raised(1)

        def project(group, src, weight, bias, dst, res, width=CH):
            projected = S("projected")
            n_chunks = T // width
            with nc.Block() as block:
                @block.tensor
                def _(pe):
                    pe.wait_ge(loaded(group).sem, loaded(group).total)
                    for c in range(n_chunks):
                        w = weight(c)
                        n_k = w.shape[1]
                        for m in range(KC):
                            for k in range(n_k):
                                last = pe.matmul(ps[:CP, KC * c + m, :width], w[:, k, m * CP:(m + 1) * CP],
                                                 src[:, k, c * width:(c + 1) * width], start=k == 0, stop=k == n_k - 1)
                            last.then_inc(projected.sem, 1)

                @block.vector
                def _(dve):
                    for c in range(n_chunks):
                        cs = slice(c * width, (c + 1) * width)
                        for m in range(KC):
                            dve.wait_ge(projected.sem, projected.at(KC * c + m + 1))
                            dve.scalar_tensor_tensor(dst[:, m, cs], ps[:CP, KC * c + m, :width], bias(c)[:, m:m + 1],
                                                     res[:, m, cs], ALU.add, ALU.add)
            projected.raised(n_chunks * KC)

        masks = sb(ctx, "masks", [TW, 4, 3 * TW], BF16)
        with ExitStack() as st:
            masks_f = sb(st, "masks_f", [TW, 4, 3 * TW])
            identity_made = S("identity_made")
            with nc.Block() as block:
                @block.sync
                def _(sp):
                    sp.dma_start(masks_f[:, :, :], a["masks"]).then_inc(loaded("const").counted(16), 16)

                @block.gpsimd
                def _(pool):
                    pool.memset(ident[:, :], 0.0).then_inc(identity_made.sem, 1)
                    pool.memset(h[:, :, T:], 0.0)
                    pool.memset(xn[:, :, T:], 0.0)
                    pool.memset(eps[:, 0:1], LN_EPS)
                    pool.memset(eps[:, 1:2], TOK_EPS)
                    pool.memset(ones_row[:, :], 1.0)
                    pool.memset(ones_mean[:, :], 1.0 / C)
                    pool.wait_ge(identity_made.sem, identity_made.at(1))
                    pool.affine_select(out=ident[:, :], in_=ident[:, :], compare_op=ALU.not_equal, fill=1.0,
                                       base=0, pattern=[[-1, 128]], channel_multiplier=1).then_inc(identity_made.sem, 1)

                @block.scalar
                def _(act):
                    act.wait_ge(identity_made.sem, identity_made.at(2))
                    act.activation(ident_bf[:, :], ident[:TW, :TW], ACT.Copy)
                    act.wait_ge(loaded("const").sem, loaded("const").total)
                    act.activation(masks[:, :, :], masks_f[:, :, :], ACT.Copy)

        def patch_embedding():
            with ExitStack() as st:
                pT = sb(st, "patches", [128, 6, T])
                sq = sb(st, "tok_sq", [128, 6, T])
                g1 = sb(st, "tok_g1", [128, 6, N])
                wt = sb(st, "tok_w", [128, 6, C])
                bt = sb(st, "tok_b", [CP, KC])
                g2 = sb(st, "tok_g2", [CP, KC, N])
                part = sb(st, "tok_part", [128, 6, B])
                r1 = sb(st, "tok_r1", [CP, B])
                s1 = sb(st, "tok_s1", [CP, B])
                y = sb(st, "tok_y", [CP, KC, T])
                sq2 = sb(st, "tok_sq2", [CP, KC, T])
                part2 = sb(st, "tok_part2", [CP, KC, B])
                r2 = sb(st, "tok_r2", [CP, B])
                s2 = sb(st, "tok_s2", [CP, B])
                squared, gained, summed, ms_made, root, inv = (S("tok_squared"), S("tok_gained"), S("tok_summed"),
                                                              S("tok_ms"), S("tok_root"), S("tok_inv"))
                embedded, y_done, y_squared, y_gained = S("tok_embedded"), S("tok_y"), S("tok_y_squared"), S("tok_y_gained")
                with nc.Block() as block:
                    @block.sync
                    def _(sp):
                        for k in range(6):
                            sp.dma_start(pT[:, k, :], a["patches"][:, k, :]).then_inc(loaded(f"patches{k}").counted(16), 16)
                        for tile, src in ((g1[:, :, :], a["tok_g1"]), (wt[:, :, :], a["tok_w"]),
                                             (bt[:, :], a["tok_b"]), (g2[:, :, :], a["tok_g2"])):
                            sp.dma_start(tile, src).then_inc(loaded("tok").counted(16), 16)

                    @block.scalar
                    def _(act):
                        for k in range(6):
                            act.wait_ge(loaded(f"patches{k}").sem, loaded(f"patches{k}").total)
                            act.activation(sq[:, k, :], pT[:, k, :], ACT.Square).then_inc(squared.sem, 1)
                        act.wait_ge(ms_made.sem, ms_made.at(1))
                        act.activation(s1[:, :], ps[:CP, 6, :B], ACT.Sqrt, bias=eps[:CP, 1:2],
                                       scale=C / (N * 768.0)).then_inc(root.sem, 1)
                        act.wait_ge(y_done.sem, y_done.at(1))
                        act.activation(sq2[:, :, :], y[:, :, :], ACT.Square).then_inc(y_squared.sem, 1)
                        act.wait_ge(ms_made.sem, ms_made.at(2))
                        act.activation(s2[:, :], ps[:CP, 7, :B], ACT.Sqrt, bias=eps[:CP, 1:2],
                                       scale=1.0 / N).then_inc(root.sem, 1)

                    @block.gpsimd
                    def _(pool):
                        pool.wait_ge(loaded("tok").sem, loaded("tok").total)
                        for k in range(6):
                            pool.wait_ge(squared.sem, squared.at(k + 1))
                            v = pT[:, k, :].rearrange("p (b n) -> p b n", n=N)
                            pool.tensor_tensor(v, v, bc(g1[:, k:k + 1, :], [128, B, N]), ALU.mult).then_inc(gained.sem, 1)

                    @block.tensor
                    def _(pe):
                        pe.wait_ge(loaded("tok").sem, loaded("tok").total)
                        for k in range(6):
                            pe.wait_ge(gained.sem, gained.at(k + 1))
                            for c in range(NCH):
                                for m in range(KC):
                                    last = pe.matmul(ps[:CP, KC * c + m, :CH], wt[:, k, m * CP:(m + 1) * CP],
                                                     pT[:, k, c * CH:(c + 1) * CH], start=k == 0, stop=k == 5)
                        last.then_inc(embedded.sem, 1)
                        pe.wait_ge(summed.sem, summed.at(1))
                        for k in range(6):
                            last = pe.matmul(ps[:CP, 6, :B], ones_mean[:, :CP], part[:, k, :], start=k == 0, stop=k == 5)
                        last.then_inc(ms_made.sem, 1)
                        pe.wait_ge(summed.sem, summed.at(2))
                        for k in range(KC):
                            last = pe.matmul(ps[:CP, 7, :B], ones_mean[:CP, :CP], part2[:, k, :], start=k == 0,
                                             stop=k == KC - 1)
                        last.then_inc(ms_made.sem, 1)

                    @block.vector
                    def _(dve):
                        for k in range(6):
                            dve.wait_ge(squared.sem, squared.at(k + 1))
                            last = dve.tensor_reduce(part[:, k, :], sq[:, k, :].rearrange("p (b n) -> p b n", n=N),
                                                     AX.X, ALU.add)
                        last.then_inc(summed.sem, 1)
                        dve.wait_ge(root.sem, root.at(1))
                        dve.reciprocal(r1[:, :], s1[:, :]).then_inc(inv.sem, 1)
                        dve.wait_ge(inv.sem, inv.at(1))
                        dve.wait_ge(embedded.sem, embedded.at(1))
                        dve.wait_ge(loaded("tok").sem, loaded("tok").total)
                        rfull = sq[:CP, 0, :]
                        dve.tensor_copy(rfull.rearrange("p (b n) -> p b n", n=N),
                                        bc(r1[:, :].unsqueeze(2), [CP, B, N])).then_inc(inv.sem, 1)
                        dve.wait_ge(inv.sem, inv.at(2))
                        for c in range(NCH):
                            for m in range(KC):
                                last = dve.tensor_tensor(y[:, m, c * CH:(c + 1) * CH], ps[:CP, KC * c + m, :CH],
                                                         rfull[:, c * CH:(c + 1) * CH], ALU.mult)
                        last.then_inc(inv.sem, 1)
                        dve.wait_ge(inv.sem, inv.at(3))
                        for m in range(KC):
                            last = dve.tensor_scalar(y[:, m, :], y[:, m, :], bt[:, m:m + 1], None, ALU.add)
                        last.then_inc(y_done.sem, 1)
                        dve.wait_ge(y_squared.sem, y_squared.at(1))
                        dve.tensor_reduce(part2[:, :, :], sq2[:, :, :].rearrange("p k (b n) -> p k b n", n=N),
                                          AX.X, ALU.add).then_inc(summed.sem, 1)
                        for m in range(KC):
                            v = y[:, m, :].rearrange("p (b n) -> p b n", n=N)
                            last = dve.tensor_tensor(v, v, bc(g2[:, m:m + 1, :], [CP, B, N]), ALU.mult)
                        last.then_inc(y_gained.sem, 1)
                        dve.wait_ge(root.sem, root.at(2))
                        dve.reciprocal(r2[:, :], s2[:, :]).then_inc(inv.sem, 1)
                        dve.wait_ge(inv.sem, inv.at(4))
                        dve.wait_ge(y_gained.sem, y_gained.at(1))
                        for m in range(KC):
                            dve.tensor_tensor(h[:, m, :T].rearrange("p (b n) -> p b n", n=N),
                                              y[:, m, :].rearrange("p (b n) -> p b n", n=N),
                                              bc(r2[:, :].unsqueeze(2), [CP, B, N]), ALU.mult)

        def l0_attention():
            with ExitStack() as st:
                wq = sb(st, "w0q", [CP, KC, H * 64])
                wk = sb(st, "w0k", [CP, KC, H * 64])
                wv = sb(st, "w0v", [CP, KC, H * 64])
                wo = sb(st, "w0o", [128, 6, C])
                bo = sb(st, "b0o", [CP, KC])
                sc = sb(st, "scale0", [128, 6])
                o_t = sb(st, "o0_t", [128, 6, TP])
                with nc.Block() as block:
                    @block.sync
                    def _(sp):
                        for tile, src in ((wq[:, :, :], a["a0_wq"]), (wk[:, :, :], a["a0_wk"]),
                                             (wv[:, :, :], a["a0_wv"]), (wo[:, :, :], a["a0_wo"]),
                                             (bo[:, :], a["a0_bo"]), (sc[:, :], a["a0_scale"])):
                            sp.dma_start(tile, src).then_inc(loaded("attn0").counted(16), 16)
                layer_norm(h, xn, "ln0")
                attention("at0", "attn0", xn, wq, wk, wv, masks[:, 0, :], o_t, heads16=False, select=sc[:, :])
                project("attn0", o_t, lambda c: wo, lambda c: bo, h, h)

        def store_output():
            with nc.Block() as block:
                @block.sync
                def _(sp):
                    stored = S("stored")
                    sp.dma_start(out, h[:, :, :T]).then_inc(stored.sem, 16)
                    sp.wait_ge(stored.sem, 16)

        def route(name, group, top_n, logits, balance, comb_t):
            tiles = T // 128
            pad = 8 - top_n
            with ExitStack() as st:
                sc = sb(st, name + "_sc", [128, tiles, 8])
                choice = sb(st, name + "_choice", [128, tiles, 8 + pad])
                marked = sb(st, name + "_marked", [128, tiles, 8 + pad])
                top = sb(st, name + "_top", [128, tiles, 8])
                comb = sb(st, name + "_comb", [128, tiles, 8])
                tot = sb(st, name + "_tot", [128, tiles])
                rtot = sb(st, name + "_rtot", [128, tiles])
                made, scored, stepped, combined, turned = (S("route_logits"), S("route_scored"), S("route_stepped"),
                                                           S("route_combined"), S("route_turned"))
                with nc.Block() as block:
                    @block.tensor
                    def _(pe):
                        pe.wait_ge(loaded(group).sem, loaded(group).total)
                        logits(pe, made)
                        pe.wait_ge(combined.sem, combined.at(1))
                        for i in range(tiles):
                            last = pe.transpose(ps[:8, 1 + i // 3, i % 3 * 128:(i % 3 + 1) * 128], comb[:, i, :],
                                                ident[:, :])
                        last.then_inc(turned.sem, 1)

                    @block.scalar
                    def _(act):
                        if top_n == 2:
                            act.wait_ge(made.sem, made.at(1))
                            act.activation(sc[:, :, :], ps[:, 0, :tiles * 8].rearrange("p (t e) -> p t e", e=8),
                                           ACT.Sigmoid).then_inc(scored.sem, 1)
                        else:
                            act.wait_ge(scored.sem, scored.at(1))
                            act.activation(sc[:, :, :], sc[:, :, :], ACT.Exp).then_inc(scored.sem, 1)

                    @block.vector
                    def _(dve):
                        dve.memset(choice[:, :, :], 3 * NEG).then_inc(stepped.sem, 1)
                        dve.wait_ge(stepped.sem, stepped.next())
                        values = choice[:, :, :8]
                        if top_n == 2:
                            dve.wait_ge(loaded(group).sem, loaded(group).total)
                            dve.wait_ge(scored.sem, scored.at(1))
                            dve.tensor_tensor(values, sc[:, :, :],
                                                   bc(balance.unsqueeze(1), [128, tiles, 8]), ALU.add).then_inc(stepped.sem, 1)
                            dve.wait_ge(stepped.sem, stepped.next())
                        else:
                            dve.wait_ge(made.sem, made.at(1))
                            dve.tensor_copy(values, ps[:, 0, :tiles * 8].rearrange("p (t e) -> p t e", e=8)).then_inc(stepped.sem, 1)
                            dve.wait_ge(stepped.sem, stepped.next())
                        for i in range(tiles):
                            last = dve.max(top[:, i, :], choice[:, i, :8])
                        last.then_inc(stepped.sem, 1)
                        dve.wait_ge(stepped.sem, stepped.next())
                        if top_n == 1:
                            dve.tensor_tensor(sc[:, :, :], values, bc(top[:, :, 0:1], [128, tiles, 8]),
                                              ALU.subtract).then_inc(scored.sem, 1)
                        dve.memset(top[:, :, top_n:], 3 * NEG).then_inc(stepped.sem, 1)
                        dve.wait_ge(stepped.sem, stepped.next())
                        for i in range(tiles):
                            last = dve.match_replace(marked[:, i, :], top[:, i, :], choice[:, i, :], 2 * NEG)
                        last.then_inc(stepped.sem, 1)
                        dve.wait_ge(stepped.sem, stepped.next())
                        dve.tensor_scalar(comb[:, :, :], marked[:, :, :8], NEG, None, ALU.is_lt).then_inc(stepped.sem, 1)
                        dve.wait_ge(stepped.sem, stepped.next())
                        if top_n == 2:
                            dve.tensor_tensor(comb[:, :, :], comb[:, :, :], sc[:, :, :], ALU.mult).then_inc(stepped.sem, 1)
                            dve.wait_ge(stepped.sem, stepped.next())
                            dve.tensor_reduce(tot[:, :], comb[:, :, :], AX.X, ALU.add).then_inc(stepped.sem, 1)
                            dve.wait_ge(stepped.sem, stepped.next())
                            dve.tensor_scalar(tot[:, :], tot[:, :], 1e-20, None, ALU.add).then_inc(stepped.sem, 1)
                            dve.wait_ge(stepped.sem, stepped.next())
                        else:
                            dve.wait_ge(scored.sem, scored.at(2))
                            dve.tensor_reduce(tot[:, :], sc[:, :, :], AX.X, ALU.add).then_inc(stepped.sem, 1)
                            dve.wait_ge(stepped.sem, stepped.next())
                        dve.reciprocal(rtot[:, :], tot[:, :]).then_inc(stepped.sem, 1)
                        dve.wait_ge(stepped.sem, stepped.next())
                        dve.tensor_tensor(comb[:, :, :], comb[:, :, :], bc(rtot[:, :].unsqueeze(2), [128, tiles, 8]),
                                          ALU.mult).then_inc(combined.sem, 1)
                        dve.wait_ge(turned.sem, turned.at(1))
                        dve.tensor_copy(comb_t[:, :].rearrange("p (b t) -> p b t", b=3), ps[:8, 1:4, :CH])
                for s in (made, combined, turned):
                    s.raised(1)
                scored.raised(1 if top_n == 2 else 2)
                stepped.restart()

        def l0_ffn():
            with ExitStack() as st:
                w1 = sb(st, "moe_w1", [CP, E8 + 1, KC, C])
                w2 = sb(st, "moe_w2", [CP, E8 + 1, KC, C])
                wr = sb(st, "moe_router", [CP, KC, E8])
                bal = sb(st, "moe_balance", [128, E8])
                comb_t = sb(st, "moe_comb_t", [E8, T])
                pick = sb(st, "moe_pick", [E8, E8, CP])
                r = sb(st, "moe_r", [CP, 2, KC, CH])
                rc = sb(st, "moe_rc", [CP, KC, CH])
                hid = sb(st, "moe_hid", [CP, 2, KC, CH])
                with nc.Block() as block:
                    @block.sync
                    def _(sp):
                        for tile, src in ((wr[:, :, :], a["moe_router"]), (bal[:, :], a["moe_balance"])):
                            sp.dma_start(tile, src).then_inc(loaded("router").counted(16), 16)
                        for tile, src in ((w1[:, :, :, :], a["moe_w1"]), (w2[:, :, :, :], a["moe_w2"])):
                            sp.dma_start(tile, src).then_inc(loaded("moe").counted(16), 16)

                    @block.vector
                    def _(dve):
                        dve.tensor_copy(pick[:, :, :], bc(ident[:E8, :E8].unsqueeze(2), [E8, E8, CP]))
                layer_norm(h, xn, "ln1")

                def logits(pe, made):
                    for i in range(T // 128):
                        for k in range(KC):
                            last = pe.matmul(ps[:, 0, 8 * i:8 * i + 8], xn[:, k, 128 * i:128 * i + 128], wr[:, k, :],
                                             start=k == 0, stop=k == KC - 1)
                    last.then_inc(made.sem, 1)
                route("r0", "router", 2, logits, bal[:, :], comb_t)

                NE = E8 + 1
                hidden, relued, shared_out, weighted, summed, added = (
                    S("moe_hidden"), S("moe_relued"), S("moe_rc_made"), S("moe_weighted"), S("moe_summed"), S("moe_added"))
                with nc.Block() as block:
                    @block.tensor
                    def _(pe):
                        pe.wait_ge(loaded("moe").sem, loaded("moe").total)

                        def first(c, e):
                            n = c * NE + e
                            if after_first(n - 1 if e else n):
                                pe.wait_ge(weighted.sem, weighted.at(n - 1 if e else n))
                            for m in range(KC):
                                for k in range(KC):
                                    last = pe.matmul(ps[:CP, 2 * (e % 2) + m, :CH], w1[:, e, k, m * CP:(m + 1) * CP],
                                                     xn[:, k, bass.ds(c * CH, CH)], start=k == 0, stop=k == KC - 1)
                            if e < E8:
                                last = pe.matmul(ps[:CP, 6 + e % 2, :CH], pick[:, e, :], comb_t[:, bass.ds(c * CH, CH)],
                                                 start=True, stop=True)
                            last.then_inc(hidden.sem, 1)

                        def second(c, e):
                            n = c * NE + e
                            pe.wait_ge(weighted.sem, weighted.at(n + 1))
                            if e == 0:
                                if after_first(c):
                                    pe.wait_ge(added.sem, added.at(c))
                            for m in range(KC):
                                for k in range(KC):
                                    last = pe.matmul(ps[:CP, 4 + m, :CH], w2[:, e, k, m * CP:(m + 1) * CP],
                                                     hid[:, e % 2, k, :], start=e == 0 and k == 0,
                                                     stop=e == NE - 1 and k == KC - 1)
                            last.then_inc(summed.sem, 1)

                        def chunk(c):
                            first(c, 0)
                            for e in range(NE):
                                if e + 1 < NE:
                                    first(c, e + 1)
                                second(c, e)
                        chunk(0)
                        with pe.Fori(1, NCH) as c:
                            chunk(c)

                    @block.scalar
                    def _(act):
                        def chunk(c):
                            for e in range(NE):
                                n = c * NE + e
                                act.wait_ge(hidden.sem, hidden.at(n + 1))
                                act.activation(r[:, e % 2, :, :], ps[:CP, 2 * (e % 2):2 * (e % 2) + 2, :CH],
                                               ACT.Relu).then_inc(relued.sem, 1)
                        chunk(0)
                        with act.Fori(1, NCH) as c:
                            chunk(c)

                    @block.vector
                    def _(dve):
                        def chunk(c):
                            for e in range(NE):
                                n = c * NE + e
                                dve.wait_ge(relued.sem, relued.at(n + 1))
                                if after_first(n - 1 if e else n):
                                    dve.wait_ge(summed.sem, summed.at(n - 1 if e else n))
                                rr = r[:, e % 2, :, :]
                                if e < E8:
                                    if after_first(n):
                                        dve.wait_ge(weighted.sem, weighted.at(n))
                                    dve.tensor_tensor(rc[:, :, :], rr, bc(ps[:CP, 6 + e % 2:7 + e % 2, :CH], [CP, KC, CH]),
                                                      ALU.mult).then_inc(shared_out.sem, 1)
                                    dve.wait_ge(shared_out.sem, shared_out.at(c * E8 + e + 1))
                                    dve.tensor_tensor(hid[:, e % 2, :, :], rc[:, :, :], rr, ALU.mult).then_inc(weighted.sem, 1)
                                else:
                                    dve.tensor_tensor(hid[:, e % 2, :, :], rr, rr, ALU.mult).then_inc(weighted.sem, 1)
                            dve.wait_ge(summed.sem, summed.at((c + 1) * NE))
                            hc = h[:, :, bass.ds(c * CH, CH)]
                            dve.tensor_tensor(hc, hc, ps[:CP, 4:6, :CH], ALU.add).then_inc(added.sem, 1)
                        chunk(0)
                        with dve.Fori(1, NCH) as c:
                            chunk(c)
                for s in (hidden, relued, weighted, summed):
                    s.raised(NE * NCH)
                shared_out.raised(E8 * NCH)
                added.raised(NCH)

        def gelu_mlp(group, x, chunks, width, variants, bias1, bias2, res, dst, hs):
            hidden, gelued, summed, added, partly = (S("mlp_hidden"), S("mlp_gelued"), S("mlp_summed"), S("mlp_added"),
                                                     S("mlp_partly"))
            n_v = len(variants)
            units = 6 * n_v
            col0, count = chunks
            rows_of = [[(k, min(CP, rows - k * CP)) for k in range(KC) if rows > k * CP] for _, rows, _, _ in variants]
            with nc.Block() as block:
                @block.tensor
                def _(pe):
                    pe.wait_ge(loaded(group).sem, loaded(group).total)

                    def chunk(c):
                        cols = bass.ds(c * width + col0, width)
                        for u in range(units):
                            v, m = divmod(u, 6)
                            w1 = variants[v][0]
                            if after_first(c * units + u - 3):
                                pe.wait_ge(gelued.sem, gelued.at(c * units + u - 3))
                            for k, kr in rows_of[v]:
                                last = pe.matmul(ps[:, u % 4 if units % 4 == 0 else RING[u % 12], :width],
                                                 w1[:kr, k, m * 128:(m + 1) * 128], x[:kr, k, cols],
                                                 start=k == 0, stop=k == rows_of[v][-1][0])
                            last.then_inc(hidden.sem, 1)
                        pe.wait_ge(gelued.sem, gelued.at((c + 1) * units))
                        if after_first(c):
                            pe.wait_ge(added.sem, added.at(c))
                        for mo in range(KC):
                            todo = [(v, m) for v in range(n_v) for m in range(6) if variants[v][3] > mo * CP]
                            for i, (v, m) in enumerate(todo):
                                w2, outs = variants[v][2], min(CP, variants[v][3] - mo * CP)
                                last = pe.matmul(ps[:outs, 4 + mo, :width], w2[:, m, mo * CP:mo * CP + outs],
                                                 hs[:, 6 * v + m, :width], start=i == 0, stop=i == len(todo) - 1,
                                                 skip_group_check=n_v > 1)
                        last.then_inc(summed.sem, 1)
                    chunk(0)
                    with pe.Fori(1, count) as c:
                        chunk(c)

                @block.scalar
                def _(act):
                    def chunk(c):
                        if after_first(c):
                            act.wait_ge(summed.sem, summed.at(c))
                        for u in range(units):
                            act.wait_ge(hidden.sem, hidden.at(c * units + u + 1))
                            act.activation(hs[:, u, :width], ps[:, u % 4 if units % 4 == 0 else RING[u % 12], :width],
                                           ACT.Gelu, bias=bias1[:, u % 6:u % 6 + 1]).then_inc(gelued.sem, 1)
                    chunk(0)
                    with act.Fori(1, count) as c:
                        chunk(c)

                @block.vector
                def _(dve):
                    def chunk(c):
                        dve.wait_ge(summed.sem, summed.at(c + 1))
                        cols = bass.ds(c * width + col0, width)
                        for m in range(KC):
                            last = dve.scalar_tensor_tensor(dst[:, m, cols], ps[:CP, 4 + m, :width], bias2[:, m:m + 1],
                                                            res[0][:, m, cols], ALU.add, ALU.add)
                        if len(res) == 2:
                            last.then_inc(partly.sem, 1)
                            dve.wait_ge(partly.sem, partly.at(c + 1))
                            last = dve.tensor_tensor(dst[:, :, cols], dst[:, :, cols], res[1][:, :, cols], ALU.add)
                        last.then_inc(added.sem, 1)
                    chunk(0)
                    with dve.Fori(1, count) as c:
                        chunk(c)
            hidden.raised(units * count)
            gelued.raised(units * count)
            summed.raised(count)
            added.raised(count)
            if len(res) == 2:
                partly.raised(count)

        RING = [0, 1, 2, 3] * 3

        def l1_attention():
            with ExitStack() as st:
                wq = sb(st, "w1q", [CP, KC, H * 32])
                wk = sb(st, "w1k", [CP, KC, H * 32])
                wv = sb(st, "w1v", [CP, KC, C])
                wo = sb(st, "w1o", [CP, KC, C])
                bo = sb(st, "b1o", [CP, KC])
                o_t = sb(st, "o1_t", [CP, KC, TP])
                with nc.Block() as block:
                    @block.sync
                    def _(sp):
                        for tile, src in ((wq[:, :, :], a["a1_wq"]), (wk[:, :, :], a["a1_wk"]),
                                             (wv[:, :, :], a["a1_wv"]), (wo[:, :, :], a["a1_wo"]),
                                             (bo[:, :], a["a1_bo"])):
                            sp.dma_start(tile, src).then_inc(loaded("attn1").counted(16), 16)
                layer_norm(h, xn, "ln2")
                attention("at1", "attn1", xn, wq, wk, wv, masks[:, 1, :], o_t)
                project("attn1", o_t, lambda c: wo, lambda c: bo, h, h)

        def l1_ffn():
            with ExitStack() as st:
                w1 = sb(st, "f1_w1", [CP, KC, 768])
                b1 = sb(st, "f1_b1", [128, 6])
                w2 = sb(st, "f1_w2", [128, 6, C])
                zero = sb(st, "f1_zero", [CP, KC])
                hs = sb(st, "f1_hs", [128, 6, CH])
                with nc.Block() as block:
                    @block.sync
                    def _(sp):
                        for tile, src in ((w1[:, :, :], a["f1_w1"]), (b1[:, :], a["f1_b1"]), (w2[:, :, :], a["f1_w2"])):
                            sp.dma_start(tile, src).then_inc(loaded("ffn1").counted(16), 16)

                    @block.gpsimd
                    def _(pool):
                        pool.memset(zero[:, :], 0.0)
                layer_norm(h, xn, "ln3")
                gelu_mlp("ffn1", xn, (0, NCH), CH, [(w1, C, w2, C)], b1, zero, [h], h, hs)

        def l2_attention():
            with ExitStack() as st:
                wq, wk, wqs, wks = (sb(st, n, [CP, KC, H * 32]) for n in ("w2q", "w2k", "w2qs", "w2ks"))
                wv = sb(st, "w2v", [CP, KC, C])
                wo = sb(st, "w2o", [CP, KC, C])
                bo = sb(st, "b2o", [CP, KC])
                bqk = sb(st, "b2qk", [128, 4, 3])
                bv = sb(st, "b2v", [1, C])
                tables = sb(st, "rope", [128, 4, TW])
                o_t = sb(st, "o2_t", [CP, KC, TP])
                with nc.Block() as block:
                    @block.sync
                    def _(sp):
                        for tile, src in ((wq[:, :, :], a["a2_wq"]), (wk[:, :, :], a["a2_wk"]),
                                             (wqs[:, :, :], a["a2_wqs"]), (wks[:, :, :], a["a2_wks"]),
                                             (wv[:, :, :], a["a2_wv"]), (wo[:, :, :], a["a2_wo"]),
                                             (bo[:, :], a["a2_bo"]), (bqk[:, :, :], a["a2_bqk"]),
                                             (bv[:, :], a["a2_bv"]), (tables[:, :, :], a["rope"])):
                            sp.dma_start(tile, src).then_inc(loaded("attn2").counted(16), 16)
                layer_norm(h, xn, "ln4")
                attention("at2", "attn2", xn, wq, wk, wv, masks[:, 2, :], o_t,
                          rope=(wqs, wks, bqk, tables, bv[:, :]))
                project("attn2", o_t, lambda c: wo, lambda c: bo, h, h)

        def l2_ffn():
            keep = [C // 1, C // 2, C // 3]
            with ExitStack() as st:
                wq = sb(st, "w3q", [CP, KC, H * 32])
                wk = sb(st, "w3k", [CP, KC, H * 32])
                wv = sb(st, "w3v", [CP, KC, C])
                wo = sb(st, "w3o", [CP, KC, C])
                wos = sb(st, "w3os", [CP, KC, C])
                bo = sb(st, "b3o", [CP, KC])
                bos = sb(st, "b3os", [CP, KC])
                gw = sb(st, "gumbel", [128, 3])
                gb = sb(st, "n12_gb", [CP, 4, 2, KC])
                w1 = sb(st, "f2_w1", [CP, KC, 768])
                b1 = sb(st, "f2_b1", [128, 6])
                w2 = sb(st, "f2_w2", [128, 6, C])
                w2s = [sb(st, f"f2_w2s{i}", [128, 6, keep[i]]) for i in range(3)]
                b2 = sb(st, "f2_b2", [CP, KC])
                b2s = sb(st, "f2_b2s", [CP, KC])
                x2 = sb(st, "x2", [CP, KC, T])
                n1 = sb(st, "n1", [CP, KC, TP])
                started, blended = S("blend_started"), S("blend_stepped")
                with nc.Block() as block:
                    @block.sync
                    def _(sp):
                        for tile, src in ((wq[:, :, :], a["a3_wq"]), (wk[:, :, :], a["a3_wk"]),
                                             (wv[:, :, :], a["a3_wv"]), (wo[:, :, :], a["a3_wo"]),
                                             (bo[:, :], a["a3_bo"]), (gw[:, :], a["gumbel"]), (gb[:, :, :, :], a["n12_gb"]),
                                             (w1[:, :, :], a["f2_w1"]), (b1[:, :], a["f2_b1"]),
                                             (w2[:, :, :], a["f2_w2"]), (b2[:, :], a["f2_b2"])):
                            sp.dma_start(tile, src).then_inc(loaded("block2").counted(16), 16)

                    @block.vector
                    def _(dve):
                        dve.wait_ge(loaded("block2").sem, loaded("block2").total)
                        dve.memset(n1[:, :, T:], 0.0)
                        dve.tensor_scalar(wos[:, :, :], wo[:, :, :], gw[:CP, 0:1], None, ALU.mult)
                        dve.tensor_scalar(bos[:, :], bo[:, :], gw[:CP, 0:1], None, ALU.mult)
                        dve.tensor_scalar(b2s[:, :], b2[:, :], gw[:CP, 0:1], None, ALU.mult)
                        for i in range(3):
                            last = dve.tensor_scalar(w2s[i][:, :, :], w2[:, :, :keep[i]], gw[:, i:i + 1], None, ALU.mult)
                        last.then_inc(blended.sem, 1)
                        for i in (1, 2):
                            if after_first(i):
                                dve.wait_ge(blended.sem, blended.at(i))
                            k = keep[i]
                            for dst, src in ((wos[:k, 0, :k], wo[:k, 0, :k]), (bos[:k, 0:1], bo[:k, 0:1]),
                                             (b2s[:k, 0:1], b2[:k, 0:1])):
                                last = dve.scalar_tensor_tensor(dst, src, gw[:k, i:i + 1], dst, ALU.mult, ALU.add)
                            last.then_inc(blended.sem, 1)
                blended.raised(3)
                layer_norm(h, xn, "ln5")
                layer_norm(xn, n1, "ln6", affine=(gb[:, 0, :, :], gb[:, 1, :, :]))
                with ExitStack() as st2:
                    o_t = sb(st2, "o3_t", [CP, KC, TP])
                    attention("at3", "block2", n1, wq, wk, wv, masks[:, 3, :], o_t)
                    project("block2", o_t, lambda c: wo if c < 2 else wos, lambda c: bo if c < 2 else bos, x2, xn, width=Q4)
                layer_norm(x2, n1, "ln7", affine=(gb[:, 2, :, :], gb[:, 3, :, :]))
                with ExitStack() as st2:
                    hs = sb(st2, "f2_hs", [128, 18, Q4])
                    gelu_mlp("block2", n1, (0, 2), Q4, [(w1, C, w2, C)], b1, b2, [h, x2], h, hs)
                    gelu_mlp("block2", n1, (HALF, 2), Q4,
                             [(w1, keep[0], w2s[0], keep[0]), (w1, keep[2], w2s[2], keep[2]),
                              (w1, keep[1], w2s[1], keep[1])], b1, b2s, [h, x2], h, hs)

        def l3_ffn():
            R = 64
            with ExitStack() as st:
                we = sb(st, "e_w", [CP, KC, R])
                be = sb(st, "e_b", [R, 1])
                ws = sb(st, "sw_w", [R, E8])
                bs = sb(st, "sw_b", [1, E8])
                w1 = sb(st, "f3_w1", [CP, KC, E8 * R])
                b1 = sb(st, "f3_b1", [128, 4])
                w2 = sb(st, "f3_w2", [128, 4, C])
                b2 = sb(st, "f3_b2", [E8, C])
                pick = sb(st, "f3_pick", [E8, E8, R])
                enc = sb(st, "enc", [R, T])
                comb_t = sb(st, "f3_comb_t", [E8, T])
                g = sb(st, "f3_g", [128, 4, CH])
                hid = sb(st, "f3_hid", [128, 4, CH])
                encoded = S("encoded")
                with nc.Block() as block:
                    @block.sync
                    def _(sp):
                        for tile, src in ((we[:, :, :], a["e_w"]), (be[:, :], a["e_b"]), (ws[:, :], a["sw_w"]),
                                             (bs[:, :], a["sw_b"]), (w1[:, :, :], a["f3_w1"]), (b1[:, :], a["f3_b1"]),
                                             (w2[:, :, :], a["f3_w2"]), (b2[:, :], a["f3_b2"])):
                            sp.dma_start(tile, src).then_inc(loaded("ffn3").counted(16), 16)

                    @block.vector
                    def _(dve):
                        dve.tensor_copy(pick[:, :, :], bc(ident[:E8, :E8].unsqueeze(2), [E8, E8, R]))
                layer_norm(h, xn, "ln9")
                with nc.Block() as block:
                    @block.tensor
                    def _(pe):
                        pe.wait_ge(loaded("ffn3").sem, loaded("ffn3").total)
                        for c in range(NCH):
                            for k in range(KC):
                                last = pe.matmul(ps[:R, c, :CH], we[:, k, :], xn[:, k, c * CH:(c + 1) * CH],
                                                 start=k == 0, stop=k == KC - 1)
                        last.then_inc(encoded.sem, 1)

                    @block.scalar
                    def _(act):
                        act.wait_ge(encoded.sem, encoded.at(1))
                        act.activation(enc[:, :].rearrange("p (c t) -> p c t", c=NCH), ps[:R, 0:NCH, :CH], ACT.Identity,
                                       bias=be[:, 0:1])
                encoded.raised(1)

                def logits(pe, made):
                    for i in range(T // 128):
                        pe.matmul(ps[:, 0, 8 * i:8 * i + 8], enc[:, 128 * i:128 * i + 128], ws[:, :], start=True, stop=False)
                        last = pe.matmul(ps[:, 0, 8 * i:8 * i + 8], ones_row[:, :], bs[:, :], start=False, stop=True)
                    last.then_inc(made.sem, 1)
                route("r3", "ffn3", 1, logits, None, comb_t)

                hidden, gelued, weighted, summed, added = (S("f3_hidden"), S("f3_gelued"), S("f3_weighted"),
                                                           S("f3_summed"), S("f3_added"))
                picks = pick[:, :, :].rearrange("p (c e) r -> p c (e r)", e=2)
                with nc.Block() as block:
                    @block.tensor
                    def _(pe):
                        def chunk(c):
                            cols = bass.ds(c * CH, CH)
                            for m in range(4):
                                if after_first(4 * c + m - 1):
                                    pe.wait_ge(weighted.sem, weighted.at(4 * c + m - 1))
                                for k in range(KC):
                                    pe.matmul(ps[:, m % 2, :CH], w1[:, k, m * 128:(m + 1) * 128], xn[:, k, cols],
                                              start=k == 0, stop=k == KC - 1)
                                pe.matmul(ps[:, 2 + m % 2, :CH], picks[:, m, :], comb_t[:, cols],
                                          start=True, stop=True).then_inc(hidden.sem, 1)
                            pe.wait_ge(weighted.sem, weighted.at(4 * c + 4))
                            if after_first(c):
                                pe.wait_ge(added.sem, added.at(c))
                            for mo in range(KC):
                                for m in range(4):
                                    pe.matmul(ps[:CP, 4 + mo, :CH], w2[:, m, mo * CP:(mo + 1) * CP], hid[:, m, :],
                                              start=m == 0, stop=False)
                                last = pe.matmul(ps[:CP, 4 + mo, :CH], b2[:, mo * CP:(mo + 1) * CP], comb_t[:, cols],
                                                 start=False, stop=True)
                            last.then_inc(summed.sem, 1)
                        chunk(0)
                        with pe.Fori(1, NCH) as c:
                            chunk(c)

                    @block.scalar
                    def _(act):
                        def chunk(c):
                            for m in range(4):
                                act.wait_ge(hidden.sem, hidden.at(4 * c + m + 1))
                                if m == 0:
                                    if after_first(4 * c):
                                        act.wait_ge(weighted.sem, weighted.at(4 * c))
                                act.activation(g[:, m, :], ps[:, m % 2, :CH], ACT.Gelu,
                                               bias=b1[:, m:m + 1]).then_inc(gelued.sem, 1)
                        chunk(0)
                        with act.Fori(1, NCH) as c:
                            chunk(c)

                    @block.vector
                    def _(dve):
                        def chunk(c):
                            if after_first(c):
                                dve.wait_ge(summed.sem, summed.at(c))
                            for m in range(4):
                                dve.wait_ge(gelued.sem, gelued.at(4 * c + m + 1))
                                dve.tensor_tensor(hid[:, m, :], g[:, m, :], ps[:, 2 + m % 2, :CH],
                                                  ALU.mult).then_inc(weighted.sem, 1)
                            dve.wait_ge(summed.sem, summed.at(c + 1))
                            hc = h[:, :, bass.ds(c * CH, CH)]
                            dve.tensor_tensor(hc, hc, ps[:CP, 4:6, :CH], ALU.add).then_inc(added.sem, 1)
                        chunk(0)
                        with dve.Fori(1, NCH) as c:
                            chunk(c)

        def l3_mamba():
            G = 8
            NG = ST // G
            U = JC * NG
            SP = 2 * ST // 2
            READ_DVE = (1, 3, 4, 5)
            IMGS = Q4 // N
            x = xn
            layer_norm(h, xn, "ln8")
            with ExitStack() as st:
                w_in = sb(st, "m_w_in", [CP, KC, 2 * DI + 1])
                w_mid = sb(st, "m_w_mid", [128, JC, 150])
                w_dt = sb(st, "m_w_dt", [DR, DI])
                w_next = sb(st, "m_w_next", [128, JC, ST + 1 + C])
                w_now = sb(st, "m_w_now", [128, JC, 1 + C])
                a_pos = sb(st, "m_a_pos", [128, JC, ST])
                spread_sel = sb(st, "m_spread_sel", [96, 2 * ST], BF16)
                sq = sb(st, "m_sq", [CP, KC, Q4])
                lnv = sb(st, "m_lnv", [CP, Q4])
                rs = sb(st, "m_rs", [CP, Q4])
                hn = sb(st, "m_hn", [CP, KC, Q4])
                cv = sb(st, "m_cv", [128, JC, Q4])
                eu = sb(st, "m_eu", [128, JC, Q4])
                w1p = sb(st, "m_w1p", [128, JC, Q4])
                u = sb(st, "m_u_t", [128, 2, JC, Q4])
                ndt = sb(st, "m_ndt", [128, 2, JC, Q4])
                dtu = sb(st, "m_dtu", [128, 2, JC, Q4])
                zs = sb(st, "m_zs", [128, 2, JC, Q4])
                yu = sb(st, "m_yu", [128, Q4])
                bch = sb(st, "m_bch", [96, Q4], BF16)
                bcm = sb(st, "m_bcm", [96, Q4], BF16)
                bcr = sb(st, "m_bcr", [96, Q4])
                dtr = sb(st, "m_dtr_t", [DR, Q4])
                bcs = sb(st, "m_bcs", [128, 2, 2 * ST, Q4])
                decay = sb(st, "m_decay_t", [128, 2, G, Q4])
                hid = sb(st, "m_hid", [128, 3, G, Q4])

                NWD = 3
                w_prep, w_scan, w_set, a_set = S("m_w_prep"), S("m_w_scan"), S("m_w_set"), S("m_a_set")
                cleared = S("m_cleared")
                squared, ms, rstd, normed = S("m_squared"), S("m_ms"), S("m_rstd"), S("m_normed")
                u_made, conv0, conv, u_ready = S("m_u_made"), S("m_conv0"), S("m_conv"), S("m_u_ready")
                z_made, z_ready = S("m_z_made"), S("m_z_ready")
                bc_made, bc_hi, bc_rest, bc_mid, bc_lo = (S("m_bc_made"), S("m_bc_hi"), S("m_bc_rest"), S("m_bc_mid"),
                                                          S("m_bc_lo"))
                dtr_made, dtr_copied, dt_made, sp_act, sp_dve = (S("m_dtr_made"), S("m_dtr_copied"), S("m_dt_made"),
                                                                 S("m_softplus_act"), S("m_softplus_dve"))
                spread, spread_copied = S("m_spread"), S("m_spread_copied")
                decayed, driven, scanned, read_pool, read_dve, y_summed = (
                    S("m_decayed"), S("m_driven"), S("m_scanned"), S("m_read_pool"), S("m_read_dve"), S("m_y_summed"))
                gated, out_made, added = S("m_gated"), S("m_out_made"), S("m_added")
                NRP = U - len(READ_DVE)
                NRD = len(READ_DVE)

                def cols(q):
                    return slice(q * Q4, (q + 1) * Q4)

                def images(ap):
                    return ap.rearrange("p (b t) -> p b t", t=N)

                class Prepare:
                    @staticmethod
                    def act1(act, P, q, l):
                        act.wait_ge(w_prep.sem, w_prep.at(16 * NWD * (l + 1)))
                        if after_first(P - 3):
                            act.wait_ge(added.sem, added.at(P - 3))
                        if after_first(P):
                            act.wait_ge(ms.sem, ms.at(P))
                        act.activation(sq[:, :, :], x[:, :, cols(q)], ACT.Square).then_inc(squared.sem, 1)
                        act.wait_ge(ms.sem, ms.at(P + 1))
                        act.activation(lnv[:, :], ps[:CP, 3, :Q4], ACT.Ln, bias=eps[:CP, 0:1]).then_inc(rstd.sem, 1)
                        act.wait_ge(rstd.sem, rstd.at(2 * P + 1))
                        if after_first(P):
                            act.wait_ge(normed.sem, normed.at(P))
                        act.activation(rs[:, :], lnv[:, :], ACT.Exp, scale=-0.5).then_inc(rstd.sem, 1)
                        act.wait_ge(u_made.sem, u_made.at(P + 1))
                        if after_first(4 * P):
                            act.wait_ge(sp_dve.sem, sp_dve.at(4 * P))
                        for j in range(JC):
                            last = act.activation(cv[:, j, :], ps[:, j, :Q4], ACT.Identity, bias=w_mid[:, j, 148:149],
                                                  scale=w_mid[:, j, 147:148])
                        last.then_inc(conv0.sem, 1)

                    @staticmethod
                    def dve1(dve, P, q, l):
                        dve.wait_ge(w_prep.sem, w_prep.at(16 * NWD * (l + 1)))
                        dve.wait_ge(rstd.sem, rstd.at(2 * P + 2))
                        if after_first(P):
                            dve.wait_ge(z_made.sem, z_made.at(P))
                        for k in range(KC):
                            last = dve.scalar_tensor_tensor(hn[:, k, :], x[:, k, cols(q)], w_in[:, k, 2 * DI:],
                                                            rs[:, :], ALU.mult, ALU.mult)
                        last.then_inc(normed.sem, 1)
                        dve.wait_ge(conv0.sem, conv0.at(P + 1))
                        for s in range(1, 4):
                            if s > 1:
                                if after_first(3 * P + s - 1):
                                    dve.wait_ge(conv.sem, conv.at(3 * P + s - 1))
                            for j in range(JC):
                                o = images(cv[:, j, :])[:, :, s:]
                                last = dve.scalar_tensor_tensor(o, images(ps[:, j, :Q4])[:, :, :N - s],
                                                                w_mid[:, j, 147 - s:148 - s], o, ALU.mult, ALU.add)
                            last.then_inc(conv.sem, 1)

                    @staticmethod
                    def pe1(pe, P, q, l):
                        pe.wait_ge(squared.sem, squared.at(P + 1))
                        if after_first(P):
                            pe.wait_ge(dtr_copied.sem, dtr_copied.at(P))
                        for k in range(KC):
                            last = pe.matmul(ps[:CP, 3, :Q4], ones_mean[:CP, :CP], sq[:, k, :], start=k == 0, stop=k == KC - 1)
                        last.then_inc(ms.sem, 1)
                        pe.wait_ge(normed.sem, normed.at(P + 1))
                        if after_first(P - 1):
                            pe.wait_ge(added.sem, added.at(P - 1))
                        if after_first(5 * P - 4):
                            pe.wait_ge(sp_act.sem, sp_act.at(5 * P - 4))
                        for j in range(JC):
                            for k in range(KC):
                                last = pe.matmul(ps[:, j, :Q4], w_in[:, k, j * 128:(j + 1) * 128], hn[:, k, :],
                                                 start=k == 0, stop=k == KC - 1)
                        last.then_inc(u_made.sem, 1)
                        pe.wait_ge(rstd.sem, rstd.at(2 * P + 1))
                        if after_first(SP * P):
                            pe.wait_ge(spread_copied.sem, spread_copied.at(SP * P))
                        for j in range(JC):
                            for k in range(KC):
                                last = pe.matmul(ps[:, 3 + j, :Q4], w_in[:, k, DI + j * 128:DI + (j + 1) * 128],
                                                 hn[:, k, :], start=k == 0, stop=k == KC - 1)
                        last.then_inc(z_made.sem, 1)

                    @staticmethod
                    def act2(act, P, q):
                        act.wait_ge(conv.sem, conv.at(3 * P + 3))
                        if after_first(2 * JC * (P - 1)):
                            act.wait_ge(gated.sem, gated.at(2 * JC * (P - 1)))
                        act.activation(u[:, q % 2, :, :], cv[:, :, :], ACT.Silu).then_inc(u_ready.sem, 1)
                        act.wait_ge(z_made.sem, z_made.at(P + 1))
                        if after_first(P - 1):
                            act.wait_ge(out_made.sem, out_made.at(P - 1))
                        act.activation(zs[:, q % 2, :, :], ps[:, 3:6, :Q4], ACT.Silu).then_inc(z_ready.sem, 1)
                        act.wait_ge(bc_made.sem, bc_made.at(P + 1))
                        if after_first(SP * P):
                            act.wait_ge(spread.sem, spread.at(SP * P))
                        act.activation(bch[:, :], ps[:96, 3, :Q4], ACT.Copy).then_inc(bc_hi.sem, 1)
                        act.wait_ge(bc_rest.sem, bc_rest.at(P + 1))
                        if after_first(P):
                            act.wait_ge(bc_lo.sem, bc_lo.at(P))
                        act.activation(bcm[:, :], bcr[:, :], ACT.Copy).then_inc(bc_mid.sem, 1)
                        act.wait_ge(bc_mid.sem, bc_mid.at(2 * P + 1))
                        act.activation(bch[32:64, :], bcm[32:64, :], ACT.Copy).then_inc(bc_mid.sem, 1)
                        act.wait_ge(dtr_made.sem, dtr_made.at(P + 1))
                        if after_first(P):
                            act.wait_ge(dt_made.sem, dt_made.at(P))
                        act.activation(dtr[:, :], ps[:DR, 3, :Q4], ACT.Copy).then_inc(dtr_copied.sem, 1)

                    @staticmethod
                    def dve2(dve, P, q):
                        dve.wait_ge(bc_hi.sem, bc_hi.at(P + 1))
                        if after_first(P):
                            dve.wait_ge(bc_lo.sem, bc_lo.at(P))
                        dve.tensor_tensor(bcr[:, :], ps[:96, 3, :Q4], bch[:, :], ALU.subtract).then_inc(bc_rest.sem, 1)
                        dve.wait_ge(bc_mid.sem, bc_mid.at(2 * P + 2))
                        dve.tensor_tensor(bch[64:96, :], bcr[64:96, :], bcm[64:96, :], ALU.subtract).then_inc(bc_lo.sem, 1)

                    @staticmethod
                    def pe2(pe, P, q):
                        pe.wait_ge(u_ready.sem, u_ready.at(P + 1))
                        pe.wait_ge(z_ready.sem, z_ready.at(P + 1))
                        for j in range(JC):
                            last = pe.matmul(ps[:96, 3, :Q4], w_mid[:, j, 0:96], u[:, q % 2, j, :], start=j == 0, stop=j == JC - 1)
                        last.then_inc(bc_made.sem, 1)
                        pe.wait_ge(bc_rest.sem, bc_rest.at(P + 1))
                        for j in range(JC):
                            last = pe.matmul(ps[:DR, 3, :Q4], w_mid[:, j, 96:96 + DR], u[:, q % 2, j, :],
                                             start=j == 0, stop=j == JC - 1)
                        last.then_inc(dtr_made.sem, 1)
                        pe.wait_ge(dtr_copied.sem, dtr_copied.at(P + 1))
                        pe.wait_ge(conv.sem, conv.at(3 * P + 3))
                        for j in range(JC):
                            last = pe.matmul(ps[:, j, :Q4], w_dt[:, j * 128:(j + 1) * 128], dtr[:, :], start=True, stop=True)
                        last.then_inc(dt_made.sem, 1)

                    @staticmethod
                    def act3(act, P, q):
                        act.wait_ge(dt_made.sem, dt_made.at(P + 1))
                        act.wait_ge(u_ready.sem, u_ready.at(P + 1))
                        for j in range(JC):
                            last = act.activation(cv[:, j, :], ps[:, j, :Q4], ACT.Identity, bias=w_mid[:, j, 149:150])
                        last.then_inc(sp_act.sem, 1)
                        act.wait_ge(sp_act.sem, sp_act.at(5 * P + 1))
                        act.activation(eu[:, :, :], cv[:, :, :], ACT.Abs).then_inc(sp_act.sem, 1)
                        act.wait_ge(sp_act.sem, sp_act.at(5 * P + 2))
                        act.activation(eu[:, :, :], eu[:, :, :], ACT.Exp, scale=-1.0).then_inc(sp_act.sem, 1)
                        act.wait_ge(sp_act.sem, sp_act.at(5 * P + 3))
                        act.activation(w1p[:, :, :], eu[:, :, :], ACT.Identity, bias=1.0).then_inc(sp_act.sem, 1)
                        act.wait_ge(sp_dve.sem, sp_dve.at(4 * P + 1))
                        act.activation(w1p[:, :, :], w1p[:, :, :], ACT.Ln).then_inc(sp_act.sem, 1)

                    @staticmethod
                    def dve3(dve, P, q):
                        dve.wait_ge(sp_act.sem, sp_act.at(5 * P + 4))
                        dve.scalar_tensor_tensor(eu[:, :, :], w1p[:, :, :], 1.0, eu[:, :, :], ALU.subtract,
                                                 ALU.subtract).then_inc(sp_dve.sem, 1)
                        dve.wait_ge(sp_act.sem, sp_act.at(5 * P + 5))
                        dve.scalar_tensor_tensor(cv[:, :, :], cv[:, :, :], 0.0, w1p[:, :, :], ALU.max,
                                                 ALU.add).then_inc(sp_dve.sem, 1)
                        dve.wait_ge(sp_dve.sem, sp_dve.at(4 * P + 2))
                        if after_first(U * (P - 1)):
                            dve.wait_ge(decayed.sem, decayed.at(U * (P - 1)))
                        dve.tensor_tensor(ndt[:, q % 2, :, :], eu[:, :, :], cv[:, :, :], ALU.subtract).then_inc(sp_dve.sem, 1)
                        dve.wait_ge(sp_dve.sem, sp_dve.at(4 * P + 3))
                        if after_first(U * (P - 1)):
                            dve.wait_ge(driven.sem, driven.at(U * (P - 1)))
                        dve.scalar_tensor_tensor(dtu[:, q % 2, :, :], ndt[:, q % 2, :, :], -1.0, u[:, q % 2, :, :],
                                                 ALU.mult, ALU.mult).then_inc(sp_dve.sem, 1)

                    @staticmethod
                    def pe4(pe, P, q, first, last_pair):
                        for i in range(first, last_pair):
                            if i == 0:
                                pe.wait_ge(bc_lo.sem, bc_lo.at(P + 1))
                            if after_first(SP * P + i):
                                pe.wait_ge(spread_copied.sem, spread_copied.at(SP * P + i))
                            for r in range(2):
                                n = 2 * i + r
                                last = pe.matmul(ps[:, 4 + r, :Q4], bc(spread_sel[:, n:n + 1], [96, 128]), bch[:, :],
                                                 start=True, stop=True)
                            last.then_inc(spread.sem, 1)

                    @staticmethod
                    def act4(act, P, q, first, last_pair):
                        for i in range(first, last_pair):
                            if i == 0:
                                if after_first(U * (P - 1)):
                                    act.wait_ge(driven.sem, driven.at(U * (P - 1)))
                                if after_first(NRP * (P - 1)):
                                    act.wait_ge(read_pool.sem, read_pool.at(NRP * (P - 1)))
                                if after_first(NRD * (P - 1)):
                                    act.wait_ge(read_dve.sem, read_dve.at(NRD * (P - 1)))
                            act.wait_ge(spread.sem, spread.at(SP * P + i + 1))
                            act.activation(bcs[:, q % 2, 2 * i:2 * i + 2, :], ps[:, 4:6, :Q4],
                                           ACT.Copy).then_inc(spread_copied.sem, 1)

                def w_prep_needed(l):
                    return w_prep, 16 * NWD * (l + 1)

                def set_a(act, l, Q):
                    act.wait_ge(w_scan.sem, w_scan.at(16 * (l + 1)))
                    if after_first(U * Q):
                        act.wait_ge(decayed.sem, decayed.at(U * Q))
                    act.activation(a_pos[:, :, :], w_next[:, :, :ST], ACT.Exp).then_inc(a_set.sem, 1)

                def decays(act, Q, q, s, l):
                    j, g = divmod(s, NG)
                    if s == 0:
                        act.wait_ge(sp_dve.sem, sp_dve.at(4 * Q + 3))
                        act.wait_ge(a_set.sem, a_set.at(l + 1))
                    if after_first(U * Q + s - 1):
                        act.wait_ge(scanned.sem, scanned.at(U * Q + s - 1))
                    for n in range(G):
                        last = act.activation(images(decay[:, s % 2, n, :])[:, :, 1:], images(ndt[:, q % 2, j, :])[:, :, 1:],
                                              ACT.Exp, scale=a_pos[:, j, g * G + n:g * G + n + 1])
                    last.then_inc(decayed.sem, 1)

                def drive(pool, Q, q, s):
                    j, g = divmod(s, NG)
                    if s == 0:
                        pool.wait_ge(sp_dve.sem, sp_dve.at(4 * Q + 4))
                    if s < 2:
                        pool.wait_ge(spread_copied.sem, spread_copied.at(SP * Q + (s + 1) * SP // 4))
                    if after_first(U * Q + s - 2):
                        pool.wait_ge(y_summed.sem, y_summed.at(U * Q + s - 2))
                    pool.tensor_tensor(hid[:, s % 3, :, :], bcs[:, q % 2, g * G:(g + 1) * G, :],
                                       bc(dtu[:, q % 2, j:j + 1, :], [128, G, Q4]), ALU.mult).then_inc(driven.sem, 1)

                def scan(dve, Q, s):
                    dve.wait_ge(decayed.sem, decayed.at(U * Q + s + 1))
                    dve.wait_ge(driven.sem, driven.at(U * Q + s + 1))
                    d = decay[:, s % 2, :, :].rearrange("p n t -> p (n t)")
                    v = hid[:, s % 3, :, :].rearrange("p n t -> p (n t)")
                    dve.tensor_tensor_scan(v, d, v, 0.0, ALU.mult, ALU.add).then_inc(scanned.sem, 1)

                def read(eng, Q, q, s, done):
                    g = s % NG
                    eng.wait_ge(scanned.sem, scanned.at(U * Q + s + 1))
                    if s < 2:
                        eng.wait_ge(spread_copied.sem, spread_copied.at(SP * (Q + 1)))
                    v = hid[:, s % 3, :, :]
                    eng.tensor_tensor(v, v, bcs[:, q % 2, ST + g * G:ST + (g + 1) * G, :], ALU.mult).then_inc(done.sem, 1)

                def sum_y(pe, Q, q, s):
                    j, g = divmod(s, NG)
                    if s in READ_DVE:
                        pe.wait_ge(read_dve.sem, read_dve.at(NRD * Q + READ_DVE.index(s) + 1))
                    else:
                        pe.wait_ge(read_pool.sem, read_pool.at(NRP * Q + len([r for r in range(s) if r not in READ_DVE]) + 1))
                    if g == 0:
                        if after_first(2 * (JC * Q + j - 1)):
                            pe.wait_ge(gated.sem, gated.at(2 * (JC * Q + j - 1)))
                    for n in range(G):
                        last = pe.matmul(ps[:, 6 + (JC * q + j) % 2, :Q4], ident[:, :], hid[:, s % 3, n, :],
                                         start=g == 0 and n == 0, stop=g == NG - 1 and n == G - 1)
                    last.then_inc(y_summed.sem, 1)

                def gate(dve, Q, q, j, l):
                    Y = JC * Q + j
                    dve.wait_ge(w_set.sem, w_set.at(l + 1))
                    dve.wait_ge(y_summed.sem, y_summed.at(U * Q + NG * (j + 1)))
                    if after_first(2 * Y):
                        dve.wait_ge(gated.sem, gated.at(2 * Y))
                    dve.scalar_tensor_tensor(yu[:, :], u[:, q % 2, j, :], w_now[:, j, 0:1],
                                             ps[:, 6 + (JC * q + j) % 2, :Q4], ALU.mult, ALU.add).then_inc(gated.sem, 1)
                    dve.wait_ge(gated.sem, gated.at(2 * Y + 1))
                    dve.wait_ge(z_ready.sem, z_ready.at(Q + 1))
                    dve.tensor_tensor(zs[:, q % 2, j, :], zs[:, q % 2, j, :], yu[:, :], ALU.mult).then_inc(gated.sem, 1)

                def out_proj(pe, Q, q, l, prepared):
                    pe.wait_ge(gated.sem, gated.at(2 * JC * (Q + 1)))
                    pe.wait_ge(w_set.sem, w_set.at(l + 1))
                    pe.wait_ge(sp_act.sem, sp_act.at(5 * (prepared - 1) + 1))
                    for m in range(KC):
                        for j in range(JC):
                            last = pe.matmul(ps[:CP, m, :Q4], w_now[:, j, 1 + m * CP:1 + (m + 1) * CP], zs[:, q % 2, j, :],
                                             start=j == 0, stop=j == JC - 1)
                    last.then_inc(out_made.sem, 1)

                def add_out(dve, Q, q):
                    dve.wait_ge(out_made.sem, out_made.at(Q + 1))
                    dve.tensor_tensor(x[:, :, cols(q)], x[:, :, cols(q)], ps[:CP, 0:2, :Q4], ALU.add).then_inc(added.sem, 1)

                def set_w(act, l, Q):
                    act.wait_ge(w_scan.sem, w_scan.at(16 * (l + 1)))
                    if after_first(Q):
                        act.wait_ge(out_made.sem, out_made.at(Q))
                    act.activation(w_now[:, :, :], w_next[:, :, ST:], ACT.Copy).then_inc(w_set.sem, 1)

                with nc.Block() as block:
                    @block.sync
                    def _(sp):
                        def prep_weights(l):
                            if after_first(l):
                                sp.wait_ge(sp_act.sem, sp_act.at(20 * l - 4))
                            sp.wait_ge(w_scan.sem, w_scan.at(16))
                            one = bass.ds(l, 1)
                            sp.dma_start(w_in[:, :, :], a["m_w_in"][one].rearrange("l p k c -> (l p) k c")
                                         ).then_inc(w_prep.sem, 16)
                            sp.dma_start(w_mid[:, :, :], a["m_w_mid"][one].rearrange("l p k c -> (l p) k c")
                                         ).then_inc(w_prep.sem, 16)
                            sp.dma_start(w_dt[:, :], a["m_w_dt"][one].rearrange("l p c -> (l p) c")
                                         ).then_inc(w_prep.sem, 16)

                        def scan_weights(l):
                            if after_first(l):
                                sp.wait_ge(a_set.sem, a_set.at(l))
                            if after_first(l):
                                sp.wait_ge(w_set.sem, w_set.at(l))
                            if not isinstance(l, int):
                                sp.wait_ge(w_scan.sem, w_scan.at(16))
                            sp.dma_start(w_next[:, :, :], a["m_w_scan"][bass.ds(l, 1)].rearrange("l p k c -> (l p) k c")
                                         ).then_inc(w_scan.sem, 16)
                        scan_weights(0)
                        prep_weights(0)
                        with sp.Fori(1, LAYERS) as l:
                            scan_weights(l)
                            prep_weights(l)

                    @block.gpsimd
                    def _(pool):
                        def layer(l):
                            for q in range(4):
                                Q = 4 * l + q
                                drive(pool, Q, q, 0)
                                drive(pool, Q, q, 1)
                                for s in range(U):
                                    if s not in READ_DVE:
                                        read(pool, Q, q, s, read_pool)
                                    if s + 2 < U:
                                        drive(pool, Q, q, s + 2)
                        layer(0)
                        with pool.Fori(1, LAYERS) as l:
                            layer(l)

                    @block.tensor
                    def _(pe):
                        def layer(l, last):
                            for q in range(4):
                                Q, P, p = 4 * l + q, 4 * l + q + 1, (q + 1) % 4
                                more = not (last and q == 3)
                                if not (isinstance(Q, int) and Q == 0):
                                    out_proj(pe, Q - 1, (q - 1) % 4, l if q else l - 1, Q + 1)
                                sum_y(pe, Q, q, 0)
                                if more:
                                    Prepare.pe1(pe, P, p, l)
                                sum_y(pe, Q, q, 1)
                                if more:
                                    Prepare.pe2(pe, P, p)
                                sum_y(pe, Q, q, 2)
                                if more:
                                    Prepare.pe4(pe, P, p, 0, SP // 2)
                                sum_y(pe, Q, q, 3)
                                if more:
                                    Prepare.pe4(pe, P, p, SP // 2, SP)
                                sum_y(pe, Q, q, 4)
                                sum_y(pe, Q, q, 5)
                        pe.wait_ge(w_prep.sem, w_prep.at(16 * NWD))
                        pe.wait_ge(cleared.sem, cleared.at(1))
                        Prepare.pe1(pe, 0, 0, 0)
                        Prepare.pe2(pe, 0, 0)
                        Prepare.pe4(pe, 0, 0, 0, SP)
                        layer(0, False)
                        with pe.Fori(1, LAYERS - 1) as l:
                            layer(l, False)
                        layer(LAYERS - 1, True)
                        out_proj(pe, 4 * LAYERS - 1, 3, LAYERS - 1, 4 * LAYERS)

                    @block.scalar
                    def _(act):
                        def layer(l, last):
                            for q in range(4):
                                Q, P, p = 4 * l + q, 4 * l + q + 1, (q + 1) % 4
                                more = not (last and q == 3)
                                if q == 0:
                                    set_a(act, l, Q)
                                decays(act, Q, q, 0, l)
                                decays(act, Q, q, 1, l)
                                if q == 0:
                                    set_w(act, l, Q)
                                if more:
                                    Prepare.act1(act, P, p, l + 1 if q == 3 else l)
                                decays(act, Q, q, 2, l)
                                if more:
                                    Prepare.act2(act, P, p)
                                decays(act, Q, q, 3, l)
                                if more:
                                    Prepare.act3(act, P, p)
                                    Prepare.act4(act, P, p, 0, SP // 2)
                                decays(act, Q, q, 4, l)
                                if more:
                                    Prepare.act4(act, P, p, SP // 2, SP)
                                decays(act, Q, q, 5, l)
                        Prepare.act1(act, 0, 0, 0)
                        Prepare.act2(act, 0, 0)
                        Prepare.act3(act, 0, 0)
                        Prepare.act4(act, 0, 0, 0, SP)
                        layer(0, False)
                        with act.Fori(1, LAYERS - 1) as l:
                            layer(l, False)
                        layer(LAYERS - 1, True)

                    @block.vector
                    def _(dve):
                        def layer(l, last):
                            for q in range(4):
                                Q, P, p = 4 * l + q, 4 * l + q + 1, (q + 1) % 4
                                more = not (last and q == 3)
                                scan(dve, Q, 0)
                                if not (isinstance(Q, int) and Q == 0):
                                    gate(dve, Q - 1, (q - 1) % 4, 2, l if q else l - 1)
                                    add_out(dve, Q - 1, (q - 1) % 4)
                                scan(dve, Q, 1)
                                read(dve, Q, q, 1, read_dve)
                                if more:
                                    Prepare.dve1(dve, P, p, l + 1 if q == 3 else l)
                                scan(dve, Q, 2)
                                gate(dve, Q, q, 0, l)
                                if more:
                                    Prepare.dve2(dve, P, p)
                                scan(dve, Q, 3)
                                read(dve, Q, q, 3, read_dve)
                                if more:
                                    Prepare.dve3(dve, P, p)
                                scan(dve, Q, 4)
                                gate(dve, Q, q, 1, l)
                                read(dve, Q, q, 4, read_dve)
                                scan(dve, Q, 5)
                                read(dve, Q, q, 5, read_dve)
                        for r in range(3):
                            dve.tensor_copy(spread_sel[32 * r:32 * r + 32, :], ident[32 * r:32 * r + 32, 32 * r:32 * r + 32])
                        dve.memset(decay[:, :, :, :], 0.0).then_inc(cleared.sem, 1)
                        Prepare.dve1(dve, 0, 0, 0)
                        Prepare.dve2(dve, 0, 0)
                        Prepare.dve3(dve, 0, 0)
                        layer(0, False)
                        with dve.Fori(1, LAYERS - 1) as l:
                            layer(l, False)
                        layer(LAYERS - 1, True)
                        gate(dve, 4 * LAYERS - 1, 3, 2, LAYERS - 1)
                        add_out(dve, 4 * LAYERS - 1, 3)

            with ExitStack() as st:
                fw = sb(st, "final_w", [CP, KC])
                sq = sb(st, "fin_sq", [CP, KC, T])
                std = sb(st, "fin_std", [CP, T])
                fsq, fms, fstd, finv = S("fin_squared"), S("fin_ms"), S("fin_std_made"), S("fin_steps")
                with nc.Block() as block:
                    @block.sync
                    def _(sp):
                        sp.dma_start(fw[:, :], a["final_w"]).then_inc(loaded("final").counted(16), 16)

                    @block.scalar
                    def _(act):
                        act.activation(sq[:, :, :], xn[:, :, :T], ACT.Square).then_inc(fsq.sem, 1)
                        act.wait_ge(fms.sem, fms.at(1))
                        act.activation(std[:, :].rearrange("p (c t) -> p c t", c=NCH), ps[:CP, 0:NCH, :CH], ACT.Sqrt,
                                       bias=eps[:CP, 0:1]).then_inc(fstd.sem, 1)

                    @block.tensor
                    def _(pe):
                        pe.wait_ge(fsq.sem, fsq.at(1))
                        for c in range(NCH):
                            for k in range(KC):
                                last = pe.matmul(ps[:CP, c, :CH], ones_mean[:CP, :CP], sq[:, k, c * CH:(c + 1) * CH],
                                                 start=k == 0, stop=k == KC - 1)
                        last.then_inc(fms.sem, 1)

                    @block.vector
                    def _(dve):
                        dve.wait_ge(fstd.sem, fstd.at(1))
                        dve.reciprocal(std[:, :], std[:, :]).then_inc(finv.sem, 1)
                        dve.wait_ge(loaded("final").sem, loaded("final").total)
                        dve.wait_ge(finv.sem, finv.at(1))
                        for k in range(KC):
                            last = dve.scalar_tensor_tensor(sq[:, k, :], xn[:, k, :T], fw[:, k:k + 1], std[:, :],
                                                            ALU.mult, ALU.mult)
                        last.then_inc(finv.sem, 1)
                        dve.wait_ge(finv.sem, finv.at(2))
                        dve.tensor_tensor(h[:, :, :T], h[:, :, :T], sq[:, :, :], ALU.add)

        for stage in (patch_embedding, l0_attention, l0_ffn, l1_attention, l1_ffn, l2_attention, l2_ffn, l3_mamba,
                      l3_ffn):
            stage()
        store_output()


def chunked(w, p):
    w = np.asarray(w)
    return np.ascontiguousarray(np.moveaxis(w.reshape((w.shape[0] // p, p) + w.shape[1:]), 0, 1))


def slots(w):
    w = np.asarray(w)
    out = np.zeros(w.shape[:-1] + (H, 32), w.dtype)
    out[..., :16] = w.reshape(w.shape[:-1] + (H, 16))
    return out.reshape(w.shape[:-1] + (H * 32,))


def swapped(w):
    w = np.asarray(w)
    return np.ascontiguousarray(w.reshape(w.shape[:-1] + (w.shape[-1] // 2, 2))[..., ::-1]).reshape(w.shape)


def attention_masks():
    i, j = np.meshgrid(np.arange(TW), np.arange(TW), indexing="ij")
    same = i // N == j // N
    kinds = [same & (i != j), same & (abs(i - j) <= 6), same & (i >= j), same]
    m = np.stack([np.where(k, 0.0, NEG) for k in kinds], 1).astype(np.float32)
    return np.ascontiguousarray(np.tile(m, (1, 1, 3)))


def rope_tables():
    inv = 1.0 / 10000.0 ** (np.arange(0, 16, 2, dtype=np.float32) / np.float32(16))
    f = np.arange(N, dtype=np.float32)[:, None] * inv[None, :].astype(np.float32)
    cos = np.repeat(np.cos(f), 2, axis=1).T
    sin = np.repeat(np.sin(f), 2, axis=1).T * np.where(np.arange(16) % 2 == 0, -1.0, 1.0)[:, None]
    t = np.zeros((4, 32, 4, IMG, N), np.float32)
    for part, (v, s) in enumerate(((cos, 0.25), (sin, 0.25), (cos, 1.0), (sin, 1.0))):
        t[:, :16, part] = (v * s)[None, :, None, :]
    return np.ascontiguousarray(t.reshape(128, 4, TW))


def layouts(i):
    i = {k: np.asarray(v) for k, v in i.items()}
    x = i["x"].reshape(B, 3, 6, 16, 6, 16).transpose(3, 5, 1, 0, 2, 4).reshape(768, T)
    d = {
        "patches": chunked(x, 128),
        "tok_g1": chunked(i["L0_tok_g1"].T, 128),
        "tok_w": chunked(i["L0_tok_W"].T, 128),
        "tok_b": chunked(i["L0_tok_b"], CP),
        "tok_g2": chunked(i["L0_tok_g2"].T, CP),
        "masks": attention_masks(),
        "a0_wq": chunked(i["L0_attn_w_qkv"][:, :768], CP),
        "a0_wk": chunked(i["L0_attn_w_qkv"][:, 768:1536], CP),
        "a0_wv": chunked(i["L0_attn_w_qkv"][:, 1536:], CP),
        "a0_wo": chunked(i["L0_attn_w_out"], 128),
        "a0_bo": chunked(i["L0_attn_b_out"], CP),
        "a0_scale": chunked(np.repeat(i["L0_attn_scale"], 64), 128),
    }
    qkv1, qkv2, qkv3 = i["L1_attn_w_qkv"], i["L2_attn_W_attn"], i["L2_ffn_w_qkv"]
    b2 = i["L2_attn_b_attn"]
    d |= {
        "moe_router": chunked(i["L0_ffn_router_w"].T, CP),
        "moe_balance": np.tile(i["L0_ffn_balance_bias"], (128, 1)),
        "moe_w1": np.concatenate([i["L0_ffn_w1"], i["L0_ffn_w_fc_sh"][None]]).reshape(9, KC, CP, C).transpose(2, 0, 1, 3),
        "moe_w2": np.concatenate([i["L0_ffn_w2"], i["L0_ffn_w_proj_sh"][None]]).reshape(9, KC, CP, C).transpose(2, 0, 1, 3),
        "a1_wq": chunked(slots(qkv1[:, :C]), CP),
        "a1_wk": chunked(slots(qkv1[:, C:2 * C]), CP),
        "a1_wv": chunked(qkv1[:, 2 * C:], CP),
        "a1_wo": chunked(i["L1_attn_w_proj"], CP),
        "a1_bo": chunked(i["L1_attn_b_proj"], CP),
        "f1_w1": chunked(i["L1_ffn_in_weight"].T, CP),
        "f1_b1": chunked(i["L1_ffn_in_bias"], 128),
        "f1_w2": chunked(i["L1_ffn_out_weight"], 128),
        "a2_wq": chunked(slots(qkv2[:, :C]), CP),
        "a2_wk": chunked(slots(qkv2[:, C:2 * C]), CP),
        "a2_wqs": chunked(slots(swapped(qkv2[:, :C])), CP),
        "a2_wks": chunked(slots(swapped(qkv2[:, C:2 * C])), CP),
        "a2_wv": chunked(qkv2[:, 2 * C:], CP),
        "a2_bqk": np.stack([chunked(slots(v), 128) for v in (b2[:C], swapped(b2[:C]), b2[C:2 * C],
                                                             swapped(b2[C:2 * C]))], 1),
        "a2_bv": b2[None, 2 * C:],
        "a2_wo": chunked(i["L2_attn_W_proj"], CP),
        "a2_bo": chunked(i["L2_attn_b_proj"], CP),
        "rope": rope_tables(),
        "a3_wq": chunked(slots(qkv3[:, :C]), CP),
        "a3_wk": chunked(slots(qkv3[:, C:2 * C]), CP),
        "a3_wv": chunked(qkv3[:, 2 * C:], CP),
        "a3_wo": chunked(i["L2_ffn_w_proj"], CP),
        "a3_bo": chunked(i["L2_ffn_b_proj"], CP),
        "gumbel": np.tile(i["L2_ffn_gumbel_weights"], (128, 1)),
        "n12_gb": np.stack([np.stack([chunked(i[f"L2_ffn_n{n}{path}_{p}"], CP) for path in "ls"], 1)
                            for n in "12" for p in "gb"], 1),
        "f2_w1": chunked(i["L2_ffn_w_fc1"], CP),
        "f2_b1": chunked(i["L2_ffn_b_fc1"], 128),
        "f2_w2": chunked(i["L2_ffn_w_fc2"], 128),
        "f2_b2": chunked(i["L2_ffn_b_fc2"], CP),
        "e_w": chunked(i["L3_ffn_enc_w"], CP),
        "e_b": i["L3_ffn_enc_b"][:, None],
        "sw_w": i["L3_ffn_sw_w"],
        "sw_b": i["L3_ffn_sw_b"][None],
        "f3_w1": chunked(i["L3_ffn_w1"].transpose(1, 0, 2).reshape(C, 512), CP),
        "f3_b1": chunked(i["L3_ffn_b1"].reshape(512), 128),
        "f3_w2": chunked(i["L3_ffn_w2"].reshape(512, C), 128),
        "f3_b2": i["L3_ffn_b2"],
    }
    proj = i["L3_attn_x_proj_w"].transpose(0, 2, 1)
    d |= {
        "m_w_in": np.stack([chunked(np.concatenate([i["L3_attn_in_proj_w"][l].T, i["L3_attn_norm_w"][l][:, None]], 1), CP)
                            for l in range(LAYERS)]),
        "m_w_mid": np.stack([chunked(np.concatenate(
            [proj[l][:, DR:]] * 3 + [proj[l][:, :DR], i["L3_attn_conv_w"][l][:, 0], i["L3_attn_conv_b"][l][:, None],
                                     i["L3_attn_dt_proj_b"][l][:, None]], 1), 128) for l in range(LAYERS)]),
        "m_w_dt": i["L3_attn_dt_proj_w"].transpose(0, 2, 1),
        "m_w_scan": np.stack([chunked(np.concatenate(
            [i["L3_attn_A_log"][l], i["L3_attn_D"][l][:, None], i["L3_attn_out_proj_w"][l].T], 1), 128)
            for l in range(LAYERS)]),
        "final_w": chunked(i["L3_attn_final_norm_w"], CP),
    }
    return d


def kernel(**inputs):
    import concourse.bacc as bacc
    from concourse.bass_utils import run_bass_kernel_spmd

    nc = bacc.Bacc("TRN2", target_bir_lowering=False, num_devices=1)
    arrays, aps = {}, {}
    for name, v in layouts(inputs).items():
        arrays["in_" + name] = np.ascontiguousarray(v)
        aps[name] = nc.dram_tensor("in_" + name, v.shape, F32, kind="ExternalInput").ap()
    out = nc.dram_tensor("out_h", (CP, KC, T), F32, kind="ExternalOutput").ap()
    build(nc, aps, out)
    r = run_bass_kernel_spmd(nc, [arrays], core_ids=[0])
    got = r.results[0]["out_h"]
    return np.ascontiguousarray(got.transpose(1, 0, 2).reshape(C, B, N).transpose(1, 2, 0))
```

```python
from contextlib import ExitStack

import numpy as np

import concourse.bass as bass
from concourse import mybir

F32 = mybir.dt.float32
BF16 = mybir.dt.bfloat16
ALU = mybir.AluOpType
ACT = mybir.ActivationFunctionType
AX = mybir.AxisListType

B = 32
N = 36
C = 192
T = B * N
CP = 96
KC = C // CP
IMG = 3
TW = IMG * N
NT = -(-B // IMG)
TP = NT * TW
CH = 384
NCH = T // CH
HALF = T // 2
Q4 = T // 4
H = 12
LN_EPS = 1e-5
TOK_EPS = 1e-4
NEG = -1e30
KEEP = int(N * 0.75)
LAYERS = 16
DI = 384
JC = DI // 128
ST = 16
DR = 48
E8 = 8


class Signal:

    def __init__(self, nc, name):
        self.sem = nc.alloc_semaphore(name)
        self.base = 0
        self.total = 0

    def at(self, n):
        return n + self.base

    def raised(self, n):
        self.base += n

    def next(self):
        self.total += 1
        return self.base + self.total

    def restart(self):
        self.base, self.total = self.base + self.total, 0

    def counted(self, n):
        self.total += n
        return self.sem


def after_first(n):
    return not isinstance(n, int) or n > 0


def bc(ap, shape):
    return ap.broadcast_to(shape)


def build(nc, a, out):
    ctx = ExitStack()
    sig = {}

    def S(name):
        if name not in sig:
            sig[name] = Signal(nc, name)
        return sig[name]

    def sb(stack, name, shape, dt=F32):
        return stack.enter_context(nc.sbuf_tensor(name, shape, dt))

    with ctx:
        h = sb(ctx, "h", [CP, KC, TP])
        xn = sb(ctx, "xn", [CP, KC, TP])
        ones_mean = sb(ctx, "ones_mean", [128, 128])
        ident = sb(ctx, "ident", [128, 128])
        ident_bf = sb(ctx, "ident_bf", [TW, TW], BF16)
        eps = sb(ctx, "eps", [128, 2])
        ones_row = sb(ctx, "ones_row", [1, 128])
        ps = ctx.enter_context(nc.psum_tensor("ps", [128, 8, 512], F32))

        def loaded(group):
            return S("loaded_" + group)

        NB = T // 128

        def layer_norm(src, dst, name, affine=None, loads=(), also_dve=None, also_pool=None):
            with ExitStack() as st:
                d = sb(st, name + "_d", [CP, KC, T])
                sq = sb(st, name + "_sq", [CP, KC, T])
                std = sb(st, name + "_std", [128, NB])
                rstd = sb(st, name + "_rstd", [128, NB])
                mean_ready, centered, squared = S("ln_mean"), S("ln_centered"), S("ln_squared")
                var_ready, std_ready, rstd_ready = S("ln_var"), S("ln_std"), S("ln_rstd")
                rstd_spread, normed = S("ln_rstd_spread"), S("ln_normed")
                with nc.Block() as block:
                    @block.sync
                    def _(sp):
                        for group, pairs in loads:
                            for tile, source in pairs:
                                sp.dma_start(tile, source).then_inc(loaded(group).counted(16), 16)

                    @block.gpsimd
                    def _(pool):
                        if also_pool:
                            also_pool(pool)

                    @block.tensor
                    def _(pe):
                        for c in range(NCH):
                            for k in range(KC):
                                last = pe.matmul(ps[:CP, c, :CH], ones_mean[:CP, :CP], src[:, k, c * CH:(c + 1) * CH],
                                                 start=k == 0, stop=k == KC - 1)
                            last.then_inc(mean_ready.sem, 1)
                        for c in range(NCH):
                            pe.wait_ge(squared.sem, squared.at(c + 1))
                            for i in range(c * NB // NCH, (c + 1) * NB // NCH):
                                for k in range(KC):
                                    last = pe.matmul(ps[:, 3, i:i + 1], sq[:, k, i * 128:(i + 1) * 128],
                                                     ones_mean[:CP, 0:1], start=k == 0, stop=k == KC - 1)
                        last.then_inc(var_ready.sem, 1)
                        pe.wait_ge(rstd_ready.sem, rstd_ready.at(1))
                        for c in range(NCH):
                            for i in range(NB // NCH):
                                block_of = c * NB // NCH + i
                                last = pe.matmul(ps[:CP, 4 + c, i * 128:(i + 1) * 128],
                                                 bc(rstd[:, block_of:block_of + 1], [128, CP]), ident[:, :],
                                                 start=True, stop=True)
                            last.then_inc(rstd_spread.sem, 1)

                    @block.vector
                    def _(dve):
                        for c in range(NCH):
                            cs = slice(c * CH, (c + 1) * CH)
                            dve.wait_ge(mean_ready.sem, mean_ready.at(c + 1))
                            dve.tensor_tensor(d[:, :, cs], src[:, :, cs], bc(ps[:CP, c:c + 1, :CH], [CP, KC, CH]),
                                              ALU.subtract).then_inc(centered.sem, 1)
                        dve.wait_ge(std_ready.sem, std_ready.at(1))
                        dve.reciprocal(rstd[:, :], std[:, :]).then_inc(rstd_ready.sem, 1)
                        for c in range(NCH):
                            cs = slice(c * CH, (c + 1) * CH)
                            dve.wait_ge(rstd_spread.sem, rstd_spread.at(c + 1))
                            dve.tensor_tensor(dst[:, :, cs], d[:, :, cs], bc(ps[:CP, 4 + c:5 + c, :CH], [CP, KC, CH]),
                                              ALU.mult).then_inc(normed.sem, 1)
                        if also_dve:
                            also_dve(dve)

                    @block.scalar
                    def _(act):
                        for c in range(NCH):
                            cs = slice(c * CH, (c + 1) * CH)
                            act.wait_ge(centered.sem, centered.at(c + 1))
                            act.activation(sq[:, :, cs], d[:, :, cs], ACT.Square).then_inc(squared.sem, 1)
                        act.wait_ge(var_ready.sem, var_ready.at(1))
                        act.activation(std[:, :], ps[:, 3, :NB], ACT.Sqrt, bias=eps[:, 0:1]).then_inc(std_ready.sem, 1)
                        if affine is not None:
                            gamma, beta = affine
                            act.wait_ge(normed.sem, normed.at(NCH))
                            for half in range(2):
                                hs = slice(half * HALF, (half + 1) * HALF)
                                for k in range(KC):
                                    act.activation(dst[:, k, hs], dst[:, k, hs], ACT.Identity,
                                                   bias=beta[:, half, k:k + 1], scale=gamma[:, half, k:k + 1])
                for s in (mean_ready, centered, squared, rstd_spread, normed):
                    s.raised(NCH)
                for s in (var_ready, std_ready, rstd_ready):
                    s.raised(1)

        def attention(name, group, x, wq, wk, wv, mask, out_t, heads16=True, rope=None, select=None):
            D = 16 if heads16 else 64
            NQ = H * (32 if heads16 else 64) // 128
            NG = 4 if heads16 else 2
            INNER = H * D
            OP = CP if heads16 else 128
            OC = INNER // OP
            VB = 7 if heads16 else 6

            def place(head):
                chunk, g = head // NG, head % NG
                if heads16:
                    return chunk, 32 * g, g, chunk
                return chunk, 64 * g, 2 * g + chunk // 3, chunk % 3

            with ExitStack() as st:
                xt = sb(st, name + "_xt", [CP, KC, TW])
                qt = sb(st, name + "_qt", [128, NQ, TW])
                kt = sb(st, name + "_kt", [128, NQ, TW])
                if rope:
                    rot = sb(st, name + "_rot", [128, 4, NQ, TW])
                vt = sb(st, name + "_vt", [TW, INNER])
                p = sb(st, name + "_p", [TW, 4, 3, TW])
                pt = sb(st, name + "_pt", [TW, 4, 3, TW])
                nmax = sb(st, name + "_nmax", [TW, 4, 3])
                total = sb(st, name + "_total", [TW, H])
                rtot = sb(st, name + "_rtot", [TW, H])
                o = sb(st, name + "_o", [TW, INNER])
                if select is not None:
                    m8 = sb(st, name + "_m8", [TW, 4, 3, 8])
                    kept = sb(st, name + "_kept", [TW, 4, 3, TW])
                    shifted = sb(st, name + "_shifted", [TW, 4, 3, TW])
                    se = sb(st, name + "_se", [TW, TW])
                    nscale = sb(st, name + "_nscale", [128, NQ])

                x_copied, qk_made, qk_copied = S("at_x_copied"), S("at_qk_made"), S("at_qk_copied")
                se_made, se_copied, scored, maxed = S("at_se_made"), S("at_se_copied"), S("at_scored"), S("at_maxed")
                exped, p_turned, p_copied = S("at_exped"), S("at_p_turned"), S("at_p_copied")
                v_made, v_copied, o_made, recip = S("at_v_made"), S("at_v_copied"), S("at_o_made"), S("at_recip")
                o_scaled, o_turned, o_copied = S("at_o_scaled"), S("at_o_turned"), S("at_o_copied")
                rotated, dropped, moved, capped, scale_set = (
                    S("at_rotated"), S("at_dropped"), S("at_moved"), S("at_capped"), S("at_scale"))
                scores_read = moved if select is not None else exped

                def chunks2(n):
                    return [(i // 3, (i % 3) * TW) for i in range(n)]

                def pair(first, n):
                    nb = n // 3
                    return ps[:, first:first + nb, :3 * TW].rearrange("p b (s t) -> p b s t", s=3)

                with nc.Block() as block:
                    @block.gpsimd
                    def _(pool):
                        def copy_x(t):
                            if after_first(t):
                                pool.wait_ge(v_made.sem, v_made.at(t))
                            pool.tensor_copy(xt[:, :, :], x[:, :, bass.ds(t * TW, TW)]).then_inc(x_copied.sem, 1)
                        copy_x(0)
                        with pool.Fori(1, NT) as t:
                            copy_x(t)

                    @block.tensor
                    def _(pe):
                        def front(t):
                            cols = bass.ds(t * TW, TW)
                            if after_first(t):
                                pe.wait_ge(v_copied.sem, v_copied.at(t))
                            if heads16 and after_first(t - 1):
                                pe.wait_ge(o_copied.sem, o_copied.at(t - 1))
                            for w, first in ((wq, 6), (wk, 4)):
                                for i, (b, col) in enumerate(chunks2(NQ)):
                                    for k in range(KC):
                                        last = pe.matmul(ps[:, first + b, col:col + TW], w[:, k, i * 128:(i + 1) * 128],
                                                         x[:, k, cols], start=k == 0, stop=k == KC - 1)
                            if rope:
                                for w, first in ((rope[0], 7), (rope[1], 5)):
                                    for i in range(NQ):
                                        for k in range(KC):
                                            last = pe.matmul(ps[:, first, i * TW:(i + 1) * TW],
                                                             w[:, k, i * 128:(i + 1) * 128], x[:, k, cols],
                                                             start=k == 0, stop=k == KC - 1)
                            last.then_inc(qk_made.sem, 1)
                            pe.wait_ge(qk_copied.sem, qk_copied.at(t + 1))
                            if select is not None:
                                for i in range(NQ):
                                    last = pe.matmul(ps[:TW, 6, :TW], qt[:, i, :], kt[:, i, :],
                                                     start=i == 0, stop=i == NQ - 1)
                                last.then_inc(se_made.sem, 1)
                            if after_first(t):
                                pe.wait_ge(scores_read.sem, scores_read.at(t))
                            for head in range(H):
                                chunk, r, b, s = place(head)
                                pe.matmul(ps[:TW, b, s * TW:(s + 1) * TW], qt[r:r + D, chunk, :],
                                          kt[r:r + D, chunk, :], start=s == 0, stop=False,
                                          skip_group_check=True)
                            for b in range(4):
                                last = pe.matmul(ps[:TW, b, :3 * TW], ident_bf[:, :], mask, start=False, stop=True,
                                                 skip_group_check=True)
                            last.then_inc(scored.sem, 1)

                        def values(t):
                            pe.wait_ge(x_copied.sem, x_copied.at(t + 1))
                            if not heads16 and after_first(t):
                                pe.wait_ge(o_copied.sem, o_copied.at(t))
                            if select is not None:
                                pe.wait_ge(se_copied.sem, se_copied.at(t + 1))
                            for half in range(1 if heads16 else 2):
                                w = INNER if heads16 else INNER // 2
                                for k in range(KC):
                                    last = pe.matmul(ps[:TW, VB + half, :w], xt[:, k, :], wv[:, k, half * w:(half + 1) * w],
                                                     start=k == 0, stop=k == KC - 1 and not rope)
                                if rope:
                                    last = pe.matmul(ps[:TW, VB, :w], ones_row[:, :TW], rope[4], start=False, stop=True)
                            last.then_inc(v_made.sem, 1)

                        def back(t, fronts):
                            pe.wait_ge(exped.sem, exped.at(t + 1))
                            pe.wait_ge(qk_copied.sem, qk_copied.at(fronts))
                            for g in range(3):
                                if g == 2:
                                    pe.wait_ge(p_copied.sem, p_copied.at(3 * t + 1))
                                for i in range(4):
                                    e = 4 * g + i
                                    last = pe.transpose(ps[:TW, 4 + g % 2, i * TW:(i + 1) * TW],
                                                        p[:, e // 3, e % 3, :], ident[:TW, :TW])
                                last.then_inc(p_turned.sem, 1)
                            pe.wait_ge(p_copied.sem, p_copied.at(3 * t + 3))
                            pe.wait_ge(v_copied.sem, v_copied.at(t + 1))
                            if select is not None:
                                pe.wait_ge(se_copied.sem, se_copied.at(fronts))
                            for head in range(H):
                                _, _, b, s = place(head)
                                half, col = (0, head * D) if heads16 else (head // 6, head % 6 * D)
                                last = pe.matmul(ps[:TW, 6 + half, col:col + D], pt[:, b, s, :],
                                                 vt[:, head * D:(head + 1) * D], start=True, stop=True)
                            last.then_inc(o_made.sem, 1)
                            pe.wait_ge(o_scaled.sem, o_scaled.at(t + 1))
                            for i in range(OC):
                                b, col = i // 3, (i % 3) * TW
                                last = pe.transpose(ps[:OP, 6 + b, col:col + TW], o[:, i * OP:(i + 1) * OP],
                                                    ident[:TW, :TW])
                            last.then_inc(o_turned.sem, 1)

                        pe.wait_ge(loaded(group).sem, loaded(group).total)
                        front(0)
                        values(0)
                        front(1)
                        back(0, 2)
                        values(1)
                        with pe.Fori(2, NT) as t:
                            front(t)
                            back(t - 1, t + 1)
                            values(t)
                        back(NT - 1, NT)

                    @block.scalar
                    def _(act):
                        def exps(t):
                            act.wait_ge(maxed.sem, maxed.at(t + 1))
                            if after_first(3 * t):
                                act.wait_ge(p_turned.sem, p_turned.at(3 * t))
                            if after_first(t):
                                act.wait_ge(recip.sem, recip.at(t))
                            for head in range(H):
                                _, _, b, s = place(head)
                                src = p[:, b, s, :] if select is not None else ps[:TW, b, s * TW:(s + 1) * TW]
                                if select is not None:
                                    src = kept[:, b, s, :]
                                last = act.activation(p[:, b, s, :], src, ACT.Exp, bias=nmax[:, b, s:s + 1],
                                                      accum_out=total[:, head:head + 1])
                            last.then_inc(exped.sem, 1)

                        def copy_turned(t):
                            if after_first(t):
                                act.wait_ge(o_made.sem, o_made.at(t))
                            ptf = pt[:, :, :, :].rearrange("p b s t -> p (b s) t")
                            for g in range(3):
                                act.wait_ge(p_turned.sem, p_turned.at(3 * t + g + 1))
                                act.activation(ptf[:, 4 * g:4 * g + 4, :],
                                               ps[:TW, 4 + g % 2, :4 * TW].rearrange("p (s t) -> p s t", s=4),
                                               ACT.Copy).then_inc(p_copied.sem, 1)
                        exps(0)
                        copy_turned(0)
                        exps(1)
                        with act.Fori(2, NT) as t:
                            copy_turned(t - 1)
                            exps(t)
                        copy_turned(NT - 1)

                    @block.vector
                    def _(dve):
                        def front(t):
                            dve.wait_ge(qk_made.sem, qk_made.at(t + 1))
                            if after_first(t):
                                dve.wait_ge(scored.sem, scored.at(t))
                            if rope:
                                bias, tables = rope[2], rope[3]
                                for part in range(4):
                                    bank = (6, 7, 4, 5)[part]
                                    for i in range(NQ):
                                        last = dve.scalar_tensor_tensor(
                                            rot[:, part, i, :], ps[:, bank, i * TW:(i + 1) * TW], bias[:, part, i:i + 1],
                                            tables[:, part, :], ALU.add, ALU.mult)
                                last.then_inc(rotated.sem, 1)
                                dve.wait_ge(rotated.sem, rotated.at(t + 1))
                                dve.tensor_tensor(qt[:, :, :], rot[:, 0, :, :], rot[:, 1, :, :], ALU.add)
                                dve.tensor_tensor(kt[:, :, :], rot[:, 2, :, :], rot[:, 3, :, :],
                                                  ALU.add).then_inc(qk_copied.sem, 1)
                            elif select is None:
                                dve.tensor_scalar(qt[:, :, :].unsqueeze(1), pair(6, NQ), D ** -0.5, None, ALU.mult)
                                dve.tensor_copy(kt[:, :, :].unsqueeze(1), pair(4, NQ)).then_inc(qk_copied.sem, 1)
                            else:
                                for i, (b, col) in enumerate(chunks2(NQ)):
                                    dve.tensor_scalar(qt[:, i, :], ps[:, 6 + b, col:col + TW], nscale[:, i:i + 1], None,
                                                      ALU.mult)
                                dve.tensor_copy(kt[:, :, :].rearrange("p (b s) t -> p b s t", s=3),
                                                pair(4, NQ)).then_inc(qk_copied.sem, 1)
                                dve.wait_ge(se_made.sem, se_made.at(t + 1))
                                dve.tensor_scalar(se[:, :], ps[:TW, 6, :TW], -1.0 / H, None,
                                                  ALU.mult).then_inc(se_copied.sem, 1)
                            dve.wait_ge(scored.sem, scored.at(t + 1))
                            if select is not None:
                                def shift(b0):
                                    dve.tensor_tensor(shifted[:, b0:b0 + 2, :, :],
                                                      bc(se[:, :].unsqueeze(1).unsqueeze(1), [TW, 2, 3, TW]),
                                                      ps[:TW, b0:b0 + 2, :3 * TW].rearrange("p b (s t) -> p b s t", s=3),
                                                      ALU.subtract)
                                dve.wait_ge(se_copied.sem, se_copied.at(t + 1))
                                shift(0)
                                for b in range(4):
                                    for s in range(3):
                                        last = dve.max(m8[:, b, s, :], ps[:TW, b, s * TW:(s + 1) * TW])
                                last.then_inc(dropped.sem, 1)
                                dve.wait_ge(dropped.sem, dropped.at(t + 1))
                                if after_first(t):
                                    dve.wait_ge(exped.sem, exped.at(t))
                                shift(2)
                                for b in range(4):
                                    for s in range(3):
                                        last = dve.match_replace(kept[:, b, s, :], m8[:, b, s, :],
                                                                 ps[:TW, b, s * TW:(s + 1) * TW], NEG)
                                last.then_inc(moved.sem, 1)
                                dve.wait_ge(moved.sem, moved.at(t + 1))
                                dve.scalar_tensor_tensor(kept[:, :, :, :].rearrange("p b s t -> p (b s t)"),
                                                         kept[:, :, :, :].rearrange("p b s t -> p (b s t)"), -0.5 * NEG,
                                                         shifted[:, :, :, :].rearrange("p b s t -> p (b s t)"),
                                                         ALU.add, ALU.min).then_inc(capped.sem, 1)
                                dve.wait_ge(capped.sem, capped.at(t + 1))
                                dve.tensor_reduce(nmax[:, :, :], kept[:, :, :, :], AX.X, ALU.max,
                                                  negate=True).then_inc(maxed.sem, 1)
                            else:
                                dve.tensor_reduce(nmax[:, :, :],
                                                  ps[:TW, 0:4, :3 * TW].rearrange("p b (s t) -> p b s t", s=3),
                                                  AX.X, ALU.max, negate=True).then_inc(maxed.sem, 1)

                        def values(t):
                            dve.wait_ge(v_made.sem, v_made.at(t + 1))
                            if after_first(t):
                                dve.wait_ge(o_made.sem, o_made.at(t))
                            if heads16:
                                dve.tensor_copy(vt[:, :], ps[:TW, VB, :INNER]).then_inc(v_copied.sem, 1)
                            else:
                                dve.tensor_copy(vt[:, :].rearrange("p (b c) -> p b c", b=2),
                                                ps[:TW, 6:8, :INNER // 2]).then_inc(v_copied.sem, 1)

                        def back(t):
                            dve.wait_ge(exped.sem, exped.at(t + 1))
                            dve.reciprocal(rtot[:, :], total[:, :]).then_inc(recip.sem, 1)
                            dve.wait_ge(recip.sem, recip.at(t + 1))
                            dve.wait_ge(o_made.sem, o_made.at(t + 1))
                            if after_first(t):
                                dve.wait_ge(o_turned.sem, o_turned.at(t))
                            nb = 1 if heads16 else 2
                            for b in range(nb):
                                hb = H // nb
                                last = dve.tensor_tensor(
                                    o[:, b * hb * D:(b + 1) * hb * D].rearrange("p (h d) -> p h d", d=D),
                                    ps[:TW, 6 + b, :hb * D].rearrange("p (h d) -> p h d", d=D),
                                    bc(rtot[:, b * hb:(b + 1) * hb].unsqueeze(2), [TW, hb, D]), ALU.mult)
                            last.then_inc(o_scaled.sem, 1)
                            dve.wait_ge(o_turned.sem, o_turned.at(t + 1))
                            if heads16:
                                dve.tensor_copy(out_t[:, :, bass.ds(t * TW, TW)],
                                                ps[:OP, 6, :OC * TW].rearrange("p (s t) -> p s t", t=TW)
                                                ).then_inc(o_copied.sem, 1)
                            else:
                                for b in range(2):
                                    last = dve.tensor_copy(out_t[:, 3 * b:3 * b + 3, bass.ds(t * TW, TW)],
                                                           ps[:OP, 6 + b, :3 * TW].rearrange("p (s t) -> p s t", s=3))
                                last.then_inc(o_copied.sem, 1)

                        dve.wait_ge(loaded(group).sem, loaded(group).total)
                        if select is not None:
                            dve.tensor_scalar(nscale[:, :], select, -1.0, None, ALU.mult).then_inc(scale_set.sem, 1)
                            dve.wait_ge(scale_set.sem, scale_set.at(1))
                        front(0)
                        values(0)
                        front(1)
                        back(0)
                        values(1)
                        with dve.Fori(2, NT) as t:
                            front(t)
                            back(t - 1)
                            values(t)
                        back(NT - 1)
                for s in (x_copied, qk_made, qk_copied, scored, maxed, exped, v_made, v_copied, o_made, recip,
                          o_scaled, o_turned, o_copied):
                    s.raised(NT)
                p_turned.raised(3 * NT)
                p_copied.raised(3 * NT)
                if rope:
                    rotated.raised(NT)
                if select is not None:
                    for s in (se_made, se_copied, dropped, moved, capped):
                        s.raised(NT)
                    scale_set.raised(1)

        def project(group, src, weight, bias, dst, res, width=CH):
            projected = S("projected")
            n_chunks = T // width
            with nc.Block() as block:
                @block.tensor
                def _(pe):
                    pe.wait_ge(loaded(group).sem, loaded(group).total)
                    for c in range(n_chunks):
                        w = weight(c)
                        n_k = w.shape[1]
                        for m in range(KC):
                            for k in range(n_k):
                                last = pe.matmul(ps[:CP, KC * c + m, :width], w[:, k, m * CP:(m + 1) * CP],
                                                 src[:, k, c * width:(c + 1) * width], start=k == 0, stop=k == n_k - 1)
                            last.then_inc(projected.sem, 1)

                @block.vector
                def _(dve):
                    for c in range(n_chunks):
                        cs = slice(c * width, (c + 1) * width)
                        for m in range(KC):
                            dve.wait_ge(projected.sem, projected.at(KC * c + m + 1))
                            dve.scalar_tensor_tensor(dst[:, m, cs], ps[:CP, KC * c + m, :width], bias(c)[:, m:m + 1],
                                                     res[:, m, cs], ALU.add, ALU.add)
            projected.raised(n_chunks * KC)

        masks = sb(ctx, "masks", [TW, 4, 3 * TW], BF16)
        with ExitStack() as st:
            masks_f = sb(st, "masks_f", [TW, 4, 3 * TW])
            identity_made = S("identity_made")
            with nc.Block() as block:
                @block.sync
                def _(sp):
                    sp.dma_start(masks_f[:, :, :], a["masks"]).then_inc(loaded("const").counted(16), 16)

                @block.gpsimd
                def _(pool):
                    pool.memset(ident[:, :], 0.0).then_inc(identity_made.sem, 1)
                    pool.memset(h[:, :, T:], 0.0)
                    pool.memset(xn[:, :, T:], 0.0)
                    pool.memset(eps[:, 0:1], LN_EPS)
                    pool.memset(eps[:, 1:2], TOK_EPS)
                    pool.memset(ones_row[:, :], 1.0)
                    pool.memset(ones_mean[:, :], 1.0 / C)
                    pool.wait_ge(identity_made.sem, identity_made.at(1))
                    pool.affine_select(out=ident[:, :], in_=ident[:, :], compare_op=ALU.not_equal, fill=1.0,
                                       base=0, pattern=[[-1, 128]], channel_multiplier=1).then_inc(identity_made.sem, 1)

                @block.scalar
                def _(act):
                    act.wait_ge(identity_made.sem, identity_made.at(2))
                    act.activation(ident_bf[:, :], ident[:TW, :TW], ACT.Copy)
                    act.wait_ge(loaded("const").sem, loaded("const").total)
                    act.activation(masks[:, :, :], masks_f[:, :, :], ACT.Copy)

        def patch_embedding():
            with ExitStack() as st:
                pT = sb(st, "patches", [128, 6, T])
                sq = sb(st, "tok_sq", [128, 6, T])
                g1 = sb(st, "tok_g1", [128, 6, N])
                wt = sb(st, "tok_w", [128, 6, C])
                bt = sb(st, "tok_b", [CP, KC])
                g2 = sb(st, "tok_g2", [CP, KC, N])
                part = sb(st, "tok_part", [128, 6, B])
                r1 = sb(st, "tok_r1", [CP, B])
                s1 = sb(st, "tok_s1", [CP, B])
                y = sb(st, "tok_y", [CP, KC, T])
                sq2 = sb(st, "tok_sq2", [CP, KC, T])
                part2 = sb(st, "tok_part2", [CP, KC, B])
                r2 = sb(st, "tok_r2", [CP, B])
                s2 = sb(st, "tok_s2", [CP, B])
                squared, gained, summed, ms_made, root, inv = (S("tok_squared"), S("tok_gained"), S("tok_summed"),
                                                              S("tok_ms"), S("tok_root"), S("tok_inv"))
                embedded, y_done, y_squared, y_gained = S("tok_embedded"), S("tok_y"), S("tok_y_squared"), S("tok_y_gained")
                with nc.Block() as block:
                    @block.sync
                    def _(sp):
                        for k in range(6):
                            sp.dma_start(pT[:, k, :], a["patches"][:, k, :]).then_inc(loaded(f"patches{k}").counted(16), 16)
                        for tile, src in ((g1[:, :, :], a["tok_g1"]), (wt[:, :, :], a["tok_w"]),
                                             (bt[:, :], a["tok_b"]), (g2[:, :, :], a["tok_g2"])):
                            sp.dma_start(tile, src).then_inc(loaded("tok").counted(16), 16)

                    @block.scalar
                    def _(act):
                        for k in range(6):
                            act.wait_ge(loaded(f"patches{k}").sem, loaded(f"patches{k}").total)
                            act.activation(sq[:, k, :], pT[:, k, :], ACT.Square).then_inc(squared.sem, 1)
                        act.wait_ge(ms_made.sem, ms_made.at(1))
                        act.activation(s1[:, :], ps[:CP, 6, :B], ACT.Sqrt, bias=eps[:CP, 1:2],
                                       scale=C / (N * 768.0)).then_inc(root.sem, 1)
                        act.wait_ge(y_done.sem, y_done.at(1))
                        act.activation(sq2[:, :, :], y[:, :, :], ACT.Square).then_inc(y_squared.sem, 1)
                        act.wait_ge(ms_made.sem, ms_made.at(2))
                        act.activation(s2[:, :], ps[:CP, 7, :B], ACT.Sqrt, bias=eps[:CP, 1:2],
                                       scale=1.0 / N).then_inc(root.sem, 1)

                    @block.gpsimd
                    def _(pool):
                        pool.wait_ge(loaded("tok").sem, loaded("tok").total)
                        for k in range(6):
                            pool.wait_ge(squared.sem, squared.at(k + 1))
                            v = pT[:, k, :].rearrange("p (b n) -> p b n", n=N)
                            pool.tensor_tensor(v, v, bc(g1[:, k:k + 1, :], [128, B, N]), ALU.mult).then_inc(gained.sem, 1)

                    @block.tensor
                    def _(pe):
                        pe.wait_ge(loaded("tok").sem, loaded("tok").total)
                        for k in range(6):
                            pe.wait_ge(gained.sem, gained.at(k + 1))
                            for c in range(NCH):
                                for m in range(KC):
                                    last = pe.matmul(ps[:CP, KC * c + m, :CH], wt[:, k, m * CP:(m + 1) * CP],
                                                     pT[:, k, c * CH:(c + 1) * CH], start=k == 0, stop=k == 5)
                        last.then_inc(embedded.sem, 1)
                        pe.wait_ge(summed.sem, summed.at(1))
                        for k in range(6):
                            last = pe.matmul(ps[:CP, 6, :B], ones_mean[:, :CP], part[:, k, :], start=k == 0, stop=k == 5)
                        last.then_inc(ms_made.sem, 1)
                        pe.wait_ge(summed.sem, summed.at(2))
                        for k in range(KC):
                            last = pe.matmul(ps[:CP, 7, :B], ones_mean[:CP, :CP], part2[:, k, :], start=k == 0,
                                             stop=k == KC - 1)
                        last.then_inc(ms_made.sem, 1)

                    @block.vector
                    def _(dve):
                        for k in range(6):
                            dve.wait_ge(squared.sem, squared.at(k + 1))
                            last = dve.tensor_reduce(part[:, k, :], sq[:, k, :].rearrange("p (b n) -> p b n", n=N),
                                                     AX.X, ALU.add)
                        last.then_inc(summed.sem, 1)
                        dve.wait_ge(root.sem, root.at(1))
                        dve.reciprocal(r1[:, :], s1[:, :]).then_inc(inv.sem, 1)
                        dve.wait_ge(inv.sem, inv.at(1))
                        dve.wait_ge(embedded.sem, embedded.at(1))
                        dve.wait_ge(loaded("tok").sem, loaded("tok").total)
                        rfull = sq[:CP, 0, :]
                        dve.tensor_copy(rfull.rearrange("p (b n) -> p b n", n=N),
                                        bc(r1[:, :].unsqueeze(2), [CP, B, N])).then_inc(inv.sem, 1)
                        dve.wait_ge(inv.sem, inv.at(2))
                        for c in range(NCH):
                            for m in range(KC):
                                last = dve.tensor_tensor(y[:, m, c * CH:(c + 1) * CH], ps[:CP, KC * c + m, :CH],
                                                         rfull[:, c * CH:(c + 1) * CH], ALU.mult)
                        last.then_inc(inv.sem, 1)
                        dve.wait_ge(inv.sem, inv.at(3))
                        for m in range(KC):
                            last = dve.tensor_scalar(y[:, m, :], y[:, m, :], bt[:, m:m + 1], None, ALU.add)
                        last.then_inc(y_done.sem, 1)
                        dve.wait_ge(y_squared.sem, y_squared.at(1))
                        dve.tensor_reduce(part2[:, :, :], sq2[:, :, :].rearrange("p k (b n) -> p k b n", n=N),
                                          AX.X, ALU.add).then_inc(summed.sem, 1)
                        for m in range(KC):
                            v = y[:, m, :].rearrange("p (b n) -> p b n", n=N)
                            last = dve.tensor_tensor(v, v, bc(g2[:, m:m + 1, :], [CP, B, N]), ALU.mult)
                        last.then_inc(y_gained.sem, 1)
                        dve.wait_ge(root.sem, root.at(2))
                        dve.reciprocal(r2[:, :], s2[:, :]).then_inc(inv.sem, 1)
                        dve.wait_ge(inv.sem, inv.at(4))
                        dve.wait_ge(y_gained.sem, y_gained.at(1))
                        for m in range(KC):
                            dve.tensor_tensor(h[:, m, :T].rearrange("p (b n) -> p b n", n=N),
                                              y[:, m, :].rearrange("p (b n) -> p b n", n=N),
                                              bc(r2[:, :].unsqueeze(2), [CP, B, N]), ALU.mult)

        def l0_attention():
            with ExitStack() as st:
                wq = sb(st, "w0q", [CP, KC, H * 64])
                wk = sb(st, "w0k", [CP, KC, H * 64])
                wv = sb(st, "w0v", [CP, KC, H * 64])
                wo = sb(st, "w0o", [128, 6, C])
                bo = sb(st, "b0o", [CP, KC])
                sc = sb(st, "scale0", [128, 6])
                o_t = sb(st, "o0_t", [128, 6, TP])
                loads = (("attn0", ((wq[:, :, :], a["a0_wq"]), (wk[:, :, :], a["a0_wk"]),
                    (wv[:, :, :], a["a0_wv"]), (wo[:, :, :], a["a0_wo"]),
                    (bo[:, :], a["a0_bo"]), (sc[:, :], a["a0_scale"]))),)
                layer_norm(h, xn, "ln0", loads=loads)
                attention("at0", "attn0", xn, wq, wk, wv, masks[:, 0, :], o_t, heads16=False, select=sc[:, :])
                project("attn0", o_t, lambda c: wo, lambda c: bo, h, h)

        def store_output():
            with nc.Block() as block:
                @block.sync
                def _(sp):
                    stored = S("stored")
                    sp.dma_start(out, h[:, :, :T]).then_inc(stored.sem, 16)
                    sp.wait_ge(stored.sem, 16)

        def route(name, group, top_n, logits, balance, comb_t):
            tiles = T // 128
            pad = 8 - top_n
            with ExitStack() as st:
                sc = sb(st, name + "_sc", [128, tiles, 8])
                choice = sb(st, name + "_choice", [128, tiles, 8 + pad])
                marked = sb(st, name + "_marked", [128, tiles, 8 + pad])
                top = sb(st, name + "_top", [128, tiles, 8])
                comb = sb(st, name + "_comb", [128, tiles, 8])
                tot = sb(st, name + "_tot", [128, tiles])
                rtot = sb(st, name + "_rtot", [128, tiles])
                made, scored, stepped, combined, turned = (S("route_logits"), S("route_scored"), S("route_stepped"),
                                                           S("route_combined"), S("route_turned"))
                with nc.Block() as block:
                    @block.tensor
                    def _(pe):
                        pe.wait_ge(loaded(group).sem, loaded(group).total)
                        logits(pe, made)
                        pe.wait_ge(combined.sem, combined.at(1))
                        for i in range(tiles):
                            last = pe.transpose(ps[:8, 1 + i // 3, i % 3 * 128:(i % 3 + 1) * 128], comb[:, i, :],
                                                ident[:, :])
                        last.then_inc(turned.sem, 1)

                    @block.scalar
                    def _(act):
                        if top_n == 2:
                            act.wait_ge(made.sem, made.at(1))
                            act.activation(sc[:, :, :], ps[:, 0, :tiles * 8].rearrange("p (t e) -> p t e", e=8),
                                           ACT.Sigmoid).then_inc(scored.sem, 1)
                        else:
                            act.wait_ge(scored.sem, scored.at(1))
                            act.activation(sc[:, :, :], sc[:, :, :], ACT.Exp).then_inc(scored.sem, 1)

                    @block.vector
                    def _(dve):
                        dve.memset(choice[:, :, :], 3 * NEG).then_inc(stepped.sem, 1)
                        dve.wait_ge(stepped.sem, stepped.next())
                        values = choice[:, :, :8]
                        if top_n == 2:
                            dve.wait_ge(loaded(group).sem, loaded(group).total)
                            dve.wait_ge(scored.sem, scored.at(1))
                            dve.tensor_tensor(values, sc[:, :, :],
                                                   bc(balance.unsqueeze(1), [128, tiles, 8]), ALU.add).then_inc(stepped.sem, 1)
                            dve.wait_ge(stepped.sem, stepped.next())
                        else:
                            dve.wait_ge(made.sem, made.at(1))
                            dve.tensor_copy(values, ps[:, 0, :tiles * 8].rearrange("p (t e) -> p t e", e=8)).then_inc(stepped.sem, 1)
                            dve.wait_ge(stepped.sem, stepped.next())
                        for i in range(tiles):
                            last = dve.max(top[:, i, :], choice[:, i, :8])
                        last.then_inc(stepped.sem, 1)
                        dve.wait_ge(stepped.sem, stepped.next())
                        if top_n == 1:
                            dve.tensor_tensor(sc[:, :, :], values, bc(top[:, :, 0:1], [128, tiles, 8]),
                                              ALU.subtract).then_inc(scored.sem, 1)
                        dve.memset(top[:, :, top_n:], 3 * NEG).then_inc(stepped.sem, 1)
                        dve.wait_ge(stepped.sem, stepped.next())
                        for i in range(tiles):
                            last = dve.match_replace(marked[:, i, :], top[:, i, :], choice[:, i, :], 2 * NEG)
                        last.then_inc(stepped.sem, 1)
                        dve.wait_ge(stepped.sem, stepped.next())
                        dve.tensor_scalar(comb[:, :, :], marked[:, :, :8], NEG, None, ALU.is_lt).then_inc(stepped.sem, 1)
                        dve.wait_ge(stepped.sem, stepped.next())
                        if top_n == 2:
                            dve.tensor_tensor(comb[:, :, :], comb[:, :, :], sc[:, :, :], ALU.mult).then_inc(stepped.sem, 1)
                            dve.wait_ge(stepped.sem, stepped.next())
                            dve.tensor_reduce(tot[:, :], comb[:, :, :], AX.X, ALU.add).then_inc(stepped.sem, 1)
                            dve.wait_ge(stepped.sem, stepped.next())
                            dve.tensor_scalar(tot[:, :], tot[:, :], 1e-20, None, ALU.add).then_inc(stepped.sem, 1)
                            dve.wait_ge(stepped.sem, stepped.next())
                        else:
                            dve.wait_ge(scored.sem, scored.at(2))
                            dve.tensor_reduce(tot[:, :], sc[:, :, :], AX.X, ALU.add).then_inc(stepped.sem, 1)
                            dve.wait_ge(stepped.sem, stepped.next())
                        dve.reciprocal(rtot[:, :], tot[:, :]).then_inc(stepped.sem, 1)
                        dve.wait_ge(stepped.sem, stepped.next())
                        dve.tensor_tensor(comb[:, :, :], comb[:, :, :], bc(rtot[:, :].unsqueeze(2), [128, tiles, 8]),
                                          ALU.mult).then_inc(combined.sem, 1)
                        dve.wait_ge(turned.sem, turned.at(1))
                        dve.tensor_copy(comb_t[:, :].rearrange("p (b t) -> p b t", b=3), ps[:8, 1:4, :CH])
                for s in (made, combined, turned):
                    s.raised(1)
                scored.raised(1 if top_n == 2 else 2)
                stepped.restart()

        def l0_ffn():
            with ExitStack() as st:
                w1 = sb(st, "moe_w1", [CP, E8 + 1, KC, C])
                w2 = sb(st, "moe_w2", [CP, E8 + 1, KC, C])
                wr = sb(st, "moe_router", [CP, KC, E8])
                bal = sb(st, "moe_balance", [128, E8])
                comb_t = sb(st, "moe_comb_t", [E8, T])
                pick = sb(st, "moe_pick", [E8, E8, CP])
                r = sb(st, "moe_r", [CP, 2, KC, CH])
                rc = sb(st, "moe_rc", [CP, KC, CH])
                hid = sb(st, "moe_hid", [CP, 2, KC, CH])
                def beside(dve):
                    dve.tensor_copy(pick[:, :, :], bc(ident[:E8, :E8].unsqueeze(2), [E8, E8, CP]))
                loads = (("router", ((wr[:, :, :], a["moe_router"]), (bal[:, :], a["moe_balance"]))),
                         ("moe", ((w1[:, :, :, :], a["moe_w1"]), (w2[:, :, :, :], a["moe_w2"]))),)
                layer_norm(h, xn, "ln1", loads=loads, also_dve=beside)

                def logits(pe, made):
                    for i in range(T // 128):
                        for k in range(KC):
                            last = pe.matmul(ps[:, 0, 8 * i:8 * i + 8], xn[:, k, 128 * i:128 * i + 128], wr[:, k, :],
                                             start=k == 0, stop=k == KC - 1)
                    last.then_inc(made.sem, 1)
                route("r0", "router", 2, logits, bal[:, :], comb_t)

                NE = E8 + 1
                hidden, relued, shared_out, weighted, summed, added = (
                    S("moe_hidden"), S("moe_relued"), S("moe_rc_made"), S("moe_weighted"), S("moe_summed"), S("moe_added"))
                with nc.Block() as block:
                    @block.tensor
                    def _(pe):
                        pe.wait_ge(loaded("moe").sem, loaded("moe").total)

                        def first(c, e):
                            n = c * NE + e
                            if after_first(n - 1 if e else n):
                                pe.wait_ge(weighted.sem, weighted.at(n - 1 if e else n))
                            for m in range(KC):
                                for k in range(KC):
                                    last = pe.matmul(ps[:CP, 2 * (e % 2) + m, :CH], w1[:, e, k, m * CP:(m + 1) * CP],
                                                     xn[:, k, bass.ds(c * CH, CH)], start=k == 0, stop=k == KC - 1)
                            if e < E8:
                                last = pe.matmul(ps[:CP, 6 + e % 2, :CH], pick[:, e, :], comb_t[:, bass.ds(c * CH, CH)],
                                                 start=True, stop=True)
                            last.then_inc(hidden.sem, 1)

                        def second(c, e):
                            n = c * NE + e
                            pe.wait_ge(weighted.sem, weighted.at(n + 1))
                            if e == 0:
                                if after_first(c):
                                    pe.wait_ge(added.sem, added.at(c))
                            for m in range(KC):
                                for k in range(KC):
                                    last = pe.matmul(ps[:CP, 4 + m, :CH], w2[:, e, k, m * CP:(m + 1) * CP],
                                                     hid[:, e % 2, k, :], start=e == 0 and k == 0,
                                                     stop=e == NE - 1 and k == KC - 1)
                            last.then_inc(summed.sem, 1)

                        def chunk(c):
                            first(c, 0)
                            for e in range(NE):
                                if e + 1 < NE:
                                    first(c, e + 1)
                                second(c, e)
                        chunk(0)
                        with pe.Fori(1, NCH) as c:
                            chunk(c)

                    @block.scalar
                    def _(act):
                        def chunk(c):
                            for e in range(NE):
                                n = c * NE + e
                                act.wait_ge(hidden.sem, hidden.at(n + 1))
                                act.activation(r[:, e % 2, :, :], ps[:CP, 2 * (e % 2):2 * (e % 2) + 2, :CH],
                                               ACT.Relu).then_inc(relued.sem, 1)
                        chunk(0)
                        with act.Fori(1, NCH) as c:
                            chunk(c)

                    @block.vector
                    def _(dve):
                        def chunk(c):
                            for e in range(NE):
                                n = c * NE + e
                                dve.wait_ge(relued.sem, relued.at(n + 1))
                                if after_first(n - 1 if e else n):
                                    dve.wait_ge(summed.sem, summed.at(n - 1 if e else n))
                                rr = r[:, e % 2, :, :]
                                if e < E8:
                                    if after_first(n):
                                        dve.wait_ge(weighted.sem, weighted.at(n))
                                    dve.tensor_tensor(rc[:, :, :], rr, bc(ps[:CP, 6 + e % 2:7 + e % 2, :CH], [CP, KC, CH]),
                                                      ALU.mult).then_inc(shared_out.sem, 1)
                                    dve.wait_ge(shared_out.sem, shared_out.at(c * E8 + e + 1))
                                    dve.tensor_tensor(hid[:, e % 2, :, :], rc[:, :, :], rr, ALU.mult).then_inc(weighted.sem, 1)
                                else:
                                    dve.tensor_tensor(hid[:, e % 2, :, :], rr, rr, ALU.mult).then_inc(weighted.sem, 1)
                            dve.wait_ge(summed.sem, summed.at((c + 1) * NE))
                            hc = h[:, :, bass.ds(c * CH, CH)]
                            dve.tensor_tensor(hc, hc, ps[:CP, 4:6, :CH], ALU.add).then_inc(added.sem, 1)
                        chunk(0)
                        with dve.Fori(1, NCH) as c:
                            chunk(c)
                for s in (hidden, relued, weighted, summed):
                    s.raised(NE * NCH)
                shared_out.raised(E8 * NCH)
                added.raised(NCH)

        def gelu_mlp(group, x, chunks, width, variants, bias1, bias2, res, dst, hs):
            hidden, gelued, summed, added, partly = (S("mlp_hidden"), S("mlp_gelued"), S("mlp_summed"), S("mlp_added"),
                                                     S("mlp_partly"))
            n_v = len(variants)
            units = 6 * n_v
            col0, count = chunks
            rows_of = [[(k, min(CP, rows - k * CP)) for k in range(KC) if rows > k * CP] for _, rows, _, _ in variants]
            with nc.Block() as block:
                @block.tensor
                def _(pe):
                    pe.wait_ge(loaded(group).sem, loaded(group).total)

                    def chunk(c):
                        cols = bass.ds(c * width + col0, width)
                        for u in range(units):
                            v, m = divmod(u, 6)
                            w1 = variants[v][0]
                            if after_first(c * units + u - 3):
                                pe.wait_ge(gelued.sem, gelued.at(c * units + u - 3))
                            for k, kr in rows_of[v]:
                                last = pe.matmul(ps[:, u % 4 if units % 4 == 0 else RING[u % 12], :width],
                                                 w1[:kr, k, m * 128:(m + 1) * 128], x[:kr, k, cols],
                                                 start=k == 0, stop=k == rows_of[v][-1][0])
                            last.then_inc(hidden.sem, 1)
                        pe.wait_ge(gelued.sem, gelued.at((c + 1) * units))
                        if after_first(c):
                            pe.wait_ge(added.sem, added.at(c))
                        for mo in range(KC):
                            todo = [(v, m) for v in range(n_v) for m in range(6) if variants[v][3] > mo * CP]
                            for i, (v, m) in enumerate(todo):
                                w2, outs = variants[v][2], min(CP, variants[v][3] - mo * CP)
                                last = pe.matmul(ps[:outs, 4 + mo, :width], w2[:, m, mo * CP:mo * CP + outs],
                                                 hs[:, 6 * v + m, :width], start=i == 0, stop=i == len(todo) - 1,
                                                 skip_group_check=n_v > 1)
                        last.then_inc(summed.sem, 1)
                    chunk(0)
                    with pe.Fori(1, count) as c:
                        chunk(c)

                @block.scalar
                def _(act):
                    def chunk(c):
                        if after_first(c):
                            act.wait_ge(summed.sem, summed.at(c))
                        for u in range(units):
                            act.wait_ge(hidden.sem, hidden.at(c * units + u + 1))
                            act.activation(hs[:, u, :width], ps[:, u % 4 if units % 4 == 0 else RING[u % 12], :width],
                                           ACT.Gelu, bias=bias1[:, u % 6:u % 6 + 1]).then_inc(gelued.sem, 1)
                    chunk(0)
                    with act.Fori(1, count) as c:
                        chunk(c)

                @block.vector
                def _(dve):
                    def chunk(c):
                        dve.wait_ge(summed.sem, summed.at(c + 1))
                        cols = bass.ds(c * width + col0, width)
                        for m in range(KC):
                            last = dve.scalar_tensor_tensor(dst[:, m, cols], ps[:CP, 4 + m, :width], bias2[:, m:m + 1],
                                                            res[0][:, m, cols], ALU.add, ALU.add)
                        if len(res) == 2:
                            last.then_inc(partly.sem, 1)
                            dve.wait_ge(partly.sem, partly.at(c + 1))
                            last = dve.tensor_tensor(dst[:, :, cols], dst[:, :, cols], res[1][:, :, cols], ALU.add)
                        last.then_inc(added.sem, 1)
                    chunk(0)
                    with dve.Fori(1, count) as c:
                        chunk(c)
            hidden.raised(units * count)
            gelued.raised(units * count)
            summed.raised(count)
            added.raised(count)
            if len(res) == 2:
                partly.raised(count)

        RING = [0, 1, 2, 3] * 3

        def l1_attention():
            with ExitStack() as st:
                wq = sb(st, "w1q", [CP, KC, H * 32])
                wk = sb(st, "w1k", [CP, KC, H * 32])
                wv = sb(st, "w1v", [CP, KC, C])
                wo = sb(st, "w1o", [CP, KC, C])
                bo = sb(st, "b1o", [CP, KC])
                o_t = sb(st, "o1_t", [CP, KC, TP])
                loads = (("attn1", ((wq[:, :, :], a["a1_wq"]), (wk[:, :, :], a["a1_wk"]),
                    (wv[:, :, :], a["a1_wv"]), (wo[:, :, :], a["a1_wo"]),
                    (bo[:, :], a["a1_bo"]))),)
                layer_norm(h, xn, "ln2", loads=loads)
                attention("at1", "attn1", xn, wq, wk, wv, masks[:, 1, :], o_t)
                project("attn1", o_t, lambda c: wo, lambda c: bo, h, h)

        def l1_ffn():
            with ExitStack() as st:
                w1 = sb(st, "f1_w1", [CP, KC, 768])
                b1 = sb(st, "f1_b1", [128, 6])
                w2 = sb(st, "f1_w2", [128, 6, C])
                zero = sb(st, "f1_zero", [CP, KC])
                hs = sb(st, "f1_hs", [128, 6, CH])
                def beside(pool):
                    pool.memset(zero[:, :], 0.0)
                loads = (("ffn1", ((w1[:, :, :], a["f1_w1"]), (b1[:, :], a["f1_b1"]), (w2[:, :, :], a["f1_w2"]))),)
                layer_norm(h, xn, "ln3", loads=loads, also_pool=beside)
                gelu_mlp("ffn1", xn, (0, NCH), CH, [(w1, C, w2, C)], b1, zero, [h], h, hs)

        def l2_attention():
            with ExitStack() as st:
                wq, wk, wqs, wks = (sb(st, n, [CP, KC, H * 32]) for n in ("w2q", "w2k", "w2qs", "w2ks"))
                wv = sb(st, "w2v", [CP, KC, C])
                wo = sb(st, "w2o", [CP, KC, C])
                bo = sb(st, "b2o", [CP, KC])
                bqk = sb(st, "b2qk", [128, 4, 3])
                bv = sb(st, "b2v", [1, C])
                tables = sb(st, "rope", [128, 4, TW])
                o_t = sb(st, "o2_t", [CP, KC, TP])
                loads = (("attn2", ((wq[:, :, :], a["a2_wq"]), (wk[:, :, :], a["a2_wk"]),
                    (wqs[:, :, :], a["a2_wqs"]), (wks[:, :, :], a["a2_wks"]),
                    (wv[:, :, :], a["a2_wv"]), (wo[:, :, :], a["a2_wo"]),
                    (bo[:, :], a["a2_bo"]), (bqk[:, :, :], a["a2_bqk"]),
                    (bv[:, :], a["a2_bv"]), (tables[:, :, :], a["rope"]))),)
                layer_norm(h, xn, "ln4", loads=loads)
                attention("at2", "attn2", xn, wq, wk, wv, masks[:, 2, :], o_t,
                          rope=(wqs, wks, bqk, tables, bv[:, :]))
                project("attn2", o_t, lambda c: wo, lambda c: bo, h, h)

        def l2_ffn():
            keep = [C // 1, C // 2, C // 3]
            with ExitStack() as st:
                wq = sb(st, "w3q", [CP, KC, H * 32])
                wk = sb(st, "w3k", [CP, KC, H * 32])
                wv = sb(st, "w3v", [CP, KC, C])
                wo = sb(st, "w3o", [CP, KC, C])
                wos = sb(st, "w3os", [CP, KC, C])
                bo = sb(st, "b3o", [CP, KC])
                bos = sb(st, "b3os", [CP, KC])
                gw = sb(st, "gumbel", [128, 3])
                gb = sb(st, "n12_gb", [CP, 4, 2, KC])
                w1 = sb(st, "f2_w1", [CP, KC, 768])
                b1 = sb(st, "f2_b1", [128, 6])
                w2 = sb(st, "f2_w2", [128, 6, C])
                w2s = [sb(st, f"f2_w2s{i}", [128, 6, keep[i]]) for i in range(3)]
                b2 = sb(st, "f2_b2", [CP, KC])
                b2s = sb(st, "f2_b2s", [CP, KC])
                x2 = sb(st, "x2", [CP, KC, T])
                n1 = sb(st, "n1", [CP, KC, TP])
                started, blended = S("blend_started"), S("blend_stepped")
                def beside(dve):
                    dve.wait_ge(loaded("block2").sem, loaded("block2").total)
                    dve.memset(n1[:, :, T:], 0.0)
                    dve.tensor_scalar(wos[:, :, :], wo[:, :, :], gw[:CP, 0:1], None, ALU.mult)
                    dve.tensor_scalar(bos[:, :], bo[:, :], gw[:CP, 0:1], None, ALU.mult)
                    dve.tensor_scalar(b2s[:, :], b2[:, :], gw[:CP, 0:1], None, ALU.mult)
                    for i in range(3):
                        last = dve.tensor_scalar(w2s[i][:, :, :], w2[:, :, :keep[i]], gw[:, i:i + 1], None, ALU.mult)
                    last.then_inc(blended.sem, 1)
                    for i in (1, 2):
                        if after_first(i):
                            dve.wait_ge(blended.sem, blended.at(i))
                        k = keep[i]
                        for dst, src in ((wos[:k, 0, :k], wo[:k, 0, :k]), (bos[:k, 0:1], bo[:k, 0:1]),
                                         (b2s[:k, 0:1], b2[:k, 0:1])):
                            last = dve.scalar_tensor_tensor(dst, src, gw[:k, i:i + 1], dst, ALU.mult, ALU.add)
                        last.then_inc(blended.sem, 1)
                loads = (("block2", ((wq[:, :, :], a["a3_wq"]), (wk[:, :, :], a["a3_wk"]),
                    (wv[:, :, :], a["a3_wv"]), (wo[:, :, :], a["a3_wo"]),
                    (bo[:, :], a["a3_bo"]), (gw[:, :], a["gumbel"]), (gb[:, :, :, :], a["n12_gb"]),
                    (w1[:, :, :], a["f2_w1"]), (b1[:, :], a["f2_b1"]),
                    (w2[:, :, :], a["f2_w2"]), (b2[:, :], a["f2_b2"]))),)
                layer_norm(h, xn, "ln5", loads=loads, also_dve=beside)
                blended.raised(3)
                layer_norm(xn, n1, "ln6", affine=(gb[:, 0, :, :], gb[:, 1, :, :]))
                with ExitStack() as st2:
                    o_t = sb(st2, "o3_t", [CP, KC, TP])
                    attention("at3", "block2", n1, wq, wk, wv, masks[:, 3, :], o_t)
                    project("block2", o_t, lambda c: wo if c < 2 else wos, lambda c: bo if c < 2 else bos, x2, xn, width=Q4)
                layer_norm(x2, n1, "ln7", affine=(gb[:, 2, :, :], gb[:, 3, :, :]))
                with ExitStack() as st2:
                    hs = sb(st2, "f2_hs", [128, 18, Q4])
                    gelu_mlp("block2", n1, (0, 2), Q4, [(w1, C, w2, C)], b1, b2, [h, x2], h, hs)
                    gelu_mlp("block2", n1, (HALF, 2), Q4,
                             [(w1, keep[0], w2s[0], keep[0]), (w1, keep[2], w2s[2], keep[2]),
                              (w1, keep[1], w2s[1], keep[1])], b1, b2s, [h, x2], h, hs)

        def l3_ffn():
            R = 64
            with ExitStack() as st:
                we = sb(st, "e_w", [CP, KC, R])
                be = sb(st, "e_b", [R, 1])
                ws = sb(st, "sw_w", [R, E8])
                bs = sb(st, "sw_b", [1, E8])
                w1 = sb(st, "f3_w1", [CP, KC, E8 * R])
                b1 = sb(st, "f3_b1", [128, 4])
                w2 = sb(st, "f3_w2", [128, 4, C])
                b2 = sb(st, "f3_b2", [E8, C])
                pick = sb(st, "f3_pick", [E8, E8, R])
                enc = sb(st, "enc", [R, T])
                comb_t = sb(st, "f3_comb_t", [E8, T])
                g = sb(st, "f3_g", [128, 4, CH])
                hid = sb(st, "f3_hid", [128, 4, CH])
                encoded = S("encoded")
                def beside(dve):
                    dve.tensor_copy(pick[:, :, :], bc(ident[:E8, :E8].unsqueeze(2), [E8, E8, R]))
                loads = (("ffn3", ((we[:, :, :], a["e_w"]), (be[:, :], a["e_b"]), (ws[:, :], a["sw_w"]),
                    (bs[:, :], a["sw_b"]), (w1[:, :, :], a["f3_w1"]), (b1[:, :], a["f3_b1"]),
                    (w2[:, :, :], a["f3_w2"]), (b2[:, :], a["f3_b2"]))),)
                layer_norm(h, xn, "ln9", loads=loads, also_dve=beside)
                with nc.Block() as block:
                    @block.tensor
                    def _(pe):
                        pe.wait_ge(loaded("ffn3").sem, loaded("ffn3").total)
                        for c in range(NCH):
                            for k in range(KC):
                                last = pe.matmul(ps[:R, c, :CH], we[:, k, :], xn[:, k, c * CH:(c + 1) * CH],
                                                 start=k == 0, stop=k == KC - 1)
                        last.then_inc(encoded.sem, 1)

                    @block.scalar
                    def _(act):
                        act.wait_ge(encoded.sem, encoded.at(1))
                        act.activation(enc[:, :].rearrange("p (c t) -> p c t", c=NCH), ps[:R, 0:NCH, :CH], ACT.Identity,
                                       bias=be[:, 0:1])
                encoded.raised(1)

                def logits(pe, made):
                    for i in range(T // 128):
                        pe.matmul(ps[:, 0, 8 * i:8 * i + 8], enc[:, 128 * i:128 * i + 128], ws[:, :], start=True, stop=False)
                        last = pe.matmul(ps[:, 0, 8 * i:8 * i + 8], ones_row[:, :], bs[:, :], start=False, stop=True)
                    last.then_inc(made.sem, 1)
                route("r3", "ffn3", 1, logits, None, comb_t)

                hidden, gelued, weighted, summed, added = (S("f3_hidden"), S("f3_gelued"), S("f3_weighted"),
                                                           S("f3_summed"), S("f3_added"))
                picks = pick[:, :, :].rearrange("p (c e) r -> p c (e r)", e=2)
                with nc.Block() as block:
                    @block.tensor
                    def _(pe):
                        def chunk(c):
                            cols = bass.ds(c * CH, CH)
                            for m in range(4):
                                if after_first(4 * c + m - 1):
                                    pe.wait_ge(weighted.sem, weighted.at(4 * c + m - 1))
                                for k in range(KC):
                                    pe.matmul(ps[:, m % 2, :CH], w1[:, k, m * 128:(m + 1) * 128], xn[:, k, cols],
                                              start=k == 0, stop=k == KC - 1)
                                pe.matmul(ps[:, 2 + m % 2, :CH], picks[:, m, :], comb_t[:, cols],
                                          start=True, stop=True).then_inc(hidden.sem, 1)
                            pe.wait_ge(weighted.sem, weighted.at(4 * c + 4))
                            if after_first(c):
                                pe.wait_ge(added.sem, added.at(c))
                            for mo in range(KC):
                                for m in range(4):
                                    pe.matmul(ps[:CP, 4 + mo, :CH], w2[:, m, mo * CP:(mo + 1) * CP], hid[:, m, :],
                                              start=m == 0, stop=False)
                                last = pe.matmul(ps[:CP, 4 + mo, :CH], b2[:, mo * CP:(mo + 1) * CP], comb_t[:, cols],
                                                 start=False, stop=True)
                            last.then_inc(summed.sem, 1)
                        chunk(0)
                        with pe.Fori(1, NCH) as c:
                            chunk(c)

                    @block.scalar
                    def _(act):
                        def chunk(c):
                            for m in range(4):
                                act.wait_ge(hidden.sem, hidden.at(4 * c + m + 1))
                                if m == 0:
                                    if after_first(4 * c):
                                        act.wait_ge(weighted.sem, weighted.at(4 * c))
                                act.activation(g[:, m, :], ps[:, m % 2, :CH], ACT.Gelu,
                                               bias=b1[:, m:m + 1]).then_inc(gelued.sem, 1)
                        chunk(0)
                        with act.Fori(1, NCH) as c:
                            chunk(c)

                    @block.vector
                    def _(dve):
                        def chunk(c):
                            if after_first(c):
                                dve.wait_ge(summed.sem, summed.at(c))
                            for m in range(4):
                                dve.wait_ge(gelued.sem, gelued.at(4 * c + m + 1))
                                dve.tensor_tensor(hid[:, m, :], g[:, m, :], ps[:, 2 + m % 2, :CH],
                                                  ALU.mult).then_inc(weighted.sem, 1)
                            dve.wait_ge(summed.sem, summed.at(c + 1))
                            hc = h[:, :, bass.ds(c * CH, CH)]
                            dve.tensor_tensor(hc, hc, ps[:CP, 4:6, :CH], ALU.add).then_inc(added.sem, 1)
                        chunk(0)
                        with dve.Fori(1, NCH) as c:
                            chunk(c)

        def l3_mamba():
            G = 8
            NG = ST // G
            U = JC * NG
            SP = 2 * ST
            SPREAD_DVE = (29, 30, 31)
            DRIVE_DVE, READ_DVE = (0,), (0, 1, 5)
            HR = 4
            DRING = 2
            QUARTERS = 4 * LAYERS
            x = xn
            layer_norm(h, xn, "ln8")
            with ExitStack() as st:
                w_in = sb(st, "m_w_in", [CP, KC, 2 * DI])
                w_norm = sb(st, "m_w_norm", [CP, LAYERS, KC])
                w_mid = sb(st, "m_w_mid", [128, JC, 150])
                w_dt = sb(st, "m_w_dt", [DR, DI])
                w_next = sb(st, "m_w_next", [128, JC, ST + 1 + C])
                w_now = sb(st, "m_w_now", [128, JC, 1 + C])
                a_pos = sb(st, "m_a_pos", [128, JC, ST])
                spread_sel = sb(st, "m_spread_sel", [96, 2 * ST], BF16)
                rs = sb(st, "m_rs", [CP, Q4])
                hn = sb(st, "m_hn", [CP, KC, Q4])
                cv = sb(st, "m_cv", [128, JC, Q4])
                eu = sb(st, "m_eu", [128, JC, Q4])
                sq = eu
                w1p = sb(st, "m_w1p", [128, JC, Q4])
                u = sb(st, "m_u_t", [128, 2, JC, Q4])
                ndt = sb(st, "m_ndt", [128, 2, JC, Q4])
                dtu = sb(st, "m_dtu", [128, 2, JC, Q4])
                zs = sb(st, "m_zs", [128, 2, JC, Q4])
                bch = sb(st, "m_bch", [96, Q4], BF16)
                bcm = sb(st, "m_bcm", [96, Q4], BF16)
                bcr = sb(st, "m_bcr", [96, Q4])
                dtr = sb(st, "m_dtr_t", [DR, Q4])
                bcs = sb(st, "m_bcs", [128, 2, 2 * ST, Q4])
                decay = sb(st, "m_decay_t", [128, DRING, G, Q4])
                hid = sb(st, "m_hid", [128, HR, G, Q4])

                w_in_got, w_mid_got, w_norm_got = S("m_w_in_got"), S("m_w_mid_got"), S("m_w_norm_got")
                w_scan, w_set, a_set = S("m_w_scan"), S("m_w_set"), S("m_a_set")
                cleared = S("m_cleared")
                squared, ms, rstd, normed = S("m_squared"), S("m_ms"), S("m_rstd"), S("m_normed")
                u_made, conv0, conv, u_ready = S("m_u_made"), S("m_conv0"), S("m_conv"), S("m_u_ready")
                z_made, z_ready = S("m_z_made"), S("m_z_ready")
                bc_made, bc_hi, bc_rest, bc_mid, bc_lo = (S("m_bc_made"), S("m_bc_hi"), S("m_bc_rest"), S("m_bc_mid"),
                                                          S("m_bc_lo"))
                dtr_made, dtr_copied, dt_made, sp_act, sp_dve = (S("m_dtr_made"), S("m_dtr_copied"), S("m_dt_made"),
                                                                 S("m_softplus_act"), S("m_softplus_dve"))
                spread, copied_act, copied_dve = S("m_spread"), S("m_copied_act"), S("m_copied_dve")
                decayed, driven_pool, scanned, read_pool, read_dve, y_summed = (
                    S("m_decayed"), S("m_driven_pool"), S("m_scanned"), S("m_read_pool"), S("m_read_dve"), S("m_y_summed"))
                driven_dve, gated, out_made, added = S("m_driven_dve"), S("m_gated"), S("m_out_made"), S("m_added")
                NRP, NRD = U - len(READ_DVE), len(READ_DVE)
                NCA, NCD = SP - len(SPREAD_DVE), len(SPREAD_DVE)
                NDP, NDD = U - len(DRIVE_DVE), len(DRIVE_DVE)

                def nth(s, on_dve):
                    return len([r for r in range(s + 1) if (r in on_dve) == (s in on_dve)])

                def cols(q):
                    return slice(q * Q4, (q + 1) * Q4)

                def images(ap):
                    return ap.rearrange("p (b t) -> p b t", t=N)

                def norms_before(P):
                    return min(P + 2, QUARTERS) if isinstance(P, int) else P + 2

                class Norm:
                    @staticmethod
                    def square(act, R, q):
                        if after_first(R - 3):
                            act.wait_ge(added.sem, added.at(R - 3))
                        if after_first(4 * (R - 1)):
                            act.wait_ge(sp_dve.sem, sp_dve.at(4 * (R - 1)))
                        if after_first(R):
                            act.wait_ge(ms.sem, ms.at(R))
                        act.activation(sq[:CP, 0:KC, :], x[:, :, cols(q)], ACT.Square).then_inc(squared.sem, 1)

                    @staticmethod
                    def mean(pe, R):
                        pe.wait_ge(squared.sem, squared.at(R + 1))
                        if after_first(R):
                            pe.wait_ge(z_ready.sem, z_ready.at(R))
                        for k in range(KC):
                            last = pe.matmul(ps[:CP, 5, :Q4], ones_mean[:CP, :CP], sq[:CP, k, :], start=k == 0, stop=k == KC - 1)
                        last.then_inc(ms.sem, 1)

                    @staticmethod
                    def rsqrt(act, R):
                        act.wait_ge(ms.sem, ms.at(R + 1))
                        if after_first(R):
                            act.wait_ge(normed.sem, normed.at(R))
                        act.activation(rs[:, :], ps[:CP, 5, :Q4], ACT.Ln, bias=eps[:CP, 0:1]).then_inc(rstd.sem, 1)
                        act.wait_ge(rstd.sem, rstd.at(2 * R + 1))
                        act.activation(rs[:, :], rs[:, :], ACT.Exp, scale=-0.5).then_inc(rstd.sem, 1)

                    @staticmethod
                    def scale(dve, R, q, l):
                        if after_first(R):
                            dve.wait_ge(z_made.sem, z_made.at(R))
                        dve.wait_ge(rstd.sem, rstd.at(2 * R + 2))
                        for k in range(KC):
                            w = w_norm[:, l, k:k + 1] if isinstance(l, int) else w_norm[:, bass.ds(l, 1), k]
                            last = dve.scalar_tensor_tensor(hn[:, k, :], x[:, k, cols(q)], w, rs[:, :], ALU.mult, ALU.mult)
                        last.then_inc(normed.sem, 1)

                class Prepare:
                    @staticmethod
                    def u_proj(pe, P, l):
                        pe.wait_ge(w_in_got.sem, w_in_got.at(16 * (l + 1)))
                        pe.wait_ge(normed.sem, normed.at(P + 1))
                        if after_first(5 * P - 4):
                            pe.wait_ge(sp_act.sem, sp_act.at(5 * P - 4))
                        for j in range(JC):
                            for k in range(KC):
                                last = pe.matmul(ps[:, j, :Q4], w_in[:, k, j * 128:(j + 1) * 128], hn[:, k, :],
                                                 start=k == 0, stop=k == KC - 1)
                        last.then_inc(u_made.sem, 1)

                    @staticmethod
                    def z_proj(pe, P):
                        if after_first(P):
                            pe.wait_ge(copied_act.sem, copied_act.at(NCA * P))
                            pe.wait_ge(copied_dve.sem, copied_dve.at(NCD * P))
                        pe.wait_ge(rstd.sem, rstd.at(2 * P + 1))
                        for j in range(JC):
                            for k in range(KC):
                                last = pe.matmul(ps[:, 3 + j, :Q4], w_in[:, k, DI + j * 128:DI + (j + 1) * 128],
                                                 hn[:, k, :], start=k == 0, stop=k == KC - 1)
                        last.then_inc(z_made.sem, 1)

                    @staticmethod
                    def taps(dve, P, l):
                        dve.wait_ge(w_mid_got.sem, w_mid_got.at(32 * (l + 1)))
                        if after_first(4 * P):
                            dve.wait_ge(sp_dve.sem, sp_dve.at(4 * P))
                        dve.wait_ge(u_made.sem, u_made.at(P + 1))
                        for j in range(JC):
                            last = dve.tensor_scalar(cv[:, j, :], ps[:, j, :Q4], w_mid[:, j, 147:148],
                                                     w_mid[:, j, 148:149], ALU.mult, ALU.add)
                        last.then_inc(conv0.sem, 1)
                        dve.wait_ge(conv0.sem, conv0.at(P + 1))
                        for s in range(1, 4):
                            if s > 1:
                                dve.wait_ge(conv.sem, conv.at(3 * P + s - 1))
                            for j in range(JC):
                                o = images(cv[:, j, :])[:, :, s:]
                                last = dve.scalar_tensor_tensor(o, images(ps[:, j, :Q4])[:, :, :N - s],
                                                                w_mid[:, j, 147 - s:148 - s], o, ALU.mult, ALU.add)
                            last.then_inc(conv.sem, 1)

                    @staticmethod
                    def silus(act, P, q):
                        act.wait_ge(conv.sem, conv.at(3 * P + 3))
                        if after_first(2 * JC * (P - 1)):
                            act.wait_ge(gated.sem, gated.at(2 * JC * (P - 1)))
                        act.activation(u[:, q % 2, :, :], cv[:, :, :], ACT.Silu).then_inc(u_ready.sem, 1)
                        act.wait_ge(z_made.sem, z_made.at(P + 1))
                        if after_first(P - 1):
                            act.wait_ge(out_made.sem, out_made.at(P - 1))
                        act.activation(zs[:, q % 2, :, :], ps[:, 3:6, :Q4], ACT.Silu).then_inc(z_ready.sem, 1)

                    @staticmethod
                    def bc_proj(pe, P, q):
                        pe.wait_ge(u_ready.sem, u_ready.at(P + 1))
                        pe.wait_ge(z_ready.sem, z_ready.at(P + 1))
                        for j in range(JC):
                            last = pe.matmul(ps[:DR, 4, :Q4], w_mid[:, j, 96:96 + DR], u[:, q % 2, j, :],
                                             start=j == 0, stop=j == JC - 1)
                        last.then_inc(dtr_made.sem, 1)
                        for j in range(JC):
                            last = pe.matmul(ps[:96, 3, :Q4], w_mid[:, j, 0:96], u[:, q % 2, j, :], start=j == 0, stop=j == JC - 1)
                        last.then_inc(bc_made.sem, 1)

                    @staticmethod
                    def copy_dtr(act, P):
                        act.wait_ge(dtr_made.sem, dtr_made.at(P + 1))
                        if after_first(P):
                            act.wait_ge(dt_made.sem, dt_made.at(P))
                        act.activation(dtr[:, :], ps[:DR, 4, :Q4], ACT.Copy).then_inc(dtr_copied.sem, 1)

                    @staticmethod
                    def split(dve, P):
                        dve.wait_ge(bc_made.sem, bc_made.at(P + 1))
                        if after_first(SP * P):
                            dve.wait_ge(spread.sem, spread.at(SP * P))
                        dve.tensor_copy(bch[:, :], ps[:96, 3, :Q4]).then_inc(bc_hi.sem, 1)
                        dve.wait_ge(bc_hi.sem, bc_hi.at(P + 1))
                        if after_first(P):
                            dve.wait_ge(bc_lo.sem, bc_lo.at(P))
                        dve.tensor_tensor(bcr[:, :], ps[:96, 3, :Q4], bch[:, :], ALU.subtract).then_inc(bc_rest.sem, 1)
                        dve.wait_ge(bc_rest.sem, bc_rest.at(P + 1))
                        dve.tensor_copy(bcm[:, :], bcr[:, :]).then_inc(bc_mid.sem, 1)
                        dve.wait_ge(bc_mid.sem, bc_mid.at(2 * P + 1))
                        dve.tensor_copy(bch[32:64, :], bcm[32:64, :]).then_inc(bc_mid.sem, 1)
                        dve.wait_ge(bc_mid.sem, bc_mid.at(2 * P + 2))
                        dve.tensor_tensor(bch[64:96, :], bcr[64:96, :], bcm[64:96, :], ALU.subtract).then_inc(bc_lo.sem, 1)

                    @staticmethod
                    def dt_proj(pe, P):
                        pe.wait_ge(dtr_copied.sem, dtr_copied.at(P + 1))
                        pe.wait_ge(conv.sem, conv.at(3 * P + 3))
                        if after_first(P - 1):
                            pe.wait_ge(added.sem, added.at(P - 1))
                        for j in range(JC):
                            last = pe.matmul(ps[:, j, :Q4], w_dt[:, j * 128:(j + 1) * 128], dtr[:, :], start=True, stop=True)
                        last.then_inc(dt_made.sem, 1)

                    @staticmethod
                    def softplus_act(act, P):
                        act.wait_ge(dt_made.sem, dt_made.at(P + 1))
                        act.wait_ge(u_ready.sem, u_ready.at(P + 1))
                        for j in range(JC):
                            last = act.activation(cv[:, j, :], ps[:, j, :Q4], ACT.Identity, bias=w_mid[:, j, 149:150])
                        last.then_inc(sp_act.sem, 1)
                        act.wait_ge(sp_act.sem, sp_act.at(5 * P + 1))
                        act.wait_ge(ms.sem, ms.at(norms_before(P)))
                        act.activation(eu[:, :, :], cv[:, :, :], ACT.Abs).then_inc(sp_act.sem, 1)
                        act.wait_ge(sp_act.sem, sp_act.at(5 * P + 2))
                        act.activation(eu[:, :, :], eu[:, :, :], ACT.Exp, scale=-1.0).then_inc(sp_act.sem, 1)
                        act.wait_ge(sp_act.sem, sp_act.at(5 * P + 3))
                        act.activation(w1p[:, :, :], eu[:, :, :], ACT.Identity, bias=1.0).then_inc(sp_act.sem, 1)
                        act.wait_ge(sp_dve.sem, sp_dve.at(4 * P + 1))
                        act.activation(w1p[:, :, :], w1p[:, :, :], ACT.Ln).then_inc(sp_act.sem, 1)

                    @staticmethod
                    def softplus_dve(dve, P, q):
                        dve.wait_ge(sp_act.sem, sp_act.at(5 * P + 4))
                        dve.scalar_tensor_tensor(eu[:, :, :], w1p[:, :, :], 1.0, eu[:, :, :], ALU.subtract,
                                                 ALU.subtract).then_inc(sp_dve.sem, 1)
                        dve.wait_ge(sp_act.sem, sp_act.at(5 * P + 5))
                        dve.scalar_tensor_tensor(cv[:, :, :], cv[:, :, :], 0.0, w1p[:, :, :], ALU.max,
                                                 ALU.add).then_inc(sp_dve.sem, 1)
                        dve.wait_ge(sp_dve.sem, sp_dve.at(4 * P + 2))
                        if after_first(U * (P - 1)):
                            dve.wait_ge(decayed.sem, decayed.at(U * (P - 1)))
                        dve.tensor_tensor(ndt[:, q % 2, :, :], eu[:, :, :], cv[:, :, :], ALU.subtract).then_inc(sp_dve.sem, 1)
                        dve.wait_ge(sp_dve.sem, sp_dve.at(4 * P + 3))
                        if after_first(P - 1):
                            dve.wait_ge(driven_pool.sem, driven_pool.at(NDP * (P - 1)))
                            dve.wait_ge(driven_dve.sem, driven_dve.at(NDD * (P - 1)))
                        dve.scalar_tensor_tensor(dtu[:, q % 2, :, :], ndt[:, q % 2, :, :], -1.0, u[:, q % 2, :, :],
                                                 ALU.mult, ALU.mult).then_inc(sp_dve.sem, 1)

                    @staticmethod
                    def spread_pe(pe, P, first, end):
                        for i in range(first, end):
                            if i == 0:
                                pe.wait_ge(bc_lo.sem, bc_lo.at(P + 1))
                            elif i == 1:
                                pe.wait_ge(dtr_copied.sem, dtr_copied.at(P + 1))
                            elif i == 2:
                                pe.wait_ge(rstd.sem, rstd.at(2 * norms_before(P) - 1))
                            elif i - 3 in SPREAD_DVE:
                                pe.wait_ge(copied_dve.sem, copied_dve.at(NCD * P + nth(i - 3, SPREAD_DVE)))
                            else:
                                pe.wait_ge(copied_act.sem, copied_act.at(NCA * P + nth(i - 3, SPREAD_DVE)))
                            pe.matmul(ps[:, 3 + i % 3, :Q4], bc(spread_sel[:, i:i + 1], [96, 128]), bch[:, :],
                                      start=True, stop=True).then_inc(spread.sem, 1)

                    @staticmethod
                    def copy_spread(copy, eng, P, q, i, done):
                        if i in (0, SPREAD_DVE[0]) and after_first(P - 1):
                            eng.wait_ge(driven_pool.sem, driven_pool.at(NDP * (P - 1)))
                            eng.wait_ge(driven_dve.sem, driven_dve.at(NDD * (P - 1)))
                            eng.wait_ge(read_pool.sem, read_pool.at(NRP * (P - 1)))
                            eng.wait_ge(read_dve.sem, read_dve.at(NRD * (P - 1)))
                        eng.wait_ge(spread.sem, spread.at(SP * P + i + 1))
                        copy(bcs[:, q % 2, i, :], ps[:, 3 + i % 3, :Q4]).then_inc(done.sem, 1)

                    @staticmethod
                    def spread_act(act, P, q, first, last_pair):
                        for i in range(first, last_pair):
                            if i not in SPREAD_DVE:
                                Prepare.copy_spread(act.copy, act, P, q, i, copied_act)

                    @staticmethod
                    def spread_dve(dve, P, q):
                        for i in SPREAD_DVE:
                            Prepare.copy_spread(dve.tensor_copy, dve, P, q, i, copied_dve)

                def set_a(act, l, Q):
                    act.wait_ge(w_scan.sem, w_scan.at(16 * (l + 1)))
                    if after_first(U * Q):
                        act.wait_ge(decayed.sem, decayed.at(U * Q))
                    act.activation(a_pos[:, :, :], w_next[:, :, :ST], ACT.Exp).then_inc(a_set.sem, 1)

                def decays(act, Q, q, s, l):
                    j, g = divmod(s, NG)
                    if s == 0:
                        act.wait_ge(sp_dve.sem, sp_dve.at(4 * Q + 3))
                        act.wait_ge(a_set.sem, a_set.at(l + 1))
                    if after_first(U * Q + s + 1 - DRING):
                        act.wait_ge(scanned.sem, scanned.at(U * Q + s + 1 - DRING))
                    for n in range(G):
                        last = act.activation(images(decay[:, s % DRING, n, :])[:, :, 1:], images(ndt[:, q % 2, j, :])[:, :, 1:],
                                              ACT.Exp, scale=a_pos[:, j, g * G + n:g * G + n + 1])
                    last.then_inc(decayed.sem, 1)

                def drive(eng, Q, q, s, done):
                    j, g = divmod(s, NG)
                    eng.wait_ge(sp_dve.sem, sp_dve.at(4 * Q + 4))
                    eng.wait_ge(copied_act.sem, copied_act.at(NCA * Q + (g + 1) * G))
                    if after_first(U * Q + s + 1 - HR):
                        eng.wait_ge(y_summed.sem, y_summed.at(U * Q + s + 1 - HR))
                    eng.tensor_tensor(hid[:, (U * q + s) % HR, :, :], bcs[:, q % 2, g * G:(g + 1) * G, :],
                                      bc(dtu[:, q % 2, j:j + 1, :], [128, G, Q4]), ALU.mult).then_inc(done.sem, 1)

                def scan(dve, Q, q, s):
                    dve.wait_ge(decayed.sem, decayed.at(U * Q + s + 1))
                    if s in DRIVE_DVE:
                        dve.wait_ge(driven_dve.sem, driven_dve.at(NDD * Q + nth(s, DRIVE_DVE)))
                    else:
                        dve.wait_ge(driven_pool.sem, driven_pool.at(NDP * Q + nth(s, DRIVE_DVE)))
                    d = decay[:, s % DRING, :, :].rearrange("p n t -> p (n t)")
                    v = hid[:, (U * q + s) % HR, :, :].rearrange("p n t -> p (n t)")
                    dve.tensor_tensor_scan(v, d, v, 0.0, ALU.mult, ALU.add).then_inc(scanned.sem, 1)

                def read(eng, Q, q, s, done):
                    g = s % NG
                    eng.wait_ge(scanned.sem, scanned.at(U * Q + s + 1))
                    eng.wait_ge(copied_act.sem, copied_act.at(NCA * (Q + 1)))
                    eng.wait_ge(copied_dve.sem, copied_dve.at(NCD * (Q + 1)))
                    v = hid[:, (U * q + s) % HR, :, :]
                    eng.tensor_tensor(v, v, bcs[:, q % 2, ST + g * G:ST + (g + 1) * G, :], ALU.mult).then_inc(done.sem, 1)

                def sum_y(pe, Q, q, s):
                    j, g = divmod(s, NG)
                    if s in READ_DVE:
                        pe.wait_ge(read_dve.sem, read_dve.at(NRD * Q + nth(s, READ_DVE)))
                    else:
                        pe.wait_ge(read_pool.sem, read_pool.at(NRP * Q + nth(s, READ_DVE)))
                    if g == 0:
                        if after_first(2 * (JC * Q + j - 1)):
                            pe.wait_ge(gated.sem, gated.at(2 * (JC * Q + j - 1)))
                    for n in range(G):
                        last = pe.matmul(ps[:, 6 + (JC * q + j) % 2, :Q4], ident[:, :], hid[:, (U * q + s) % HR, n, :],
                                         start=g == 0 and n == 0, stop=g == NG - 1 and n == G - 1)
                    last.then_inc(y_summed.sem, 1)

                def gate(dve, Q, q, j, l):
                    Y = JC * Q + j
                    dve.wait_ge(w_set.sem, w_set.at(l + 1))
                    dve.wait_ge(y_summed.sem, y_summed.at(U * Q + NG * (j + 1)))
                    dve.scalar_tensor_tensor(u[:, q % 2, j, :], u[:, q % 2, j, :], w_now[:, j, 0:1],
                                             ps[:, 6 + (JC * q + j) % 2, :Q4], ALU.mult, ALU.add).then_inc(gated.sem, 1)
                    dve.wait_ge(gated.sem, gated.at(2 * Y + 1))
                    dve.wait_ge(z_ready.sem, z_ready.at(Q + 1))
                    dve.tensor_tensor(zs[:, q % 2, j, :], zs[:, q % 2, j, :], u[:, q % 2, j, :], ALU.mult).then_inc(gated.sem, 1)

                def out_proj(pe, Q, q, l, prepared):
                    pe.wait_ge(gated.sem, gated.at(2 * JC * (Q + 1)))
                    pe.wait_ge(w_set.sem, w_set.at(l + 1))
                    pe.wait_ge(conv.sem, conv.at(3 * prepared))
                    for m in range(KC):
                        for j in range(JC):
                            last = pe.matmul(ps[:CP, m, :Q4], w_now[:, j, 1 + m * CP:1 + (m + 1) * CP], zs[:, q % 2, j, :],
                                             start=j == 0, stop=j == JC - 1)
                    last.then_inc(out_made.sem, 1)

                def add_out(dve, Q, q):
                    dve.wait_ge(out_made.sem, out_made.at(Q + 1))
                    dve.tensor_tensor(x[:, :, cols(q)], x[:, :, cols(q)], ps[:CP, 0:2, :Q4], ALU.add).then_inc(added.sem, 1)

                def set_w(act, l, Q):
                    act.wait_ge(w_scan.sem, w_scan.at(16 * (l + 1)))
                    if after_first(Q):
                        act.wait_ge(out_made.sem, out_made.at(Q))
                    act.activation(w_now[:, :, :], w_next[:, :, ST:], ACT.Copy).then_inc(w_set.sem, 1)

                with nc.Block() as block:
                    @block.sync
                    def _(sp):
                        def prep_weights(l):
                            if after_first(l):
                                sp.wait_ge(z_made.sem, z_made.at(4 * l))
                            sp.wait_ge(w_scan.sem, w_scan.at(16))
                            one = bass.ds(l, 1)
                            sp.dma_start(w_in[:, :, :], a["m_w_in"][one].rearrange("l p k c -> (l p) k c")
                                         ).then_inc(w_in_got.sem, 16)
                            if after_first(l):
                                sp.wait_ge(sp_act.sem, sp_act.at(20 * l - 4))
                            sp.wait_ge(w_scan.sem, w_scan.at(16))
                            sp.dma_start(w_mid[:, :, :], a["m_w_mid"][one].rearrange("l p k c -> (l p) k c")
                                         ).then_inc(w_mid_got.sem, 16)
                            sp.dma_start(w_dt[:, :], a["m_w_dt"][one].rearrange("l p c -> (l p) c")
                                         ).then_inc(w_mid_got.sem, 16)

                        def scan_weights(l):
                            if after_first(l):
                                sp.wait_ge(a_set.sem, a_set.at(l))
                            if after_first(l):
                                sp.wait_ge(w_set.sem, w_set.at(l))
                            if not isinstance(l, int):
                                sp.wait_ge(w_scan.sem, w_scan.at(16))
                            sp.dma_start(w_next[:, :, :], a["m_w_scan"][bass.ds(l, 1)].rearrange("l p k c -> (l p) k c")
                                         ).then_inc(w_scan.sem, 16)
                        sp.dma_start(w_norm[:, :, :], a["m_w_norm"]).then_inc(w_norm_got.sem, 16)
                        scan_weights(0)
                        prep_weights(0)
                        with sp.Fori(1, LAYERS) as l:
                            scan_weights(l)
                            prep_weights(l)

                    @block.gpsimd
                    def _(pool):
                        def layer(l):
                            for q in range(4):
                                Q = 4 * l + q
                                drive(pool, Q, q, 1, driven_pool)
                                drive(pool, Q, q, 2, driven_pool)
                                drive(pool, Q, q, 3, driven_pool)
                                drive(pool, Q, q, 4, driven_pool)
                                read(pool, Q, q, 2, read_pool)
                                read(pool, Q, q, 3, read_pool)
                                read(pool, Q, q, 4, read_pool)
                                drive(pool, Q, q, 5, driven_pool)
                        layer(0)
                        with pool.Fori(1, LAYERS) as l:
                            layer(l)

                    @block.tensor
                    def _(pe):
                        def layer(l, last):
                            for q in range(4):
                                Q, P, p = 4 * l + q, 4 * l + q + 1, (q + 1) % 4
                                more = not (last and q == 3)
                                norm = not (last and q >= 2)
                                if more:
                                    Prepare.z_proj(pe, P)
                                if not (isinstance(Q, int) and Q == 0):
                                    out_proj(pe, Q - 1, (q - 1) % 4, l if q else l - 1, min(Q + 2, QUARTERS) if last else Q + 2)
                                sum_y(pe, Q, q, 0)
                                sum_y(pe, Q, q, 1)
                                if more:
                                    Prepare.bc_proj(pe, P, p)
                                    Prepare.dt_proj(pe, P)
                                if norm:
                                    Norm.mean(pe, Q + 2)
                                sum_y(pe, Q, q, 2)
                                sum_y(pe, Q, q, 3)
                                sum_y(pe, Q, q, 4)
                                if norm:
                                    Prepare.u_proj(pe, Q + 2, l + 1 if q >= 2 else l)
                                if more:
                                    Prepare.spread_pe(pe, P, 0, ST)
                                    Prepare.spread_pe(pe, P, ST, SP)
                                sum_y(pe, Q, q, 5)
                        pe.wait_ge(cleared.sem, cleared.at(1))
                        Norm.mean(pe, 0)
                        Prepare.u_proj(pe, 0, 0)
                        Prepare.z_proj(pe, 0)
                        Prepare.bc_proj(pe, 0, 0)
                        Norm.mean(pe, 1)
                        Prepare.dt_proj(pe, 0)
                        Prepare.spread_pe(pe, 0, 0, ST)
                        Prepare.u_proj(pe, 1, 0)
                        Prepare.spread_pe(pe, 0, ST, SP)
                        layer(0, False)
                        with pe.Fori(1, LAYERS - 1) as l:
                            layer(l, False)
                        layer(LAYERS - 1, True)
                        out_proj(pe, QUARTERS - 1, 3, LAYERS - 1, QUARTERS)

                    @block.scalar
                    def _(act):
                        def layer(l, last):
                            for q in range(4):
                                Q, P, p = 4 * l + q, 4 * l + q + 1, (q + 1) % 4
                                more = not (last and q == 3)
                                if q == 0:
                                    set_a(act, l, Q)
                                norm = not (last and q >= 2)
                                decays(act, Q, q, 0, l)
                                if q == 0:
                                    set_w(act, l, Q)
                                decays(act, Q, q, 1, l)
                                if norm:
                                    Norm.square(act, Q + 2, (q + 2) % 4)
                                decays(act, Q, q, 2, l)
                                if more:
                                    Prepare.silus(act, P, p)
                                decays(act, Q, q, 3, l)
                                decays(act, Q, q, 4, l)
                                if more:
                                    Prepare.copy_dtr(act, P)
                                    Prepare.softplus_act(act, P)
                                if norm:
                                    Norm.rsqrt(act, Q + 2)
                                decays(act, Q, q, 5, l)
                                if more:
                                    Prepare.spread_act(act, P, p, 0, ST)
                                    Prepare.spread_act(act, P, p, ST, SP)
                        Norm.square(act, 0, 0)
                        Norm.rsqrt(act, 0)
                        Norm.square(act, 1, 1)
                        Prepare.silus(act, 0, 0)
                        Prepare.copy_dtr(act, 0)
                        Prepare.softplus_act(act, 0)
                        Norm.rsqrt(act, 1)
                        Prepare.spread_act(act, 0, 0, 0, ST)
                        Prepare.spread_act(act, 0, 0, ST, SP)
                        layer(0, False)
                        with act.Fori(1, LAYERS - 1) as l:
                            layer(l, False)
                        layer(LAYERS - 1, True)

                    @block.vector
                    def _(dve):
                        def layer(l, last):
                            for q in range(4):
                                Q, P, p = 4 * l + q, 4 * l + q + 1, (q + 1) % 4
                                more = not (last and q == 3)
                                norm = not (last and q >= 2)
                                if isinstance(Q, int) and Q == 0:
                                    drive(dve, Q, q, 0, driven_dve)
                                scan(dve, Q, q, 0)
                                if not (isinstance(Q, int) and Q == 0):
                                    gate(dve, Q - 1, (q - 1) % 4, 2, l if q else l - 1)
                                read(dve, Q, q, 0, read_dve)
                                if not (isinstance(Q, int) and Q == 0):
                                    add_out(dve, Q - 1, (q - 1) % 4)
                                scan(dve, Q, q, 1)
                                read(dve, Q, q, 1, read_dve)
                                scan(dve, Q, q, 2)
                                gate(dve, Q, q, 0, l)
                                scan(dve, Q, q, 3)
                                if more:
                                    Prepare.split(dve, P)
                                scan(dve, Q, q, 4)
                                if more:
                                    Prepare.softplus_dve(dve, P, p)
                                if norm:
                                    Norm.scale(dve, Q + 2, (q + 2) % 4, l + 1 if q >= 2 else l)
                                scan(dve, Q, q, 5)
                                read(dve, Q, q, 5, read_dve)
                                if more:
                                    drive(dve, P, p, 0, driven_dve)
                                if norm:
                                    Prepare.taps(dve, Q + 2, l + 1 if q >= 2 else l)
                                gate(dve, Q, q, 1, l)
                                if more:
                                    Prepare.spread_dve(dve, P, p)
                        for r in range(3):
                            dve.tensor_copy(spread_sel[32 * r:32 * r + 32, :], ident[32 * r:32 * r + 32, 32 * r:32 * r + 32])
                        dve.memset(decay[:, :, :, :], 0.0).then_inc(cleared.sem, 1)
                        dve.wait_ge(w_norm_got.sem, w_norm_got.at(16))
                        Norm.scale(dve, 0, 0, 0)
                        Prepare.taps(dve, 0, 0)
                        Prepare.split(dve, 0)
                        Prepare.softplus_dve(dve, 0, 0)
                        Norm.scale(dve, 1, 1, 0)
                        Prepare.taps(dve, 1, 0)
                        Prepare.spread_dve(dve, 0, 0)
                        layer(0, False)
                        with dve.Fori(1, LAYERS - 1) as l:
                            layer(l, False)
                        layer(LAYERS - 1, True)
                        gate(dve, QUARTERS - 1, 3, 2, LAYERS - 1)
                        add_out(dve, QUARTERS - 1, 3)

            with ExitStack() as st:
                fw = sb(st, "final_w", [CP, KC])
                sq = sb(st, "fin_sq", [CP, KC, T])
                std = sb(st, "fin_std", [CP, T])
                fsq, fms, fstd, finv = S("fin_squared"), S("fin_ms"), S("fin_std_made"), S("fin_steps")
                with nc.Block() as block:
                    @block.sync
                    def _(sp):
                        sp.dma_start(fw[:, :], a["final_w"]).then_inc(loaded("final").counted(16), 16)

                    @block.scalar
                    def _(act):
                        act.activation(sq[:, :, :], xn[:, :, :T], ACT.Square).then_inc(fsq.sem, 1)
                        act.wait_ge(fms.sem, fms.at(1))
                        act.activation(std[:, :].rearrange("p (c t) -> p c t", c=NCH), ps[:CP, 0:NCH, :CH], ACT.Sqrt,
                                       bias=eps[:CP, 0:1]).then_inc(fstd.sem, 1)

                    @block.tensor
                    def _(pe):
                        pe.wait_ge(fsq.sem, fsq.at(1))
                        for c in range(NCH):
                            for k in range(KC):
                                last = pe.matmul(ps[:CP, c, :CH], ones_mean[:CP, :CP], sq[:, k, c * CH:(c + 1) * CH],
                                                 start=k == 0, stop=k == KC - 1)
                        last.then_inc(fms.sem, 1)

                    @block.vector
                    def _(dve):
                        dve.wait_ge(fstd.sem, fstd.at(1))
                        dve.reciprocal(std[:, :], std[:, :]).then_inc(finv.sem, 1)
                        dve.wait_ge(loaded("final").sem, loaded("final").total)
                        dve.wait_ge(finv.sem, finv.at(1))
                        for k in range(KC):
                            last = dve.scalar_tensor_tensor(sq[:, k, :], xn[:, k, :T], fw[:, k:k + 1], std[:, :],
                                                            ALU.mult, ALU.mult)
                        last.then_inc(finv.sem, 1)
                        dve.wait_ge(finv.sem, finv.at(2))
                        dve.tensor_tensor(h[:, :, :T], h[:, :, :T], sq[:, :, :], ALU.add)

        for stage in (patch_embedding, l0_attention, l0_ffn, l1_attention, l1_ffn, l2_attention, l2_ffn, l3_mamba,
                      l3_ffn):
            stage()
        store_output()


def chunked(w, p):
    w = np.asarray(w)
    return np.ascontiguousarray(np.moveaxis(w.reshape((w.shape[0] // p, p) + w.shape[1:]), 0, 1))


def slots(w):
    w = np.asarray(w)
    out = np.zeros(w.shape[:-1] + (H, 32), w.dtype)
    out[..., :16] = w.reshape(w.shape[:-1] + (H, 16))
    return out.reshape(w.shape[:-1] + (H * 32,))


def swapped(w):
    w = np.asarray(w)
    return np.ascontiguousarray(w.reshape(w.shape[:-1] + (w.shape[-1] // 2, 2))[..., ::-1]).reshape(w.shape)


def attention_masks():
    i, j = np.meshgrid(np.arange(TW), np.arange(TW), indexing="ij")
    same = i // N == j // N
    kinds = [same & (i != j), same & (abs(i - j) <= 6), same & (i >= j), same]
    m = np.stack([np.where(k, 0.0, NEG) for k in kinds], 1).astype(np.float32)
    return np.ascontiguousarray(np.tile(m, (1, 1, 3)))


def rope_tables():
    inv = 1.0 / 10000.0 ** (np.arange(0, 16, 2, dtype=np.float32) / np.float32(16))
    f = np.arange(N, dtype=np.float32)[:, None] * inv[None, :].astype(np.float32)
    cos = np.repeat(np.cos(f), 2, axis=1).T
    sin = np.repeat(np.sin(f), 2, axis=1).T * np.where(np.arange(16) % 2 == 0, -1.0, 1.0)[:, None]
    t = np.zeros((4, 32, 4, IMG, N), np.float32)
    for part, (v, s) in enumerate(((cos, 0.25), (sin, 0.25), (cos, 1.0), (sin, 1.0))):
        t[:, :16, part] = (v * s)[None, :, None, :]
    return np.ascontiguousarray(t.reshape(128, 4, TW))


def layouts(i):
    i = {k: np.asarray(v) for k, v in i.items()}
    x = i["x"].reshape(B, 3, 6, 16, 6, 16).transpose(3, 5, 1, 0, 2, 4).reshape(768, T)
    d = {
        "patches": chunked(x, 128),
        "tok_g1": chunked(i["L0_tok_g1"].T, 128),
        "tok_w": chunked(i["L0_tok_W"].T, 128),
        "tok_b": chunked(i["L0_tok_b"], CP),
        "tok_g2": chunked(i["L0_tok_g2"].T, CP),
        "masks": attention_masks(),
        "a0_wq": chunked(i["L0_attn_w_qkv"][:, :768], CP),
        "a0_wk": chunked(i["L0_attn_w_qkv"][:, 768:1536], CP),
        "a0_wv": chunked(i["L0_attn_w_qkv"][:, 1536:], CP),
        "a0_wo": chunked(i["L0_attn_w_out"], 128),
        "a0_bo": chunked(i["L0_attn_b_out"], CP),
        "a0_scale": chunked(np.repeat(i["L0_attn_scale"], 64), 128),
    }
    qkv1, qkv2, qkv3 = i["L1_attn_w_qkv"], i["L2_attn_W_attn"], i["L2_ffn_w_qkv"]
    b2 = i["L2_attn_b_attn"]
    d |= {
        "moe_router": chunked(i["L0_ffn_router_w"].T, CP),
        "moe_balance": np.tile(i["L0_ffn_balance_bias"], (128, 1)),
        "moe_w1": np.concatenate([i["L0_ffn_w1"], i["L0_ffn_w_fc_sh"][None]]).reshape(9, KC, CP, C).transpose(2, 0, 1, 3),
        "moe_w2": np.concatenate([i["L0_ffn_w2"], i["L0_ffn_w_proj_sh"][None]]).reshape(9, KC, CP, C).transpose(2, 0, 1, 3),
        "a1_wq": chunked(slots(qkv1[:, :C]), CP),
        "a1_wk": chunked(slots(qkv1[:, C:2 * C]), CP),
        "a1_wv": chunked(qkv1[:, 2 * C:], CP),
        "a1_wo": chunked(i["L1_attn_w_proj"], CP),
        "a1_bo": chunked(i["L1_attn_b_proj"], CP),
        "f1_w1": chunked(i["L1_ffn_in_weight"].T, CP),
        "f1_b1": chunked(i["L1_ffn_in_bias"], 128),
        "f1_w2": chunked(i["L1_ffn_out_weight"], 128),
        "a2_wq": chunked(slots(qkv2[:, :C]), CP),
        "a2_wk": chunked(slots(qkv2[:, C:2 * C]), CP),
        "a2_wqs": chunked(slots(swapped(qkv2[:, :C])), CP),
        "a2_wks": chunked(slots(swapped(qkv2[:, C:2 * C])), CP),
        "a2_wv": chunked(qkv2[:, 2 * C:], CP),
        "a2_bqk": np.stack([chunked(slots(v), 128) for v in (b2[:C], swapped(b2[:C]), b2[C:2 * C],
                                                             swapped(b2[C:2 * C]))], 1),
        "a2_bv": b2[None, 2 * C:],
        "a2_wo": chunked(i["L2_attn_W_proj"], CP),
        "a2_bo": chunked(i["L2_attn_b_proj"], CP),
        "rope": rope_tables(),
        "a3_wq": chunked(slots(qkv3[:, :C]), CP),
        "a3_wk": chunked(slots(qkv3[:, C:2 * C]), CP),
        "a3_wv": chunked(qkv3[:, 2 * C:], CP),
        "a3_wo": chunked(i["L2_ffn_w_proj"], CP),
        "a3_bo": chunked(i["L2_ffn_b_proj"], CP),
        "gumbel": np.tile(i["L2_ffn_gumbel_weights"], (128, 1)),
        "n12_gb": np.stack([np.stack([chunked(i[f"L2_ffn_n{n}{path}_{p}"], CP) for path in "ls"], 1)
                            for n in "12" for p in "gb"], 1),
        "f2_w1": chunked(i["L2_ffn_w_fc1"], CP),
        "f2_b1": chunked(i["L2_ffn_b_fc1"], 128),
        "f2_w2": chunked(i["L2_ffn_w_fc2"], 128),
        "f2_b2": chunked(i["L2_ffn_b_fc2"], CP),
        "e_w": chunked(i["L3_ffn_enc_w"], CP),
        "e_b": i["L3_ffn_enc_b"][:, None],
        "sw_w": i["L3_ffn_sw_w"],
        "sw_b": i["L3_ffn_sw_b"][None],
        "f3_w1": chunked(i["L3_ffn_w1"].transpose(1, 0, 2).reshape(C, 512), CP),
        "f3_b1": chunked(i["L3_ffn_b1"].reshape(512), 128),
        "f3_w2": chunked(i["L3_ffn_w2"].reshape(512, C), 128),
        "f3_b2": i["L3_ffn_b2"],
    }
    proj = i["L3_attn_x_proj_w"].transpose(0, 2, 1)
    d |= {
        "m_w_in": np.stack([chunked(i["L3_attn_in_proj_w"][l].T, CP) for l in range(LAYERS)]),
        "m_w_norm": np.stack([chunked(i["L3_attn_norm_w"][l], CP) for l in range(LAYERS)], 1),
        "m_w_mid": np.stack([chunked(np.concatenate(
            [proj[l][:, DR:]] * 3 + [proj[l][:, :DR], i["L3_attn_conv_w"][l][:, 0], i["L3_attn_conv_b"][l][:, None],
                                     i["L3_attn_dt_proj_b"][l][:, None]], 1), 128) for l in range(LAYERS)]),
        "m_w_dt": i["L3_attn_dt_proj_w"].transpose(0, 2, 1),
        "m_w_scan": np.stack([chunked(np.concatenate(
            [i["L3_attn_A_log"][l], i["L3_attn_D"][l][:, None], i["L3_attn_out_proj_w"][l].T], 1), 128)
            for l in range(LAYERS)]),
        "final_w": chunked(i["L3_attn_final_norm_w"], CP),
    }
    return d


def kernel(**inputs):
    import concourse.bacc as bacc
    from concourse.bass_utils import run_bass_kernel_spmd

    nc = bacc.Bacc("TRN2", target_bir_lowering=False, num_devices=1)
    arrays, aps = {}, {}
    for name, v in layouts(inputs).items():
        arrays["in_" + name] = np.ascontiguousarray(v)
        aps[name] = nc.dram_tensor("in_" + name, v.shape, F32, kind="ExternalInput").ap()
    out = nc.dram_tensor("out_h", (CP, KC, T), F32, kind="ExternalOutput").ap()
    build(nc, aps, out)
    r = run_bass_kernel_spmd(nc, [arrays], core_ids=[0])
    got = r.results[0]["out_h"]
    return np.ascontiguousarray(got.transpose(1, 0, 2).reshape(C, B, N).transpose(1, 2, 0))
```
